# Optimizing a Trainium2 kernel written in Bass

```python
import numpy as np
import jax
import jax.numpy as jnp

def _softmax(x, axis=-1):
    return jax.nn.softmax(x, axis=axis)
def _gelu(x):
    return jax.nn.gelu(x, approximate=True)
def _silu(x):
    return jax.nn.silu(x)
def _sigmoid(x):
    return jax.nn.sigmoid(x)
def _layernorm(x, axis=-1, eps=1e-5):
    m = jnp.mean(x, axis=axis, keepdims=True)
    v = jnp.var(x, axis=axis, keepdims=True)
    return (x - m) / jnp.sqrt(v + eps)
def _scatter_add(tgt, idx, src, axis=0):
    return tgt.at[idx].add(src)
def _segment_sum(src, seg, n):
    return jax.ops.segment_sum(src, seg, n)

kernel_name = 'mk_adj_ffn_d2_adj_256_f1d5fb'

def setup_inputs(seed: int = 0):
    np.random.seed(seed)
    _w = jnp.asarray
    def _rec_inputs():
        import jax
        import jax.numpy as jnp
        _gk = jax.random.key(seed)
        x = -0.0002928 + 1 * jax.random.normal(jax.random.fold_in(_gk, 1), (4096, 256), jnp.float32)
        _w = (1.0 + jnp.arange(4096, dtype=jnp.float32)) ** -0.5
        _w = _w / _w.mean()
        _pij = jnp.clip(0.00195312 * _w[:, None] * _w[None, :], 0.0, 1.0)
        _a = jax.random.uniform(jax.random.fold_in(_gk, 2), (4096, 4096)) < _pij
        _a = jnp.logical_or(_a, jnp.eye(4096, dtype=bool))
        _af = _a.astype(jnp.float32)
        _af = _af * jax.random.uniform(jax.random.fold_in(_gk, 3), (4096, 4096), jnp.float32, 0.05, 1)
        adj = _af
        return x, adj
    x, adj = _rec_inputs()
    def _L0_gnn_setup():
        import jax, jax.numpy as jnp
        import numpy as np
        EPS = 1e-12
        key = jax.random.key(seed)
        k1, k2, k3 = jax.random.split(key, 3)
        N, F_IN, F_OUT = (16384, 256, 256)
        feat = jax.random.normal(k1, (N, F_IN), dtype=jnp.float32)
        A = jax.random.uniform(k2, (N, N), dtype=jnp.float32)
        bound = float(np.sqrt(6.0 / (F_IN + F_OUT)))
        W = jax.random.uniform(k3, (F_IN, F_OUT), minval=-bound, maxval=bound, dtype=jnp.float32)
        return {'feat': feat, 'A': A, 'W': W}
    _L0_gnn_all = _L0_gnn_setup()
    _L0_gnn_in = {k: v for k, v in _L0_gnn_all.items() if k in ('W', )}
    del _L0_gnn_all

    def _L0_ffn_setup():
        import jax, jax.numpy as jnp
        import numpy as np
        D_MODEL = 256
        EXPERT_DIM = 512
        NUM_EXPERTS = 8
        TOP_K = 2
        SEQ_LEN = 2048
        BATCH = 2
        key = jax.random.key(seed)
        ks = jax.random.split(key, 8)
        s = 0.02
        x = jax.random.normal(ks[0], (SEQ_LEN, BATCH, D_MODEL), dtype=jnp.float32)
        Wg = jax.random.normal(ks[1], (D_MODEL, NUM_EXPERTS), dtype=jnp.float32) * s
        bg = jax.random.normal(ks[2], (NUM_EXPERTS,), dtype=jnp.float32) * s
        bias = jnp.zeros((NUM_EXPERTS,), dtype=jnp.float32)
        W1 = jax.random.normal(ks[3], (NUM_EXPERTS, D_MODEL, EXPERT_DIM), dtype=jnp.float32) * s
        b1 = jax.random.normal(ks[4], (NUM_EXPERTS, EXPERT_DIM), dtype=jnp.float32) * s
        W2 = jax.random.normal(ks[5], (NUM_EXPERTS, EXPERT_DIM, D_MODEL), dtype=jnp.float32) * s
        b2 = jax.random.normal(ks[6], (NUM_EXPERTS, D_MODEL), dtype=jnp.float32) * s
        return {'x': x, 'Wg': Wg, 'bg': bg, 'bias': bias, 'W1': W1, 'b1': b1, 'W2': W2, 'b2': b2}
    _L0_ffn_all = _L0_ffn_setup()
    _L0_ffn_in = {k: v for k, v in _L0_ffn_all.items() if k in ('Wg', 'bg', 'bias', 'W1', 'b1', 'W2', 'b2', )}
    del _L0_ffn_all

    def _L1_gnn_setup():
        import jax, jax.numpy as jnp
        import numpy as np
        N = 8192
        D_IN = 256
        D_OUT = 256
        key = jax.random.key(seed)
        k1, k2, k3, k4 = jax.random.split(key, 4)
        x = jax.random.normal(k1, (N, D_IN), dtype=jnp.float32)
        adj = jax.random.uniform(k2, (N, N), dtype=jnp.float32)
        W = jax.random.normal(k3, (D_OUT, D_IN), dtype=jnp.float32) * (1.0 / np.sqrt(D_IN))
        b = jax.random.normal(k4, (D_OUT,), dtype=jnp.float32) * 0.01
        return {'x': x, 'adj': adj, 'W': W, 'b': b}
    _L1_gnn_all = _L1_gnn_setup()
    _L1_gnn_in = {k: v for k, v in _L1_gnn_all.items() if k in ('W', 'b', )}
    del _L1_gnn_all

    def _L1_ffn_setup():
        import math
        import jax, jax.numpy as jnp
        import numpy as np
        CAPACITY_FACTOR = 1.25
        TOP_K = 2
        LN_EPS = 1e-05

        def _layer_norm(x, gamma, beta):
            mu = jnp.mean(x, axis=-1, keepdims=True)
            var = jnp.var(x, axis=-1, keepdims=True)
            return (x - mu) * jax.lax.rsqrt(var + LN_EPS) * gamma + beta
        key = jax.random.key(seed)
        ks = jax.random.split(key, 4)
        B, S, D, F, E = (8, 4096, 256, 512, 8)
        x = jax.random.normal(ks[0], (B, S, D), dtype=jnp.float32)
        Wr = jax.random.normal(ks[1], (D, E), dtype=jnp.float32) / np.sqrt(D)
        br = jnp.zeros((E,), jnp.float32)
        W1 = jax.random.normal(ks[2], (E, D, F), dtype=jnp.float32) / np.sqrt(D)
        b1 = jnp.zeros((E, F), jnp.float32)
        W2 = jax.random.normal(ks[3], (E, F, D), dtype=jnp.float32) / np.sqrt(F)
        b2 = jnp.zeros((E, D), jnp.float32)
        gamma = jnp.ones((D,), jnp.float32)
        beta = jnp.zeros((D,), jnp.float32)
        return {'x': x, 'Wr': Wr, 'br': br, 'W1': W1, 'b1': b1, 'W2': W2, 'b2': b2, 'gamma': gamma, 'beta': beta}
    _L1_ffn_all = _L1_ffn_setup()
    _L1_ffn_in = {k: v for k, v in _L1_ffn_all.items() if k in ('Wr', 'br', 'W1', 'b1', 'W2', 'b2', 'gamma', 'beta', )}
    del _L1_ffn_all

    return {
        "x": x,
        "adj": adj,
        "L0_gnn_W": _L0_gnn_in["W"],
        "L0_ffn_Wg": _L0_ffn_in["Wg"],
        "L0_ffn_bg": _L0_ffn_in["bg"],
        "L0_ffn_bias": _L0_ffn_in["bias"],
        "L0_ffn_W1": _L0_ffn_in["W1"],
        "L0_ffn_b1": _L0_ffn_in["b1"],
        "L0_ffn_W2": _L0_ffn_in["W2"],
        "L0_ffn_b2": _L0_ffn_in["b2"],
        "L1_gnn_W": _L1_gnn_in["W"],
        "L1_gnn_b": _L1_gnn_in["b"],
        "L1_ffn_Wr": _L1_ffn_in["Wr"],
        "L1_ffn_br": _L1_ffn_in["br"],
        "L1_ffn_W1": _L1_ffn_in["W1"],
        "L1_ffn_b1": _L1_ffn_in["b1"],
        "L1_ffn_W2": _L1_ffn_in["W2"],
        "L1_ffn_b2": _L1_ffn_in["b2"],
        "L1_ffn_gamma": _L1_ffn_in["gamma"],
        "L1_ffn_beta": _L1_ffn_in["beta"],
    }

def reference(x, adj, L0_gnn_W, L0_ffn_Wg, L0_ffn_bg, L0_ffn_bias, L0_ffn_W1, L0_ffn_b1, L0_ffn_W2, L0_ffn_b2, L1_gnn_W, L1_gnn_b, L1_ffn_Wr, L1_ffn_br, L1_ffn_W1, L1_ffn_b1, L1_ffn_W2, L1_ffn_b2, L1_ffn_gamma, L1_ffn_beta):
    import jax
    import jax.numpy as jnp
    def _L0_gnn_ref(feat, A, W):
        import jax, jax.numpy as jnp
        import numpy as np
        EPS = 1e-12
        N = A.shape[0]
        A_hat = A + jnp.eye(N, dtype=A.dtype)
        d = jnp.sum(A_hat, axis=1)
        dinv = 1.0 / jnp.sqrt(d)
        A_norm = dinv[:, None] * A_hat * dinv[None, :]
        feat_agg = A_norm @ feat
        agg = jax.nn.relu(feat_agg @ W)
        norm = jnp.linalg.norm(agg, axis=1, keepdims=True)
        out = agg / jnp.maximum(norm, EPS)
        return out

    def _L0_ffn_ref(x, Wg, bg, bias, W1, b1, W2, b2):
        import jax, jax.numpy as jnp
        import numpy as np
        D_MODEL = 256
        EXPERT_DIM = 512
        NUM_EXPERTS = 8
        TOP_K = 2
        SEQ_LEN = 2048
        BATCH = 2
        x_flat = x.reshape(-1, D_MODEL)
        gate_logits = x_flat @ Wg + bg + bias
        topk_vals, topk_idx = jax.lax.top_k(gate_logits, TOP_K)
        topk_w = jax.nn.softmax(topk_vals, axis=-1)
        combine = (jax.nn.one_hot(topk_idx, NUM_EXPERTS, dtype=x.dtype) * topk_w[..., None]).sum(axis=1)
        h = jax.nn.relu(jnp.einsum('td,edh->teh', x_flat, W1) + b1)
        y = jnp.einsum('teh,ehd->ted', h, W2) + b2
        out = jnp.einsum('ted,te->td', y, combine)
        return out.reshape(x.shape)

    def _L1_gnn_ref(x, adj, W, b):
        import jax, jax.numpy as jnp
        import numpy as np
        N = 8192
        D_IN = 256
        D_OUT = 256
        h = x @ W.T + b
        A = adj + jnp.eye(adj.shape[0], dtype=adj.dtype)
        rowsum = A.sum(axis=1)
        r_inv_sqrt = jnp.power(rowsum, -0.5)
        r_inv_sqrt = jnp.where(jnp.isinf(r_inv_sqrt), 0.0, r_inv_sqrt)
        A_norm = r_inv_sqrt[:, None] * A * r_inv_sqrt[None, :]
        return A_norm.astype(jnp.float32) @ h.astype(jnp.float32)

    def _L1_ffn_ref(x, Wr, br, W1, b1, W2, b2, gamma, beta):
        import math
        import jax, jax.numpy as jnp
        import numpy as np
        CAPACITY_FACTOR = 1.25
        TOP_K = 2
        LN_EPS = 1e-05

        def _layer_norm(x, gamma, beta):
            mu = jnp.mean(x, axis=-1, keepdims=True)
            var = jnp.var(x, axis=-1, keepdims=True)
            return (x - mu) * jax.lax.rsqrt(var + LN_EPS) * gamma + beta
        B, S, D = x.shape
        E = Wr.shape[1]
        N = B * S
        K = TOP_K
        logits = jnp.mean(x, axis=1) @ Wr + br
        routing_weights = jax.nn.softmax(logits, axis=-1)
        capacity = float(math.ceil(N * CAPACITY_FACTOR / E))
        expected_loads = routing_weights.sum(axis=0) * (N / B)
        scale = jnp.where(expected_loads > capacity, capacity / expected_loads, 1.0)
        routing_weights = jax.nn.softmax(routing_weights * scale, axis=-1)
        rw_tok = jnp.broadcast_to(routing_weights[:, None, :], (B, S, E)).reshape(N, E)
        top_w, top_i = jax.lax.top_k(rw_tok, K)
        top_w = jax.nn.softmax(top_w, axis=-1)
        xf = x.reshape(N, D)
        h = jax.nn.gelu(jnp.einsum('nd,edf->enf', xf, W1) + b1[:, None, :], approximate=False)
        y = jnp.einsum('enf,efd->end', h, W2) + b2[:, None, :]
        w_dense = jnp.zeros((N, E), x.dtype).at[jnp.arange(N)[:, None], top_i].add(top_w)
        out = jnp.einsum('ne,end->nd', w_dense, y).reshape(B, S, D)
        out = _layer_norm(out + x, gamma, beta)
        return out

    x = x + _L0_gnn_ref(_layernorm(x, axis=-1), adj, L0_gnn_W)
    x = x + _L0_ffn_ref((_layernorm(x, axis=-1))[None], L0_ffn_Wg, L0_ffn_bg, L0_ffn_bias, L0_ffn_W1, L0_ffn_b1, L0_ffn_W2, L0_ffn_b2)[0]
    x = x + _L1_gnn_ref(_layernorm(x, axis=-1), adj, L1_gnn_W, L1_gnn_b)
    x = x + _L1_ffn_ref((_layernorm(x, axis=-1))[None], L1_ffn_Wr, L1_ffn_br, L1_ffn_W1, L1_ffn_b1, L1_ffn_W2, L1_ffn_b2, L1_ffn_gamma, L1_ffn_beta)[0]
    return x


_drawn_inputs = setup_inputs


def setup_inputs(seed=0):
    import zlib

    import numpy as np

    out = dict(_drawn_inputs(seed))
    spreads = {'L0_ffn_bias': (0.0, 0.1),
     'L1_ffn_br': (0.0, 0.8),
     'L1_ffn_b1': (0.0, 0.358),
     'L1_ffn_b2': (0.0, 0.1),
     'L1_ffn_gamma': (1.0, 0.2),
     'L1_ffn_beta': (0.0, 0.1)}
    factors = {'L0_ffn_bg': 4.406, 'L0_ffn_b1': 8.0, 'L0_ffn_b2': 3.579, 'L1_gnn_b': 6.967}
    for name, (base, spread) in spreads.items():
        noise = np.random.default_rng([zlib.crc32(name.encode()), seed]).standard_normal(out[name].shape)
        drawn = base * np.exp(spread * noise) if base else spread * noise
        out[name] = jnp.asarray(drawn.astype(out[name].dtype))
    for name, factor in factors.items():
        out[name] = (out[name] * factor).astype(out[name].dtype)
    return out
```

```python
from contextlib import ExitStack

import concourse.bass as bass
from concourse import mybir

P = 128
F32 = mybir.dt.float32
F32R = mybir.dt.float32r
U32 = mybir.dt.uint32
I32 = mybir.dt.int32
ALU = mybir.AluOpType
ACT = mybir.ActivationFunctionType
AX_X = mybir.AxisListType.X
LN_EPS = 1e-5
NORM_EPS = 1e-12
CAPACITY_FACTOR = 1.25
TOP = 2

NAMES = ["x", "adj", "adjT", "L0_gnn_W", "L0_ffn_Wg", "L0_ffn_bg", "L0_ffn_bias", "L0_ffn_W1", "L0_ffn_b1",
         "L0_ffn_W2", "L0_ffn_b2", "L1_gnn_WT", "L1_gnn_b", "L1_ffn_Wr", "L1_ffn_br", "L1_ffn_W1", "L1_ffn_b1",
         "L1_ffn_W2", "L1_ffn_b2", "L1_ffn_gamma", "L1_ffn_beta"]


class Tally:

    def __init__(self, eng, sem):
        self.eng, self.sem, self.n = eng, sem, 0

    def add(self, ins):
        ins.then_inc(self.sem, 1)
        self.n = self.n + 1
        return ins

    def settle(self):
        self.eng.wait_ge(self.sem, self.n)

    def link(self, ins):
        self.add(ins)
        self.settle()


def row_over_partitions(ap, parts=P):
    return ap.rearrange("(a n) -> a n", a=1).broadcast_to([parts, ap.shape[0]])


def newton_rsqrt(dve, own, act_sqrt_done, count, a, r, t):
    dve.wait_ge(act_sqrt_done, count)
    own.link(dve.reciprocal(r, r))
    own.link(dve.tensor_tensor(t, r, r, ALU.mult))
    own.link(dve.tensor_tensor(t, t, a, ALU.mult))
    own.link(dve.tensor_scalar(t, t, -0.5, 1.5, ALU.mult, ALU.add))
    own.link(dve.tensor_tensor(r, r, t, ALU.mult))


def gnn(nc, ctx, layer, x_dram, adj, adjT, W, b, x_sb, dinv, ident, ps):
    N, D = x_dram.shape
    T = N // P
    DC = D // P
    HALF = N // 2
    IT = HALF // P
    GS = 4
    NBLK = 2 * T // GS
    BANKS = 8
    HALF_BANKS = BANKS // 2
    PER_BANK = IT // BANKS
    PIECE = HALF // 2
    SLOTS = 4
    GT = 2 * GS
    L = f"g{layer}_"

    def sb(name, shape, dt=F32):
        return ctx.enter_context(nc.sbuf_tensor(L + name, shape, dt))

    def sem(name):
        return ctx.enter_context(nc.semaphore(L + name))

    U = sb("U", [P, T, D])
    G = sb("G", [P, GT, 2, D], F32R)
    ACC = sb("ACC", [P, T, D])
    raw = [sb(f"raw{s}", [P, HALF]) for s in range(SLOTS)]
    ahi = [sb(f"ahi{s}", [P, PIECE], F32R) for s in range(SLOTS)]
    alo = [sb(f"alo{s}", [P, PIECE], F32R) for s in range(SLOTS)]
    nat = [sb(f"nat{s}", [P, HALF]) for s in range(2)] if layer == 0 else None
    degp = sb("degp", [P, T, 2])
    deg = sb("deg", [P, T])
    tmp = sb("tmp", [P, T])
    stats = sb("stats", [P, T, 6])
    mv = sb("mv", [P, T, 2])
    var = sb("var", [P, T])
    rstd = sb("rstd", [P, T])
    xn = [sb(f"xn{s}", [P, D]) for s in range(2)]
    xt = [[sb(f"xt{s}{h}", [P, DC, P], F32R) for h in range(2)] for s in range(2)]
    Wp = sb("Wp", [P, DC, 2, D], F32R)
    bias = sb("bias", [P, D]) if layer == 1 else None
    Wraw = ACC[:, 0:DC, :]

    x_in, w_in = sem("x_in"), sem("w_in")
    raw_full = [sem(f"raw_full{s}") for s in range(SLOTS)]
    nat_full = [sem(f"nat_full{s}") for s in range(2)]
    nat_sum = sem("nat_sum")
    act_own, dve_own, pool_own = sem("act_own"), sem("dve_own"), sem("pool_own")
    stats_done, sqrt_done, dve_small = sem("stats_done"), sem("sqrt_done"), sem("dve_small")
    w_split = sem("w_split")
    xn_ready, xt_psum, xt_hi, xt_lo, u_psum, u_ready = (
        sem(n) for n in ("xn_ready", "xt_psum", "xt_hi", "xt_lo", "u_psum", "u_ready"))
    acc_zero = sem("acc_zero")
    hi_ready, lo_ready, step_done = sem("hi_ready"), sem("lo_ready"), sem("step_done")
    g_hi, g_lo = sem("g_hi"), sem("g_lo")
    deg_ready, deg_sqrt, dinv_ready = sem("deg_ready"), sem("deg_sqrt"), sem("dinv_ready")
    bank_done, bank_free = sem("bank_done"), sem("bank_free")
    sum_ready, relu_ready, square_ready, norm_ready, norm_sqrt = (
        sem(n) for n in ("sum_ready", "relu_ready", "square_ready", "norm_ready", "norm_sqrt"))
    block = ctx.enter_context(nc.Block())

    def nat_of(t, h):
        return adj[bass.ds(t * P, P), h * HALF:(h + 1) * HALF]

    @block.sync
    def _(sp):
        if layer == 0:
            sp.dma_start(x_sb[:, :, :], x_dram.rearrange("(t p) d -> p t d", p=P)).then_inc(x_in, 16)
        sp.dma_start(Wraw, W.rearrange("(c p) n -> p c n", p=P)).then_inc(w_in, 16)
        if layer == 1:
            sp.dma_start(bias[:, :], row_over_partitions(b)).then_inc(w_in, 16)

        def load_nat(t, h, first=False):
            if not first:
                sp.wait_ge(nat_sum, 2 * t + h - 1)
            sp.dma_start(nat[h][:, :], nat_of(t, h)).then_inc(nat_full[h], 16)

        def load_raw(jt, half, s, n=None):
            if n is not None:
                sp.wait_ge(lo_ready, 2 * n - 2 * SLOTS + 2)
            sp.dma_start(raw[s][:, :], adjT[bass.ds(jt * P, P), bass.ds(half * HALF, HALF)]).then_inc(raw_full[s], 16)

        def blk(bb, with_nat, first=False):
            for j in range(GS):
                jt = (bb // 2) * GS + j
                load_raw(jt, bb % 2, j, None if first else GS * bb + j)
                if with_nat:
                    load_nat(2 * bb + GS + j // 2, j % 2)

        if layer == 0:
            for t in range(GS):
                for h in range(2):
                    load_nat(t, h, first=(t == 0))
        blk(0, layer == 0, first=True)
        last = NBLK - 2 if layer == 0 else 1
        if layer == 0:
            with sp.Fori(1, last) as bb:
                blk(bb, True)
        with sp.Fori(last, NBLK) as bb:
            blk(bb, False)

    @block.gpsimd
    def _(pool):
        pool.wait_ge(w_split, 2)
        pool.memset(ACC[:, :, :], 0.0).then_inc(acc_zero, 1)

    @block.scalar
    def _(act):
        def sum_nat(t, h):
            act.wait_ge(nat_full[h], t * 16 + 16)
            act.activation(nat[h][:, :], nat[h][:, :], ACT.Copy,
                           accum_out=degp[:, bass.ds(t, 1), h]).then_inc(nat_sum, 1)

        if layer == 0:
            for t in range(GS):
                for h in range(2):
                    sum_nat(t, h)
        act.wait_ge(w_in, 16 * (1 + layer))
        act.activation(Wp[:, :, 0, :], Wraw, ACT.Copy).then_inc(w_split, 1)
        act.wait_ge(stats_done, 1)
        act.activation(rstd[:, :], var[:, :], ACT.Sqrt).then_inc(sqrt_done, 1)

        def prep(t, u, first):
            act.wait_ge(xt_psum, t + 1)
            if not first:
                act.wait_ge(u_psum, t - 1)
            act.activation(xt[u][0][:, :, :], ps[:, u, 0:D].rearrange("p (c n) -> p c n", c=DC),
                           ACT.Copy).then_inc(xt_hi, 1)
            if layer == 0:
                act.wait_ge(u_psum, t + 1)
                act.activation(U[:, bass.ds(t, 1), :], ps[:, 2 + u:3 + u, 0:D], ACT.Copy).then_inc(u_ready, 1)

        for u in range(2):
            prep(u, u, True)
        with act.Fori(1, T // 2) as pair:
            t = 2 * pair
            for u in range(2):
                prep(t + u, u, False)

        def g_tile(t):
            act.activation(G[:, bass.ds(t % GT, 1), 0, :], U[:, bass.ds(t, 1), :], ACT.Copy,
                           scale=dinv[:, bass.ds(t, 1)]).then_inc(g_hi, 1)

        def deg_sqrt_of(t):
            act.wait_ge(deg_ready, t // 2 + 1)
            act.activation(dinv[:, bass.ds(t, 2)], deg[:, bass.ds(t, 2)], ACT.Sqrt).then_inc(deg_sqrt, 1)

        act.wait_ge(u_ready, T)
        if layer == 0:
            deg_sqrt_of(0)
            act.wait_ge(dinv_ready, 1)
        for t in range(2):
            g_tile(t)

        def blk(bb, with_nat, with_g=True):
            if with_g and layer == 0:
                deg_sqrt_of(2 * bb + 2)
            for j in range(GS):
                act.wait_ge(raw_full[j], bb * 16 + 16)
                for q in range(2):
                    act.wait_ge(step_done, 2 * GS * bb + 2 * j + q + 1)
                    act.activation(ahi[(2 * j + q) % SLOTS][:, :], raw[j][:, q * PIECE:(q + 1) * PIECE],
                                   ACT.Copy).then_inc(hi_ready, 1)
                if j == 0 and with_g:
                    if layer == 0:
                        act.wait_ge(dinv_ready, bb + 2)
                    for v in range(2):
                        g_tile(2 * bb + 2 + v)
                if with_nat:
                    sum_nat(2 * bb + GS + j // 2, j % 2)

        mid = NBLK - 2 if layer == 0 else 0
        if layer == 0:
            with act.Fori(0, mid) as bb:
                blk(bb, True)
        with act.Fori(mid, NBLK - 1) as bb:
            blk(bb, False)
        blk(NBLK - 1, False, with_g=False)
        if layer == 0:
            def finish(t, u, first):
                act.wait_ge(sum_ready, t + 1)
                act.activation(ACC[:, bass.ds(t, 1), :], ACC[:, bass.ds(t, 1), :], ACT.Relu,
                               scale=dinv[:, bass.ds(t, 1)]).then_inc(relu_ready, 1)
                act.wait_ge(relu_ready, t + 1)
                act.activation(xn[u][:, :], ACC[:, bass.ds(t, 1), :], ACT.Square,
                               accum_out=deg[:, bass.ds(t, 1)]).then_inc(square_ready, 1)

            with act.Fori(0, T // 2) as pair:
                t = 2 * pair
                for u in range(2):
                    finish(t + u, u, False)
            act.wait_ge(square_ready, T)
            act.activation(tmp[:, :], deg[:, :], ACT.Sqrt).then_inc(norm_sqrt, 1)

    @block.vector
    def _(dve):
        own = Tally(dve, dve_own)
        if layer == 0:
            dve.wait_ge(x_in, 16)
        for t in range(T):
            own.add(dve.bn_stats(stats[:, t, :], x_sb[:, t, :]))
        own.settle()
        for t in range(T):
            own.add(dve.bn_aggr(mv[:, t, :], stats[:, t, :]))
        own.settle()
        dve.tensor_scalar(var[:, :], mv[:, :, 1], LN_EPS, None, ALU.add).then_inc(stats_done, 1)
        dve.wait_ge(w_split, 1)
        dve.tensor_tensor(Wp[:, :, 1, :], Wraw, Wp[:, :, 0, :], ALU.subtract).then_inc(w_split, 1)
        dve.wait_ge(stats_done, 1)
        newton_rsqrt(dve, own, sqrt_done, 1, var[:, :], rstd[:, :], tmp[:, :])

        def normalise(t, u, first):
            if not first:
                dve.wait_ge(xt_psum, t - 1)
            dve.tensor_scalar(xn[u][:, :], x_sb[:, bass.ds(t, 1), :], mv[:, bass.ds(t, 1), 0], rstd[:, bass.ds(t, 1)],
                              ALU.subtract, ALU.mult).then_inc(xn_ready, 1)

        def split(t, u):
            dve.wait_ge(xt_hi, t + 1)
            dve.tensor_tensor(xt[u][1][:, :, :], ps[:, u, 0:D].rearrange("p (c n) -> p c n", c=DC), xt[u][0][:, :, :],
                              ALU.subtract).then_inc(xt_lo, 1)

        def product(t, u):
            if layer == 1:
                dve.wait_ge(u_psum, t + 1)
                dve.tensor_tensor(U[:, bass.ds(t, 1), :], ps[:, 2 + u:3 + u, 0:D],
                                  bias[:, :].rearrange("p (a n) -> p a n", a=1), ALU.add).then_inc(u_ready, 1)

        for u in range(2):
            normalise(u, u, True)
        for u in range(2):
            split(u, u)
        with dve.Fori(1, T // 2) as pair:
            t = 2 * pair
            for u in range(2):
                normalise(t + u, u, False)
            for u in range(2):
                product(t + u - 2, u)
                split(t + u, u)
        for u in range(2):
            product(T - 2 + u, u)

        small = Tally(dve, dve_small)

        def degrees(t, n):
            d2 = deg[:, bass.ds(t, 2)]
            dve.wait_ge(nat_sum, 2 * t + 4)
            dve.tensor_tensor(d2, degp[:, bass.ds(t, 2), 0], degp[:, bass.ds(t, 2), 1], ALU.add).then_inc(dve_small, 1)
            dve.wait_ge(dve_small, n + 1)
            dve.tensor_scalar(d2, d2, 1.0, None, ALU.add).then_inc(deg_ready, 1)

        def inverse_root(t, n):
            d2, r2, t2 = deg[:, bass.ds(t, 2)], dinv[:, bass.ds(t, 2)], tmp[:, bass.ds(t, 2)]
            dve.wait_ge(deg_sqrt, t // 2 + 1)
            dve.reciprocal(r2, r2).then_inc(dve_small, 1)
            dve.wait_ge(dve_small, n + 2)
            dve.tensor_tensor(t2, r2, r2, ALU.mult).then_inc(dve_small, 1)
            dve.wait_ge(dve_small, n + 3)
            dve.tensor_tensor(t2, t2, d2, ALU.mult).then_inc(dve_small, 1)
            dve.wait_ge(dve_small, n + 4)
            dve.tensor_scalar(t2, t2, -0.5, 1.5, ALU.mult, ALU.add).then_inc(dve_small, 1)
            dve.wait_ge(dve_small, n + 5)
            dve.tensor_tensor(r2, r2, t2, ALU.mult).then_inc(dinv_ready, 1)

        PER_DEG = 5

        def g_tile(t):
            dve.wait_ge(g_hi, t + 1)
            dve.scalar_tensor_tensor(G[:, bass.ds(t % GT, 1), 1, :], U[:, bass.ds(t, 1), :], dinv[:, bass.ds(t, 1)],
                                     G[:, bass.ds(t % GT, 1), 0, :], ALU.mult, ALU.subtract).then_inc(g_lo, 1)

        dve.wait_ge(acc_zero, 1)
        dve.wait_ge(u_ready, T)
        if layer == 0:
            degrees(0, 0)
            inverse_root(0, 0)
            dve.wait_ge(dinv_ready, 1)
        for t in range(2):
            g_tile(t)

        def lo(bb, j, q):
            dve.wait_ge(hi_ready, 2 * GS * bb + 2 * j + q + 1)
            dve.tensor_tensor(alo[(2 * j + q) % SLOTS][:, :], raw[j][:, q * PIECE:(q + 1) * PIECE],
                              ahi[(2 * j + q) % SLOTS][:, :], ALU.subtract).then_inc(lo_ready, 1)

        def evacuate(bb, banks):
            for k in banks:
                if k % HALF_BANKS == HALF_BANKS - 1:
                    dve.wait_ge(step_done, SLOTS + 2 * GS * (bb + 1) - 1 + k // HALF_BANKS)
                else:
                    dve.wait_ge(bank_done, (BANKS - 2) * bb + k - k // HALF_BANKS + 1)
                half = ACC[:, bass.ds((bb % 2) * IT + PER_BANK * k, PER_BANK), :]
                dve.tensor_tensor(half, ps[:, k, :].rearrange("p (t n) -> p t n", n=D), half,
                                  ALU.add).then_inc(bank_free, 1)

        def blk(bb, first=False, with_g=True):
            if with_g and layer == 0:
                degrees(2 * bb + 2, PER_DEG * (bb + 1))
            for q in range(2):
                lo(bb, 0, q)
            if with_g and layer == 0:
                inverse_root(2 * bb + 2, PER_DEG * (bb + 1))
            if not first:
                evacuate(bb - 1, range(0, BANKS // 2))
            lo(bb, 1, 0)
            if not first:
                evacuate(bb - 1, range(BANKS // 2, BANKS))
            if with_g:
                for v in range(2):
                    g_tile(2 * bb + 2 + v)
            lo(bb, 1, 1)
            for j in range(2, GS):
                for q in range(2):
                    lo(bb, j, q)

        blk(0, first=True)
        with dve.Fori(1, NBLK - 1) as bb:
            blk(bb)
        blk(NBLK - 1, with_g=False)
        evacuate(NBLK - 1, range(BANKS))

        dve.wait_ge(bank_free, BANKS * (NBLK + 1))

        def finish(t):
            dve.scalar_tensor_tensor(ACC[:, bass.ds(t, 1), :], U[:, bass.ds(t, 1), :], dinv[:, bass.ds(t, 1)],
                                     ACC[:, bass.ds(t, 1), :], ALU.mult, ALU.add).then_inc(sum_ready, 1)
            if layer == 1:
                dve.wait_ge(sum_ready, t + 1)
                dve.scalar_tensor_tensor(x_sb[:, bass.ds(t, 1), :], ACC[:, bass.ds(t, 1), :], dinv[:, bass.ds(t, 1)],
                                         x_sb[:, bass.ds(t, 1), :], ALU.mult, ALU.add)

        with dve.Fori(0, T) as t:
            finish(t)
        if layer == 0:
            dve.wait_ge(norm_sqrt, 1)
            own.link(dve.tensor_scalar(tmp[:, :], tmp[:, :], NORM_EPS, None, ALU.max))
            own.link(dve.reciprocal(tmp[:, :], tmp[:, :]))
            with dve.Fori(0, T) as t:
                dve.scalar_tensor_tensor(x_sb[:, bass.ds(t, 1), :], ACC[:, bass.ds(t, 1), :], tmp[:, bass.ds(t, 1)],
                                         x_sb[:, bass.ds(t, 1), :], ALU.mult, ALU.add)

    @block.tensor
    def _(pe):
        def transposes(t, u, first):
            pe.wait_ge(xn_ready, t + 1)
            if not first:
                pe.wait_ge(xt_lo, t - 1)
            for c in range(DC):
                mm = pe.transpose(ps[:, u, c * P:(c + 1) * P], xn[u][:, c * P:(c + 1) * P], ident[:, :])
            mm.then_inc(xt_psum, 1)

        def product(t, u, first, last=False):
            pe.wait_ge(xt_lo, t + 1)
            if not first:
                pe.wait_ge(u_ready, t - 1)
            n = 0
            for c in range(DC):
                for a, w in ((0, 0), (0, 1), (1, 0)):
                    mm = pe.matmul(ps[:, 2 + u, 0:D], xt[u][a][:, c, :], Wp[:, c, w, :],
                                   start=(n == 0), stop=(n == 3 * DC - 1))
                    n += 1
            mm.then_inc(u_psum, 1)
            return mm

        pe.wait_ge(w_split, 2)
        for u in range(2):
            transposes(u, u, True)
        for u in range(2):
            product(u, u, True)
        with pe.Fori(1, T // 2) as pair:
            t = 2 * pair
            for u in range(2):
                transposes(t + u, u, False)
            for u in range(2):
                product(t + u, u, False)
        pe.wait_ge(u_ready, T)
        pe.wait_ge(g_lo, 2)
        pe.sem_inc(step_done, SLOTS)
        pe.sem_inc(bank_free, BANKS)

        with pe.Fori(0, NBLK) as bb:
            g0 = ((bb // 2) % 2) * GS
            for j in range(GS):
                pe.wait_ge(g_lo, (bb // 2) * GS + j + 1)
                ghi, glo = (G[:, bass.ds(g0 + j, 1), w, :] for w in range(2))
                for q in range(2):
                    s = (2 * j + q) % SLOTS
                    out = [ps[:, (q * BANKS // 2) + i // PER_BANK, (i % PER_BANK) * D:(i % PER_BANK + 1) * D]
                           for i in range(IT // 2)]
                    a = [slice(i * P, (i + 1) * P) for i in range(IT // 2)]
                    pe.wait_ge(hi_ready, 2 * GS * bb + 2 * j + q + 1)
                    for i in range(IT // 2):
                        lead = j == 0 and i % PER_BANK == 0
                        if lead:
                            pe.wait_ge(bank_free, BANKS * bb + (q * BANKS // 2) + i // PER_BANK + 1)
                        pe.matmul(out[i], ahi[s][:, a[i]], ghi, start=lead, stop=False, skip_group_check=True)
                        pe.matmul(out[i], ahi[s][:, a[i]], glo, start=False, stop=False, skip_group_check=True)
                    pe.wait_ge(lo_ready, 2 * GS * bb + 2 * j + q + 1)
                    for i in range(IT // 2):
                        mm = pe.matmul(out[i], alo[s][:, a[i]], ghi, start=False, stop=(j == GS - 1),
                                       skip_group_check=True)
                        if j == GS - 1 and i % PER_BANK == PER_BANK - 1 and i < IT // 2 - 1:
                            mm.then_inc(bank_done, 1)
                    mm.then_inc(step_done, 1)


def ffn(nc, ctx, layer, w, x_sb, ident, ps, out_dram):
    E, D, H = w["W1"].shape
    N = x_sb.shape[1] * P
    T = N // P
    DC, HC = D // P, H // P
    BLK = 512
    NT = N // BLK
    TB = BLK // P
    KE = E if layer == 0 else TOP
    L = f"f{layer}_"

    def sb(name, shape, dt=F32):
        return ctx.enter_context(nc.sbuf_tensor(L + name, shape, dt))

    def sem(name):
        return ctx.enter_context(nc.semaphore(L + name))

    XT = [sb(f"XT{h}", [P, DC, N], F32R) for h in range(2)]
    Y = sb("Y", [P, T, D])
    W1r = sb("W1r", [P, DC, H])
    W2r = sb("W2r", [P, HC, D])
    W1 = [[sb(f"W1_{s}{h}", [P, DC, H], F32R) for h in range(2)] for s in range(2)]
    W2 = [[sb(f"W2_{s}{h}", [P, HC, D], F32R) for h in range(2)] for s in range(2)]
    b1 = [sb(f"b1_{s}", [P, HC]) for s in range(2)]
    b2 = [sb(f"b2_{s}", [P, D]) for s in range(2)]
    act_out = [sb(f"act{s}", [P, BLK]) for s in range(2)]
    hT = [[sb(f"hT{s}{h}", [P, BLK], F32R) for h in range(2)] for s in range(HC)]
    stats = sb("stats", [P, T, 6])
    mv = sb("mv", [P, T, 2])
    var = sb("var", [P, T])
    rstd = sb("rstd", [P, T])
    tmp = sb("tmp", [P, T])
    xn = [sb(f"xn{s}", [P, D]) for s in range(2)]
    xt = [sb(f"xt{s}", [P, DC, P]) for s in range(2)]
    Wg = sb("Wg", [P, DC, E])
    bg = sb("bg", [P, E])
    bg2 = sb("bg2", [P, E])
    comb = sb("comb", [P, T, E]) if layer == 0 else sb("comb", [P, 1, TOP])
    iota = sb("iota", [P, E])
    ones = sb("ones", [P, 1])
    if layer == 0:
        logit = sb("logit", [P, T, E])
        best = sb("best", [P, T, 8])
        besti = sb("besti", [P, T, 8], U32)
        bestf = sb("bestf", [P, T, TOP])
        wtop = sb("wtop", [P, T, TOP])
        pick = sb("pick", [P, T, E])
    else:
        rt = sb("rt", [P, 12, E])
        besti = sb("besti", [P, 8], U32)
        meanT = sb("meanT", [P, DC, P])
        gamma = sb("gamma", [P, D])
        beta = sb("beta", [P, D])
        y2 = [sb(f"y2{s}", [P, D]) for s in range(2)]

    g_in = sem("g_in")
    dve_own, pool_own, act_own = sem("dve_own"), sem("pool_own"), sem("act_own")
    stats_done, sqrt_done = sem("stats_done"), sem("sqrt_done")
    xn_ready, xt_psum, xt_sb, xt_hi, xt_lo, gate_psum = (
        sem(n) for n in ("xn_ready", "xt_psum", "xt_sb", "xt_hi", "xt_lo", "gate_psum"))
    consts, y_zero = sem("consts"), sem("y_zero")
    mean_ready, mean_b, soft_in, soft_out = sem("mean_ready"), sem("mean_b"), sem("soft_in"), sem("soft_out")
    comb_ready = sem("comb_ready")
    w_in, b_in = sem("w_in"), [sem(f"b_in{s}") for s in range(2)]
    w_hi, w_lo = sem("w_hi"), sem("w_lo")
    h_psum, h_act, h_hi, h_lo, h_used = (sem(n) for n in ("h_psum", "h_act", "h_hi", "h_lo", "h_used"))
    y_psum, y_added = sem("y_psum"), sem("y_added")
    last_stats, last_sqrt, out_ready = (sem(n) for n in ("last_stats", "last_sqrt", "out_ready"))
    out_done = [sem(f"out_done{s}") for s in range(2)]
    block = ctx.enter_context(nc.Block())
    HB0, YB0 = 0, 4

    @block.sync
    def _(sp):
        sp.dma_start(Wg[:, :, :], w["Wg"].rearrange("(c p) e -> p c e", p=P)).then_inc(g_in, 16)
        sp.dma_start(bg[:, :], row_over_partitions(w["bg"])).then_inc(g_in, 16)
        if layer == 0:
            sp.dma_start(bg2[:, :], row_over_partitions(w["bias"])).then_inc(g_in, 16)
        else:
            sp.dma_start(gamma[:, :], row_over_partitions(w["gamma"])).then_inc(g_in, 16)
            sp.dma_start(beta[:, :], row_over_partitions(w["beta"])).then_inc(g_in, 16)
            sp.wait_ge(comb_ready, 1)
        for k in range(KE):
            e = k if layer == 0 else sp.value_load(besti[0:1, k:k + 1], min_val=0, max_val=E - 1)
            if k >= 1:
                sp.wait_ge(w_lo, 2 * k)
            sp.dma_start(W1r[:, :, :], w["W1"][bass.ds(e, 1), :, :].rearrange("a (c p) h -> p (a c) h", p=P)).then_inc(w_in, 16)
            sp.dma_start(W2r[:, :, :], w["W2"][bass.ds(e, 1), :, :].rearrange("a (c p) h -> p (a c) h", p=P)).then_inc(w_in, 16)
            if k >= 2:
                sp.wait_ge(y_added, NT * TB // 2 * (k - 1))
            sp.dma_start(b1[k % 2][:, :], w["b1"][bass.ds(e, 1), :, :].rearrange("a p c -> p (a c)")).then_inc(b_in[k % 2], 16)
            sp.dma_start(b2[k % 2][:, :], w["b2"][bass.ds(e, 1), :].broadcast_to([P, D])).then_inc(b_in[k % 2], 16)
        if layer == 1:
            with sp.Fori(0, T // 2) as pair:
                t = 2 * pair
                for u in range(2):
                    sp.wait_ge(out_ready, t + u + 1)
                    sp.dma_start(out_dram[bass.ds((t + u) * P, P), :], y2[u][:, :]).then_inc(out_done[u], 16)
            for u in range(2):
                sp.wait_ge(out_done[u], 16 * (T // 2))

    @block.gpsimd
    def _(pool):
        pool.memset(ones[:, :], 1.0).then_inc(consts, 1)
        pool.iota(iota[:, :], [[1, E]], base=0, channel_multiplier=0,
                  allow_small_or_imprecise_dtypes=True).then_inc(consts, 1)
        pool.memset(Y[:, :, :], 0.0).then_inc(y_zero, 1)
        with pool.Fori(0, T // 2) as pair:
            t = 2 * pair
            for u in range(2):
                pool.wait_ge(xt_sb, t + u + 1)
                pool.tensor_copy(XT[0][:, :, bass.ds((t + u) * P, P)], xt[u][:, :, :]).then_inc(xt_hi, 1)

    @block.scalar
    def _(act):
        act.wait_ge(stats_done, 1)
        act.activation(rstd[:, :], var[:, :], ACT.Sqrt).then_inc(sqrt_done, 1)

        def evac(t, u, first):
            act.wait_ge(xt_psum, t + 1)
            if not first:
                act.wait_ge(xt_lo, t - 1)
                if layer == 0:
                    act.wait_ge(gate_psum, t - 1)
            act.activation(xt[u][:, :, :], ps[:, u, 0:D].rearrange("p (c n) -> p c n", c=DC), ACT.Copy).then_inc(xt_sb, 1)

        for u in range(2):
            evac(u, u, True)
        with act.Fori(1, T // 2) as pair:
            t = 2 * pair
            for u in range(2):
                evac(t + u, u, False)
        if layer == 0:
            act.wait_ge(soft_in, 1)
            act.activation(wtop[:, :, 1], wtop[:, :, 0], ACT.Exp).then_inc(soft_out, 1)
        else:
            act.wait_ge(mean_ready, 1)
            act.activation(meanT[:, :, :], ps[:, 2, 0:DC].unsqueeze(2).broadcast_to([P, DC, P]), ACT.Copy,
                           scale=1.0 / N).then_inc(mean_b, 1)
            for n, (dst, src) in enumerate([(2, 1), (6, 5), (10, 9)]):
                act.wait_ge(soft_in, n + 1)
                act.activation(rt[:, dst, :], rt[:, src, :], ACT.Exp).then_inc(soft_out, 1)

        func = ACT.Relu if layer == 0 else ACT.Gelu

        def split_hi(k):
            act.wait_ge(w_in, 32 * (k + 1))
            if k >= 2:
                act.wait_ge(h_used, HC + HC * NT * (k - 1))
            act.activation(W1[k % 2][0][:, :, :], W1r[:, :, :], ACT.Copy).then_inc(w_hi, 1)
            act.activation(W2[k % 2][0][:, :, :], W2r[:, :, :], ACT.Copy).then_inc(w_hi, 1)

        split_hi(0)
        for k in range(KE):
            act.wait_ge(b_in[k % 2], 32 * (k // 2 + 1))
            with act.Fori(0, NT) as tb:
                for c in range(HC):
                    act.wait_ge(h_psum, HC * NT * k + HC * tb + c + 1)
                    act.wait_ge(h_lo, HC * NT * k + HC * tb + c + 1)
                    act.activation(act_out[c % 2][:, :], ps[:, HB0 + c, :], func,
                                   bias=b1[k % 2][:, c:c + 1]).then_inc(h_act, 1)
            if k + 1 < KE:
                split_hi(k + 1)
        if layer == 1:
            act.wait_ge(last_stats, 1)
            act.activation(rstd[:, :], var[:, :], ACT.Sqrt).then_inc(last_sqrt, 1)

    @block.vector
    def _(dve):
        own = Tally(dve, dve_own)
        for t in range(T):
            own.add(dve.bn_stats(stats[:, t, :], x_sb[:, t, :]))
        own.settle()
        for t in range(T):
            own.add(dve.bn_aggr(mv[:, t, :], stats[:, t, :]))
        own.settle()
        dve.tensor_scalar(var[:, :], mv[:, :, 1], LN_EPS, None, ALU.add).then_inc(stats_done, 1)
        dve.wait_ge(stats_done, 1)
        newton_rsqrt(dve, own, sqrt_done, 1, var[:, :], rstd[:, :], tmp[:, :])

        def normalise(t, u, first):
            if not first:
                dve.wait_ge(xt_psum, t - 1)
                if layer == 1:
                    dve.wait_ge(gate_psum, t - 1)
            dve.tensor_scalar(xn[u][:, :], x_sb[:, bass.ds(t, 1), :], mv[:, bass.ds(t, 1), 0], rstd[:, bass.ds(t, 1)],
                              ALU.subtract, ALU.mult).then_inc(xn_ready, 1)

        def split(t, u):
            dve.wait_ge(xt_hi, t + 1)
            dve.tensor_tensor(XT[1][:, :, bass.ds(t * P, P)], xt[u][:, :, :], XT[0][:, :, bass.ds(t * P, P)],
                              ALU.subtract).then_inc(xt_lo, 1)

        for u in range(2):
            normalise(u, u, True)
        for u in range(2):
            split(u, u)
        with dve.Fori(1, T // 2) as pair:
            t = 2 * pair
            for u in range(2):
                normalise(t + u, u, False)
            for u in range(2):
                split(t + u, u)
        dve.wait_ge(g_in, 48 if layer == 0 else 64)
        dve.wait_ge(consts, 2)
        if layer == 0:
            def over_tiles(a):
                return a.unsqueeze(1).broadcast_to([P, T, E])

            dve.wait_ge(gate_psum, T)
            own.link(dve.tensor_tensor(logit[:, :, :], ps[:, 2, 0:T * E].rearrange("p (t e) -> p t e", e=E),
                                       over_tiles(bg[:, :]), ALU.add))
            own.link(dve.tensor_tensor(logit[:, :, :], logit[:, :, :], over_tiles(bg2[:, :]), ALU.add))
            for t in range(T):
                own.add(dve.max(best[:, t, :], logit[:, t, :]))
            own.settle()
            for t in range(T):
                own.add(dve.max_index(besti[:, t, :], best[:, t, :], logit[:, t, :]))
            dve.tensor_tensor(wtop[:, :, 0], best[:, :, 1], best[:, :, 0], ALU.subtract).then_inc(soft_in, 1)
            dve.wait_ge(soft_out, 1)
            own.link(dve.tensor_scalar(tmp[:, :], wtop[:, :, 1], 1.0, None, ALU.add))
            own.link(dve.reciprocal(wtop[:, :, 0], tmp[:, :]))
            own.link(dve.tensor_tensor(wtop[:, :, 1], wtop[:, :, 1], wtop[:, :, 0], ALU.mult))
            own.link(dve.tensor_copy(bestf[:, :, :], besti[:, :, 0:TOP]))
            for k in range(TOP):
                dst = comb if k == 0 else pick
                own.link(dve.tensor_tensor(dst[:, :, :], bestf[:, :, k:k + 1].broadcast_to([P, T, E]),
                                           over_tiles(iota[:, :]), ALU.is_equal))
                own.link(dve.tensor_tensor(dst[:, :, :], dst[:, :, :], wtop[:, :, k:k + 1].broadcast_to([P, T, E]),
                                           ALU.mult))
            own.link(dve.tensor_tensor(comb[:, :, :], comb[:, :, :], pick[:, :, :], ALU.add))
        else:
            r = [rt[:, i, :] for i in range(12)]
            c = [rt[:, 11, i:i + 1] for i in range(8)]
            tokens = float(N)
            cap = float(-(-int(N * CAPACITY_FACTOR * 4) // (E * 4)))

            def softmax(src, diff, ex, n, m, s, dst):
                own.link(dve.reduce_max(m, src, AX_X))
                own.link(dve.tensor_scalar(diff, src, m, None, ALU.subtract))
                dve.sem_inc(soft_in, 1)
                dve.wait_ge(soft_out, n)
                own.link(dve.reduce_sum(s, ex, AX_X))
                own.link(dve.reciprocal(s, s))
                own.link(dve.tensor_scalar(dst, ex, s, None, ALU.mult))

            dve.wait_ge(gate_psum, T + 1)
            own.link(dve.tensor_tensor(r[0], ps[:, 3, 0:E], bg[:, :], ALU.add))
            softmax(r[0], r[1], r[2], 1, c[0], c[1], r[3])
            own.link(dve.tensor_scalar(r[4], r[3], tokens, None, ALU.mult))
            own.link(dve.reciprocal(r[4], r[4]))
            own.link(dve.tensor_scalar(r[4], r[4], cap, 1.0, ALU.mult, ALU.min))
            own.link(dve.tensor_tensor(r[4], r[4], r[3], ALU.mult))
            softmax(r[4], r[5], r[6], 2, c[2], c[3], r[7])
            own.link(dve.max(r[8], r[7]))
            own.link(dve.max_index(besti[:, :], r[8], r[7]))
            own.link(dve.tensor_scalar(r[9], r[8], c8 := rt[:, 8, 0:1], None, ALU.subtract))
            dve.sem_inc(soft_in, 1)
            dve.wait_ge(soft_out, 3)
            own.link(dve.reduce_sum(c[4], rt[:, 10, 0:TOP], AX_X))
            own.link(dve.reciprocal(c[4], c[4]))
            own.link(dve.tensor_scalar(comb[:, 0, :], rt[:, 10, 0:TOP], c[4], None, ALU.mult))
        dve.sem_inc(comb_ready, 1)
        dve.wait_ge(y_zero, 1)

        def split_lo(k):
            for n, (Wk, Wr) in enumerate(((W1, W1r), (W2, W2r))):
                dve.wait_ge(w_hi, 2 * k + n + 1)
                dve.tensor_tensor(Wk[k % 2][1][:, :, :], Wr[:, :, :], Wk[k % 2][0][:, :, :],
                                  ALU.subtract).then_inc(w_lo, 1)

        def split_h(m, c):
            dve.wait_ge(h_act, m + 1)
            dve.wait_ge(h_used, m + 1)
            dve.tensor_copy(hT[c][0][:, :], act_out[c % 2][:, :]).then_inc(h_hi, 1)
            dve.wait_ge(h_hi, m + 1)
            dve.tensor_tensor(hT[c][1][:, :], act_out[c % 2][:, :], hT[c][0][:, :], ALU.subtract).then_inc(h_lo, 1)

        def add_y(k, tb, n):
            m = TB // 2 * n
            for g in range(TB // 2):
                if g < TB // 2 - 1:
                    dve.wait_ge(y_psum, n + g + 1)
                else:
                    dve.wait_ge(h_used, HC * n + 2 * HC)
                pair = ps[:, YB0 + g, :].rearrange("p (a n) -> p a n", n=D)
                dve.tensor_tensor(pair, pair, b2[k % 2][:, :].unsqueeze(1).broadcast_to([P, 2, D]),
                                  ALU.add).then_inc(act_own, 1)
                dve.wait_ge(act_own, m + g + 1)
                for v in range(2):
                    t = TB * tb + 2 * g + v
                    cw = comb[:, bass.ds(t, 1), k] if layer == 0 else comb[:, 0, k:k + 1]
                    ins = dve.scalar_tensor_tensor(Y[:, bass.ds(t, 1), :], pair[:, v:v + 1, :], cw,
                                                   Y[:, bass.ds(t, 1), :], ALU.mult, ALU.add)
                ins.then_inc(y_added, 1)

        dve.sem_inc(h_lo, 2)
        split_lo(0)
        for k in range(KE):
            dve.wait_ge(b_in[k % 2], 32 * (k // 2 + 1))
            for c in range(HC):
                split_h(HC * NT * k + c, c)
            with dve.Fori(1, NT) as tb:
                for c in range(HC):
                    split_h(HC * NT * k + HC * tb + c, c)
                    if c == 1:
                        add_y(k, tb - 1, NT * k + tb - 1)
            add_y(k, NT - 1, NT * k + NT - 1)
            if k + 1 < KE:
                split_lo(k + 1)
        dve.wait_ge(y_added, KE * NT * TB // 2)
        if layer == 0:
            for t in range(0, T, 4):
                dve.tensor_tensor(x_sb[:, t:t + 4, :], x_sb[:, t:t + 4, :], Y[:, t:t + 4, :], ALU.add)
        else:
            for t in range(T):
                xt_, yt = x_sb[:, t, :], Y[:, t, :]
                own.link(dve.tensor_scalar(xn[t % 2][:, :], xt_, mv[:, t, 0:1], rstd[:, t:t + 1], ALU.subtract, ALU.mult))
                own.link(dve.tensor_tensor(yt, yt, xn[t % 2][:, :], ALU.add))
                own.add(dve.bn_stats(stats[:, t, :], yt))
            own.settle()
            for t in range(T):
                own.add(dve.bn_aggr(mv[:, t, :], stats[:, t, :]))
            own.settle()
            own.link(dve.tensor_scalar(var[:, :], mv[:, :, 1], LN_EPS, None, ALU.add))
            dve.sem_inc(last_stats, 1)
            newton_rsqrt(dve, own, last_sqrt, 1, var[:, :], rstd[:, :], tmp[:, :])
            for t in range(T):
                yt, o = Y[:, t, :], y2[t % 2][:, :]
                own.link(dve.tensor_scalar(yt, yt, mv[:, t, 0:1], rstd[:, t:t + 1], ALU.subtract, ALU.mult))
                own.link(dve.tensor_tensor(yt, yt, gamma[:, :], ALU.mult))
                own.link(dve.tensor_tensor(yt, yt, beta[:, :], ALU.add))
                if t >= 2:
                    dve.wait_ge(out_done[t % 2], 16 * (t // 2))
                dve.tensor_tensor(o, yt, x_sb[:, t, :], ALU.add).then_inc(out_ready, 1)

    @block.tensor
    def _(pe):
        pe.wait_ge(g_in, 48 if layer == 0 else 64)
        pe.wait_ge(consts, 2)

        def transposes(t, u, first):
            pe.wait_ge(xn_ready, t + 1)
            if not first:
                pe.wait_ge(xt_sb, t - 1)
            for c in range(DC):
                mm = pe.transpose(ps[:, u, c * P:(c + 1) * P], xn[u][:, c * P:(c + 1) * P], ident[:, :])
            mm.then_inc(xt_psum, 1)

        def gate(t, u, first):
            if layer == 0:
                pe.wait_ge(xt_sb, t + 1)
                for c in range(DC):
                    mm = pe.matmul(ps[:, 2, bass.ds(t * E, E)], xt[u][:, c, :], Wg[:, c, :],
                                   start=(c == 0), stop=(c == DC - 1), skip_group_check=True)
            else:
                for c in range(DC):
                    mm = pe.matmul(ps[:, 2, c:c + 1], xn[u][:, c * P:(c + 1) * P], ones[:, :],
                                   start=(first and u == 0 and c == 0), stop=False, skip_group_check=True)
            mm.then_inc(gate_psum, 1)

        for u in range(2):
            transposes(u, u, True)
        for u in range(2):
            gate(u, u, True)
        with pe.Fori(1, T // 2) as pair:
            t = 2 * pair
            for u in range(2):
                transposes(t + u, u, False)
            for u in range(2):
                gate(t + u, u, False)
        if layer == 1:
            pe.wait_ge(gate_psum, T)
            pe.sem_inc(mean_ready, 1)
            pe.wait_ge(mean_b, 1)
            for c in range(DC):
                mm = pe.matmul(ps[:, 3, 0:E], meanT[:, c, :], Wg[:, c, :], start=(c == 0), stop=(c == DC - 1))
            mm.then_inc(gate_psum, 1)
        pe.wait_ge(xt_lo, T)
        pe.wait_ge(comb_ready, 1)
        pe.sem_inc(h_used, HC)

        def up(k, tb, c, m):
            n = 0
            if m is not None:
                pe.wait_ge(h_act, m - HC + 1)
            for d in range(DC):
                for a, b in ((0, 0), (0, 1), (1, 0)):
                    mm = pe.matmul(ps[:, HB0 + c, :], W1[k % 2][a][:, d, c * P:(c + 1) * P],
                                   XT[b][:, d, bass.ds(tb * BLK, BLK)], start=(n == 0), stop=(n == 3 * DC - 1))
                    n += 1
            mm.then_inc(h_psum, 1)

        def down(k, tb, c, m, my):
            pe.wait_ge(h_lo, m + 3)
            for t in range(TB):
                if c == 0 and t % 2 == 0 and my is not None:
                    pe.wait_ge(y_added, my + t // 2 - 1)
                for n, (a, b) in enumerate(((0, 0), (0, 1), (1, 0))):
                    mm = pe.matmul(ps[:, YB0 + t // 2, (t % 2) * D:(t % 2 + 1) * D], hT[c][a][:, t * P:(t + 1) * P],
                                   W2[k % 2][b][:, c, :], start=(c == 0 and t % 2 == 0 and n == 0), stop=(c == HC - 1),
                                   skip_group_check=True)
                if c == HC - 1 and t % 2 == 1 and t < TB - 1:
                    mm.then_inc(y_psum, 1)
            mm.then_inc(h_used, 1)

        def block_of(k, tb, m, my, has_next):
            for c in range(HC):
                if c + 2 < HC:
                    up(k, tb, c + 2, m + c + 2 if m is not None else None)
                elif has_next:
                    up(k, tb + 1, c + 2 - HC, (m if m is not None else 0) + c + 2)
                down(k, tb, c, (m if m is not None else 0) + c, my)

        for k in range(KE):
            pe.wait_ge(w_lo, 2 * (k + 1))
            base = HC * NT * k
            for c in range(2):
                up(k, 0, c, base + c if k else None)
            block_of(k, 0, base if k else None, (TB // 2) * NT * k if k else None, True)
            with pe.Fori(1, NT - 1) as tb:
                block_of(k, tb, base + HC * tb, (TB // 2) * (NT * k + tb), True)
            block_of(k, NT - 1, base + HC * (NT - 1), (TB // 2) * (NT * k + NT - 1), False)


def build(nc, a, out):
    N, D = a["x"].shape
    T = N // P
    with ExitStack() as top:
        x_sb = top.enter_context(nc.sbuf_tensor("x_sb", [P, T, D], F32))
        dinv = top.enter_context(nc.sbuf_tensor("dinv", [P, T], F32))
        ident = top.enter_context(nc.sbuf_tensor("ident", [P, P], F32))
        ps = top.enter_context(nc.psum_tensor("ps", [P, 8, 512], F32))
        made = top.enter_context(nc.semaphore("ident_made"))
        with nc.Block() as block:
            @block.gpsimd
            def _(pool):
                pool.memset(ident[:, :], 0.0).then_inc(made, 1)
                pool.wait_ge(made, 1)
                pool.affine_select(out=ident[:, :], in_=ident[:, :], compare_op=ALU.not_equal, fill=1.0,
                                   base=0, pattern=[[-1, P]], channel_multiplier=1)
        for layer in range(2):
            with ExitStack() as ctx:
                gnn(nc, ctx, layer, a["x"], a["adj"], a["adjT"],
                    a["L0_gnn_W"] if layer == 0 else a["L1_gnn_WT"],
                    None if layer == 0 else a["L1_gnn_b"], x_sb, dinv, ident, ps)
            with ExitStack() as ctx:
                if layer == 0:
                    w = {"Wg": a["L0_ffn_Wg"], "bg": a["L0_ffn_bg"], "bias": a["L0_ffn_bias"]}
                else:
                    w = {"Wg": a["L1_ffn_Wr"], "bg": a["L1_ffn_br"], "gamma": a["L1_ffn_gamma"], "beta": a["L1_ffn_beta"]}
                w |= {n: a[f"L{layer}_ffn_{n}"] for n in ("W1", "b1", "W2", "b2")}
                ffn(nc, ctx, layer, w, x_sb, ident, ps, out)


def kernel(**inputs):
    import numpy as np
    import concourse.bacc as bacc
    from concourse.bass_utils import run_bass_kernel_spmd

    data = {n: np.asarray(v) for n, v in inputs.items()}
    data["adjT"] = data["adj"].T
    data["L1_gnn_WT"] = data.pop("L1_gnn_W").T
    for n in ("L0_ffn_b1", "L1_ffn_b1"):
        E, H = data[n].shape
        data[n] = data[n].reshape(E, H // P, P).transpose(0, 2, 1)
    nc = bacc.Bacc("TRN2", target_bir_lowering=False, num_devices=1)
    arrays = {f"in_{n}": np.ascontiguousarray(data[n]) for n in NAMES}
    aps = {n: nc.dram_tensor(f"in_{n}", arrays[f"in_{n}"].shape, mybir.dt.from_np(arrays[f"in_{n}"].dtype),
                             kind="ExternalInput").ap() for n in NAMES}
    out = nc.dram_tensor("out", data["x"].shape, F32, kind="ExternalOutput").ap()
    build(nc, aps, out)
    return run_bass_kernel_spmd(nc, [arrays], core_ids=[0]).results[0]["out"]
```

```python
from contextlib import ExitStack

import concourse.bass as bass
from concourse import mybir

P = 128
F32 = mybir.dt.float32
F32R = mybir.dt.float32r
U32 = mybir.dt.uint32
I32 = mybir.dt.int32
ALU = mybir.AluOpType
ACT = mybir.ActivationFunctionType
AX_X = mybir.AxisListType.X
LN_EPS = 1e-5
NORM_EPS = 1e-12
CAPACITY_FACTOR = 1.25
TOP = 2

NAMES = ["x", "adj", "adjT", "L0_gnn_W", "L0_ffn_Wg", "L0_ffn_bg", "L0_ffn_bias", "L0_ffn_W1", "L0_ffn_b1",
         "L0_ffn_W2", "L0_ffn_b2", "L1_gnn_WT", "L1_gnn_b", "L1_ffn_Wr", "L1_ffn_br", "L1_ffn_W1", "L1_ffn_b1",
         "L1_ffn_W2", "L1_ffn_b2", "L1_ffn_gamma", "L1_ffn_beta"]


class Tally:

    def __init__(self, eng, sem):
        self.eng, self.sem, self.n = eng, sem, 0

    def add(self, ins):
        ins.then_inc(self.sem, 1)
        self.n = self.n + 1
        return ins

    def settle(self):
        self.eng.wait_ge(self.sem, self.n)

    def link(self, ins):
        self.add(ins)
        self.settle()


def row_over_partitions(ap, parts=P):
    return ap.rearrange("(a n) -> a n", a=1).broadcast_to([parts, ap.shape[0]])


def newton_rsqrt(dve, own, act_sqrt_done, count, a, r, t):
    dve.wait_ge(act_sqrt_done, count)
    own.link(dve.reciprocal(r, r))
    own.link(dve.tensor_tensor(t, r, r, ALU.mult))
    own.link(dve.tensor_tensor(t, t, a, ALU.mult))
    own.link(dve.tensor_scalar(t, t, -0.5, 1.5, ALU.mult, ALU.add))
    own.link(dve.tensor_tensor(r, r, t, ALU.mult))


def eng_values(nc, eng, ap, top):
    _, values = nc.values_load_multi_w_load_instructions(
        ap, engines=[eng.engine], min_val=0, max_val=top,
        skip_runtime_bounds_check_because="computed on chip as min(count of experts, top), never below 0")
    return values


def clear(pool, sems):
    for s in sems:
        pool.sem_clear(s)


def gnn(nc, ctx, layer, x_dram, adj, adjT, W, b, x_sb, dinv, ident, ps):
    N, D = x_dram.shape
    T = N // P
    DC = D // P
    HALF = N // 2
    IT = HALF // P
    GS = 4
    NBLK = 2 * T // GS
    BANKS = 8
    HALF_BANKS = BANKS // 2
    PER_BANK = IT // BANKS
    PIECE = HALF // 2
    SLOTS = 4
    GT = 2 * GS
    QUAD = 4
    NQ = T // QUAD
    L = f"g{layer}_"

    def sb(name, shape, dt=F32):
        return ctx.enter_context(nc.sbuf_tensor(L + name, shape, dt))

    sems = []

    def sem(name):
        sems.append(ctx.enter_context(nc.semaphore(L + name)))
        return sems[-1]

    U = sb("U", [P, T, D])
    G = sb("G", [P, GT, 2, D], F32R)
    ACC = sb("ACC", [P, T, D])
    raw = [sb(f"raw{s}", [P, HALF]) for s in range(SLOTS)]
    ahi = [sb(f"ahi{s}", [P, PIECE], F32R) for s in range(SLOTS)]
    alo = [sb(f"alo{s}", [P, PIECE], F32R) for s in range(SLOTS)]
    nat = [sb(f"nat{s}", [P, HALF]) for s in range(2)] if layer == 0 else None
    degp = sb("degp", [P, T, 2])
    deg = sb("deg", [P, T])
    tmp = sb("tmp", [P, T])
    stats = sb("stats", [P, T, 6])
    mv = sb("mv", [P, T, 2])
    var = sb("var", [P, T])
    rstd = sb("rstd", [P, T])
    xn = [ACC[:, QUAD * (s + 1):QUAD * (s + 2), :] for s in range(2)]
    sq = [sb(f"sq{s}", [P, D]) for s in range(2)] if layer == 0 else None
    Wp = sb("Wp", [P, DC, 2, D], F32R)
    bias = sb("bias", [P, D]) if layer == 1 else None
    Wraw = ACC[:, 0:DC, :]

    x_in, w_in = sem("x_in"), sem("w_in")
    raw_full = [sem(f"raw_full{s}") for s in range(SLOTS)]
    nat_full = [sem(f"nat_full{s}") for s in range(2)]
    nat_sum = sem("nat_sum")
    act_own, dve_own, pool_own = sem("act_own"), sem("dve_own"), sem("pool_own")
    stats_done, sqrt_done, dve_small = sem("stats_done"), sem("sqrt_done"), sem("dve_small")
    w_split = sem("w_split")
    xn_ready, xt_psum, xt_hi, xt_lo, u_psum, u_ready = (
        sem(n) for n in ("xn_ready", "xt_psum", "xt_hi", "xt_lo", "u_psum", "u_ready"))
    acc_zero = sem("acc_zero")
    hi_ready, lo_ready, step_done = sem("hi_ready"), sem("lo_ready"), sem("step_done")
    g_hi, g_lo = sem("g_hi"), sem("g_lo")
    deg_ready, deg_sqrt, dinv_ready = sem("deg_ready"), sem("deg_sqrt"), sem("dinv_ready")
    bank_done, bank_free = sem("bank_done"), sem("bank_free")
    sum_ready, relu_ready, square_ready, norm_ready, norm_sqrt = (
        sem(n) for n in ("sum_ready", "relu_ready", "square_ready", "norm_ready", "norm_sqrt"))
    block = ctx.enter_context(nc.Block())

    def two_banks(n):
        return ps[:, 2 * n:2 * n + 2, :].rearrange("p b n -> p (b n)")

    def nat_of(t, h):
        return adj[bass.ds(t * P, P), h * HALF:(h + 1) * HALF]

    @block.sync
    def _(sp):
        if layer == 0:
            sp.dma_start(x_sb[:, :, :], x_dram.rearrange("(t p) d -> p t d", p=P)).then_inc(x_in, 16)
        sp.dma_start(Wraw, W.rearrange("(c p) n -> p c n", p=P)).then_inc(w_in, 16)
        if layer == 1:
            sp.dma_start(bias[:, :], row_over_partitions(b)).then_inc(w_in, 16)

        def load_nat(t, h, first=False):
            if not first:
                sp.wait_ge(nat_sum, 2 * t + h - 1)
            sp.dma_start(nat[h][:, :], nat_of(t, h)).then_inc(nat_full[h], 16)

        def load_raw(jt, half, s, n=None):
            if n is not None:
                sp.wait_ge(lo_ready, 2 * n - 2 * SLOTS + 2)
            sp.dma_start(raw[s][:, :], adjT[bass.ds(jt * P, P), bass.ds(half * HALF, HALF)]).then_inc(raw_full[s], 16)

        def blk(bb, with_nat, first=False):
            for j in range(GS):
                jt = (bb // 2) * GS + j
                load_raw(jt, bb % 2, j, None if first else GS * bb + j)
                if with_nat:
                    load_nat(2 * bb + GS + j // 2, j % 2)

        if layer == 0:
            for t in range(GS):
                for h in range(2):
                    load_nat(t, h, first=(t == 0))
        blk(0, layer == 0, first=True)
        last = NBLK - 2 if layer == 0 else 1
        if layer == 0:
            with sp.Fori(1, last) as bb:
                blk(bb, True)
        with sp.Fori(last, NBLK) as bb:
            blk(bb, False)

    @block.gpsimd
    def _(pool):
        pool.wait_ge(w_split, 2)
        pool.wait_ge(xt_psum, NQ)
        pool.memset(ACC[:, :, :], 0.0).then_inc(acc_zero, 1)

    @block.scalar
    def _(act):
        def sum_nat(t, h):
            act.wait_ge(nat_full[h], t * 16 + 16)
            act.activation(nat[h][:, :], nat[h][:, :], ACT.Copy,
                           accum_out=degp[:, bass.ds(t, 1), h]).then_inc(nat_sum, 1)

        if layer == 0:
            for t in range(GS):
                for h in range(2):
                    sum_nat(t, h)
        act.wait_ge(w_in, 16 * (1 + layer))
        act.activation(Wp[:, :, 0, :], Wraw, ACT.Copy).then_inc(w_split, 1)
        act.wait_ge(stats_done, 1)
        act.activation(rstd[:, :], var[:, :], ACT.Sqrt).then_inc(sqrt_done, 1)

        def prep(q, par, first):
            act.wait_ge(xt_psum, q + 1)
            if not first:
                act.wait_ge(u_psum, q - 1)
            act.activation(ahi[par][:, :], two_banks(par), ACT.Copy).then_inc(xt_hi, 1)

        def u_copy(q, par):
            if layer == 0:
                act.wait_ge(u_psum, q + 1)
                act.activation(U[:, bass.ds(q * QUAD, QUAD), :], two_banks(2 + par).rearrange("p (t n) -> p t n", n=D),
                               ACT.Copy).then_inc(u_ready, 1)

        prep(0, 0, True)
        prep(1, 1, True)
        u_copy(0, 0)
        with act.Fori(1, NQ // 2) as pair:
            q = 2 * pair
            prep(q, 0, False)
            u_copy(q - 1, 1)
            prep(q + 1, 1, False)
            u_copy(q, 0)
        u_copy(NQ - 1, 1)

        def g_tile(t):
            act.activation(G[:, bass.ds(t % GT, 1), 0, :], U[:, bass.ds(t, 1), :], ACT.Copy,
                           scale=dinv[:, bass.ds(t, 1)]).then_inc(g_hi, 1)

        def deg_sqrt_of(t):
            act.wait_ge(deg_ready, t // 2 + 1)
            act.activation(dinv[:, bass.ds(t, 2)], deg[:, bass.ds(t, 2)], ACT.Sqrt).then_inc(deg_sqrt, 1)

        act.wait_ge(u_ready, NQ)
        if layer == 0:
            deg_sqrt_of(0)
            act.wait_ge(dinv_ready, 1)
        for t in range(2):
            g_tile(t)

        def blk(bb, with_nat, with_g=True):
            if with_g and layer == 0:
                deg_sqrt_of(2 * bb + 2)
            for j in range(GS):
                act.wait_ge(raw_full[j], bb * 16 + 16)
                for q in range(2):
                    act.wait_ge(step_done, 2 * GS * bb + 2 * j + q + 1)
                    act.activation(ahi[(2 * j + q) % SLOTS][:, :], raw[j][:, q * PIECE:(q + 1) * PIECE],
                                   ACT.Copy).then_inc(hi_ready, 1)
                if j == 0 and with_g:
                    if layer == 0:
                        act.wait_ge(dinv_ready, bb + 2)
                    for v in range(2):
                        g_tile(2 * bb + 2 + v)
                if with_nat:
                    sum_nat(2 * bb + GS + j // 2, j % 2)

        mid = NBLK - 2 if layer == 0 else 0
        if layer == 0:
            with act.Fori(0, mid) as bb:
                blk(bb, True)
        with act.Fori(mid, NBLK - 1) as bb:
            blk(bb, False)
        blk(NBLK - 1, False, with_g=False)
        if layer == 0:
            def finish(t, u, first):
                act.wait_ge(sum_ready, t + 1)
                act.activation(ACC[:, bass.ds(t, 1), :], ACC[:, bass.ds(t, 1), :], ACT.Relu,
                               scale=dinv[:, bass.ds(t, 1)]).then_inc(relu_ready, 1)
                act.wait_ge(relu_ready, t + 1)
                act.activation(sq[u][:, :], ACC[:, bass.ds(t, 1), :], ACT.Square,
                               accum_out=deg[:, bass.ds(t, 1)]).then_inc(square_ready, 1)

            with act.Fori(0, T // 2) as pair:
                t = 2 * pair
                for u in range(2):
                    finish(t + u, u, False)
            act.wait_ge(square_ready, T)
            act.activation(tmp[:, :], deg[:, :], ACT.Sqrt).then_inc(norm_sqrt, 1)

    @block.vector
    def _(dve):
        own = Tally(dve, dve_own)
        if layer == 0:
            dve.wait_ge(x_in, 16)
        for t in range(T):
            own.add(dve.bn_stats(stats[:, t, :], x_sb[:, t, :]))
        own.settle()
        for t in range(T):
            own.add(dve.bn_aggr(mv[:, t, :], stats[:, t, :]))
        own.settle()
        dve.tensor_scalar(var[:, :], mv[:, :, 1], LN_EPS, None, ALU.add).then_inc(stats_done, 1)
        dve.wait_ge(w_split, 1)
        dve.tensor_tensor(Wp[:, :, 1, :], Wraw, Wp[:, :, 0, :], ALU.subtract).then_inc(w_split, 1)
        dve.wait_ge(stats_done, 1)
        newton_rsqrt(dve, own, sqrt_done, 1, var[:, :], rstd[:, :], tmp[:, :])

        def normalise(q, par, first):
            if not first:
                dve.wait_ge(xt_psum, q - 1)
            for v in range(QUAD):
                t = q * QUAD + v
                ins = dve.tensor_scalar(xn[par][:, v, :], x_sb[:, bass.ds(t, 1), :], mv[:, bass.ds(t, 1), 0],
                                        rstd[:, bass.ds(t, 1)], ALU.subtract, ALU.mult)
            ins.then_inc(xn_ready, 1)

        def split(q, par):
            dve.wait_ge(xt_hi, q + 1)
            dve.tensor_tensor(alo[par][:, :], two_banks(par), ahi[par][:, :], ALU.subtract).then_inc(xt_lo, 1)

        def u_bias(q, par):
            if layer == 1:
                dve.wait_ge(u_psum, q + 1)
                dve.tensor_tensor(U[:, bass.ds(q * QUAD, QUAD), :], two_banks(2 + par).rearrange("p (t n) -> p t n", n=D),
                                  bias[:, :].unsqueeze(1).broadcast_to([P, QUAD, D]), ALU.add).then_inc(u_ready, 1)

        if layer == 1:
            dve.wait_ge(w_in, 32)
        normalise(0, 0, True)
        normalise(1, 1, True)
        split(0, 0)
        normalise(2, 0, False)
        split(1, 1)
        u_bias(0, 0)
        normalise(3, 1, False)
        with dve.Fori(1, NQ // 2 - 1) as pair:
            for par in range(2):
                q = 2 * pair + par
                split(q, par)
                u_bias(q - 1, 1 - par)
                normalise(q + 2, par, False)
        for q in (NQ - 2, NQ - 1):
            split(q, q % 2)
            u_bias(q - 1, 1 - q % 2)
        u_bias(NQ - 1, 1)

        small = Tally(dve, dve_small)

        def degrees(t, n):
            d2 = deg[:, bass.ds(t, 2)]
            dve.wait_ge(nat_sum, 2 * t + 4)
            dve.tensor_tensor(d2, degp[:, bass.ds(t, 2), 0], degp[:, bass.ds(t, 2), 1], ALU.add).then_inc(dve_small, 1)
            dve.wait_ge(dve_small, n + 1)
            dve.tensor_scalar(d2, d2, 1.0, None, ALU.add).then_inc(deg_ready, 1)

        def inverse_root(t, n):
            d2, r2, t2 = deg[:, bass.ds(t, 2)], dinv[:, bass.ds(t, 2)], tmp[:, bass.ds(t, 2)]
            dve.wait_ge(deg_sqrt, t // 2 + 1)
            dve.reciprocal(r2, r2).then_inc(dve_small, 1)
            dve.wait_ge(dve_small, n + 2)
            dve.tensor_tensor(t2, r2, r2, ALU.mult).then_inc(dve_small, 1)
            dve.wait_ge(dve_small, n + 3)
            dve.tensor_tensor(t2, t2, d2, ALU.mult).then_inc(dve_small, 1)
            dve.wait_ge(dve_small, n + 4)
            dve.tensor_scalar(t2, t2, -0.5, 1.5, ALU.mult, ALU.add).then_inc(dve_small, 1)
            dve.wait_ge(dve_small, n + 5)
            dve.tensor_tensor(r2, r2, t2, ALU.mult).then_inc(dinv_ready, 1)

        PER_DEG = 5

        def g_tile(t):
            dve.wait_ge(g_hi, t + 1)
            dve.scalar_tensor_tensor(G[:, bass.ds(t % GT, 1), 1, :], U[:, bass.ds(t, 1), :], dinv[:, bass.ds(t, 1)],
                                     G[:, bass.ds(t % GT, 1), 0, :], ALU.mult, ALU.subtract).then_inc(g_lo, 1)

        dve.wait_ge(acc_zero, 1)
        dve.wait_ge(u_ready, NQ)
        if layer == 0:
            degrees(0, 0)
            inverse_root(0, 0)
            dve.wait_ge(dinv_ready, 1)
        for t in range(2):
            g_tile(t)

        def lo(bb, j, q):
            dve.wait_ge(hi_ready, 2 * GS * bb + 2 * j + q + 1)
            dve.tensor_tensor(alo[(2 * j + q) % SLOTS][:, :], raw[j][:, q * PIECE:(q + 1) * PIECE],
                              ahi[(2 * j + q) % SLOTS][:, :], ALU.subtract).then_inc(lo_ready, 1)

        def evacuate(bb, banks):
            for k in banks:
                if k % HALF_BANKS == HALF_BANKS - 1:
                    dve.wait_ge(step_done, SLOTS + 2 * GS * (bb + 1) - 1 + k // HALF_BANKS)
                else:
                    dve.wait_ge(bank_done, (BANKS - 2) * bb + k - k // HALF_BANKS + 1)
                half = ACC[:, bass.ds((bb % 2) * IT + PER_BANK * k, PER_BANK), :]
                dve.tensor_tensor(half, ps[:, k, :].rearrange("p (t n) -> p t n", n=D), half,
                                  ALU.add).then_inc(bank_free, 1)

        def blk(bb, first=False, with_g=True):
            if with_g and layer == 0:
                degrees(2 * bb + 2, PER_DEG * (bb + 1))
            for q in range(2):
                lo(bb, 0, q)
            if with_g and layer == 0:
                inverse_root(2 * bb + 2, PER_DEG * (bb + 1))
            if not first:
                evacuate(bb - 1, range(0, BANKS // 2))
            lo(bb, 1, 0)
            if not first:
                evacuate(bb - 1, range(BANKS // 2, BANKS))
            if with_g:
                for v in range(2):
                    g_tile(2 * bb + 2 + v)
            lo(bb, 1, 1)
            for j in range(2, GS):
                for q in range(2):
                    lo(bb, j, q)

        blk(0, first=True)
        with dve.Fori(1, NBLK - 1) as bb:
            blk(bb)
        blk(NBLK - 1, with_g=False)
        evacuate(NBLK - 1, range(BANKS))

        dve.wait_ge(bank_free, BANKS * (NBLK + 1))

        def finish(t):
            dve.scalar_tensor_tensor(ACC[:, bass.ds(t, 1), :], U[:, bass.ds(t, 1), :], dinv[:, bass.ds(t, 1)],
                                     ACC[:, bass.ds(t, 1), :], ALU.mult, ALU.add).then_inc(sum_ready, 1)
            if layer == 1:
                dve.wait_ge(sum_ready, t + 1)
                dve.scalar_tensor_tensor(x_sb[:, bass.ds(t, 1), :], ACC[:, bass.ds(t, 1), :], dinv[:, bass.ds(t, 1)],
                                         x_sb[:, bass.ds(t, 1), :], ALU.mult, ALU.add)

        with dve.Fori(0, T) as t:
            finish(t)
        if layer == 0:
            dve.wait_ge(norm_sqrt, 1)
            own.link(dve.tensor_scalar(tmp[:, :], tmp[:, :], NORM_EPS, None, ALU.max))
            own.link(dve.reciprocal(tmp[:, :], tmp[:, :]))
            with dve.Fori(0, T) as t:
                dve.scalar_tensor_tensor(x_sb[:, bass.ds(t, 1), :], ACC[:, bass.ds(t, 1), :], tmp[:, bass.ds(t, 1)],
                                         x_sb[:, bass.ds(t, 1), :], ALU.mult, ALU.add)

    @block.tensor
    def _(pe):
        def transposes(q, par, first):
            pe.wait_ge(xn_ready, q + 1)
            if not first:
                pe.wait_ge(xt_lo, q - 1)
            for v in range(QUAD):
                for c in range(DC):
                    at = (v % 2) * D + c * P
                    mm = pe.transpose(ps[:, 2 * par + v // 2, at:at + P], xn[par][:, v, c * P:(c + 1) * P], ident[:, :])
            mm.then_inc(xt_psum, 1)

        def product(q, par, first):
            pe.wait_ge(xt_lo, q + 1)
            if not first:
                pe.wait_ge(u_ready, q - 1)
            for v in range(QUAD):
                n = 0
                for c in range(DC):
                    for a, w in ((ahi, 0), (ahi, 1), (alo, 0)):
                        mm = pe.matmul(ps[:, 4 + 2 * par + v // 2, (v % 2) * D:(v % 2 + 1) * D],
                                       a[par][:, (v * DC + c) * P:(v * DC + c + 1) * P], Wp[:, c, w, :],
                                       start=(n == 0), stop=(n == 3 * DC - 1))
                        n += 1
            mm.then_inc(u_psum, 1)

        pe.wait_ge(w_split, 2)
        transposes(0, 0, True)
        transposes(1, 1, True)
        product(0, 0, True)
        transposes(2, 0, False)
        product(1, 1, True)
        transposes(3, 1, False)
        with pe.Fori(1, NQ // 2 - 1) as pair:
            for par in range(2):
                q = 2 * pair + par
                product(q, par, False)
                transposes(q + 2, par, False)
        product(NQ - 2, 0, False)
        product(NQ - 1, 1, False)
        pe.wait_ge(u_ready, NQ)
        pe.wait_ge(g_lo, 2)
        pe.sem_inc(step_done, SLOTS)
        pe.sem_inc(bank_free, BANKS)

        with pe.Fori(0, NBLK) as bb:
            g0 = ((bb // 2) % 2) * GS
            for j in range(GS):
                pe.wait_ge(g_lo, (bb // 2) * GS + j + 1)
                ghi, glo = (G[:, bass.ds(g0 + j, 1), w, :] for w in range(2))
                for q in range(2):
                    s = (2 * j + q) % SLOTS
                    out = [ps[:, (q * BANKS // 2) + i // PER_BANK, (i % PER_BANK) * D:(i % PER_BANK + 1) * D]
                           for i in range(IT // 2)]
                    a = [slice(i * P, (i + 1) * P) for i in range(IT // 2)]
                    pe.wait_ge(hi_ready, 2 * GS * bb + 2 * j + q + 1)
                    for i in range(IT // 2):
                        lead = j == 0 and i % PER_BANK == 0
                        if lead:
                            pe.wait_ge(bank_free, BANKS * bb + (q * BANKS // 2) + i // PER_BANK + 1)
                        pe.matmul(out[i], ahi[s][:, a[i]], ghi, start=lead, stop=False, skip_group_check=True)
                        pe.matmul(out[i], ahi[s][:, a[i]], glo, start=False, stop=False, skip_group_check=True)
                    pe.wait_ge(lo_ready, 2 * GS * bb + 2 * j + q + 1)
                    for i in range(IT // 2):
                        mm = pe.matmul(out[i], alo[s][:, a[i]], ghi, start=False, stop=(j == GS - 1),
                                       skip_group_check=True)
                        if j == GS - 1 and i % PER_BANK == PER_BANK - 1 and i < IT // 2 - 1:
                            mm.then_inc(bank_done, 1)
                    mm.then_inc(step_done, 1)
    return sems


def ffn(nc, ctx, layer, w, x_sb, ident, ps, out_dram):
    E, D, H = w["W1"].shape
    N = x_sb.shape[1] * P
    T = N // P
    DC, HC = D // P, H // P
    BLK = 512
    NT = N // BLK
    TB = BLK // P
    KE = E if layer == 0 else TOP
    L = f"f{layer}_"

    def sb(name, shape, dt=F32):
        return ctx.enter_context(nc.sbuf_tensor(L + name, shape, dt))

    def sem(name):
        return ctx.enter_context(nc.semaphore(L + name))

    XT = [sb(f"XT{h}", [P, DC, N], F32R) for h in range(2)]
    Y = sb("Y", [P, T, D])
    W1r = sb("W1r", [P, DC, H])
    W2r = sb("W2r", [P, HC, D])
    W1 = [[sb(f"W1_{s}{h}", [P, DC, H], F32R) for h in range(2)] for s in range(2)]
    W2 = [[sb(f"W2_{s}{h}", [P, HC, D], F32R) for h in range(2)] for s in range(2)]
    b1 = [sb(f"b1_{s}", [P, HC]) for s in range(2)]
    b2 = [sb(f"b2_{s}", [P, D]) for s in range(2)]
    act_out = [sb(f"act{s}", [P, BLK]) for s in range(2)]
    hT = [[sb(f"hT{s}{h}", [P, BLK], F32R) for h in range(2)] for s in range(HC)]
    stats = sb("stats", [P, T, 6])
    mv = sb("mv", [P, T, 2])
    var = sb("var", [P, T])
    rstd = sb("rstd", [P, T])
    tmp = sb("tmp", [P, T])
    xn = [sb(f"xn{s}", [P, D]) for s in range(2)]
    xt = [sb(f"xt{s}", [P, DC, P]) for s in range(2)]
    Wg = sb("Wg", [P, DC, E])
    bg = sb("bg", [P, E])
    bg2 = sb("bg2", [P, E])
    comb = sb("comb", [P, T, E]) if layer == 0 else sb("comb", [P, 1, TOP])
    iota = sb("iota", [P, E])
    ones = sb("ones", [P, 1])
    if layer == 0:
        logit = sb("logit", [P, T, E])
        best = sb("best", [P, T, 8])
        besti = sb("besti", [P, T, 8], U32)
        bestf = sb("bestf", [P, T, TOP])
        wtop = sb("wtop", [P, T, TOP])
        pick = sb("pick", [P, T, E])
    else:
        rt = sb("rt", [P, 12, E])
        besti = sb("besti", [P, 8], U32)
        meanT = sb("meanT", [P, DC, P])
        gamma = sb("gamma", [P, D])
        beta = sb("beta", [P, D])
        y2 = [sb(f"y2{s}", [P, D]) for s in range(2)]

    g_in = sem("g_in")
    dve_own, pool_own, act_own = sem("dve_own"), sem("pool_own"), sem("act_own")
    stats_done, sqrt_done = sem("stats_done"), sem("sqrt_done")
    xn_ready, xt_psum, xt_sb, xt_hi, xt_lo, gate_psum = (
        sem(n) for n in ("xn_ready", "xt_psum", "xt_sb", "xt_hi", "xt_lo", "gate_psum"))
    consts, y_zero = sem("consts"), sem("y_zero")
    mean_ready, mean_b, soft_in, soft_out = sem("mean_ready"), sem("mean_b"), sem("soft_in"), sem("soft_out")
    comb_ready = sem("comb_ready")
    w_in, b_in = sem("w_in"), [sem(f"b_in{s}") for s in range(2)]
    w_hi, w_lo = sem("w_hi"), sem("w_lo")
    h_psum, h_act, h_hi, h_lo, h_used = (sem(n) for n in ("h_psum", "h_act", "h_hi", "h_lo", "h_used"))
    y_psum, y_added = sem("y_psum"), sem("y_added")
    last_stats, last_sqrt, out_ready = (sem(n) for n in ("last_stats", "last_sqrt", "out_ready"))
    out_done = [sem(f"out_done{s}") for s in range(2)]
    block = ctx.enter_context(nc.Block())
    HB0, YB0 = 0, 4

    @block.sync
    def _(sp):
        sp.dma_start(Wg[:, :, :], w["Wg"].rearrange("(c p) e -> p c e", p=P)).then_inc(g_in, 16)
        sp.dma_start(bg[:, :], row_over_partitions(w["bg"])).then_inc(g_in, 16)
        if layer == 0:
            sp.dma_start(bg2[:, :], row_over_partitions(w["bias"])).then_inc(g_in, 16)
        else:
            sp.dma_start(gamma[:, :], row_over_partitions(w["gamma"])).then_inc(g_in, 16)
            sp.dma_start(beta[:, :], row_over_partitions(w["beta"])).then_inc(g_in, 16)
            sp.wait_ge(comb_ready, 1)
        for k in range(KE):
            e = k if layer == 0 else sp.value_load(besti[0:1, k:k + 1], min_val=0, max_val=E - 1)
            if k >= 1:
                sp.wait_ge(w_lo, 2 * k)
            sp.dma_start(W1r[:, :, :], w["W1"][bass.ds(e, 1), :, :].rearrange("a (c p) h -> p (a c) h", p=P)).then_inc(w_in, 16)
            sp.dma_start(W2r[:, :, :], w["W2"][bass.ds(e, 1), :, :].rearrange("a (c p) h -> p (a c) h", p=P)).then_inc(w_in, 16)
            if k >= 2:
                sp.wait_ge(y_added, NT * TB // 2 * (k - 1))
            sp.dma_start(b1[k % 2][:, :], w["b1"][bass.ds(e, 1), :, :].rearrange("a p c -> p (a c)")).then_inc(b_in[k % 2], 16)
            sp.dma_start(b2[k % 2][:, :], w["b2"][bass.ds(e, 1), :].broadcast_to([P, D])).then_inc(b_in[k % 2], 16)
        if layer == 1:
            with sp.Fori(0, T // 2) as pair:
                t = 2 * pair
                for u in range(2):
                    sp.wait_ge(out_ready, t + u + 1)
                    sp.dma_start(out_dram[bass.ds((t + u) * P, P), :], y2[u][:, :]).then_inc(out_done[u], 16)
            for u in range(2):
                sp.wait_ge(out_done[u], 16 * (T // 2))

    @block.gpsimd
    def _(pool):
        pool.memset(ones[:, :], 1.0).then_inc(consts, 1)
        pool.iota(iota[:, :], [[1, E]], base=0, channel_multiplier=0,
                  allow_small_or_imprecise_dtypes=True).then_inc(consts, 1)
        pool.memset(Y[:, :, :], 0.0).then_inc(y_zero, 1)
        with pool.Fori(0, T // 2) as pair:
            t = 2 * pair
            for u in range(2):
                pool.wait_ge(xt_sb, t + u + 1)
                pool.tensor_copy(XT[0][:, :, bass.ds((t + u) * P, P)], xt[u][:, :, :]).then_inc(xt_hi, 1)

    @block.scalar
    def _(act):
        act.wait_ge(stats_done, 1)
        act.activation(rstd[:, :], var[:, :], ACT.Sqrt).then_inc(sqrt_done, 1)

        def evac(t, u, first):
            act.wait_ge(xt_psum, t + 1)
            if not first:
                act.wait_ge(xt_lo, t - 1)
                if layer == 0:
                    act.wait_ge(gate_psum, t - 1)
            act.activation(xt[u][:, :, :], ps[:, u, 0:D].rearrange("p (c n) -> p c n", c=DC), ACT.Copy).then_inc(xt_sb, 1)

        for u in range(2):
            evac(u, u, True)
        with act.Fori(1, T // 2) as pair:
            t = 2 * pair
            for u in range(2):
                evac(t + u, u, False)
        if layer == 0:
            act.wait_ge(soft_in, 1)
            act.activation(wtop[:, :, 1], wtop[:, :, 0], ACT.Exp).then_inc(soft_out, 1)
        else:
            act.wait_ge(mean_ready, 1)
            act.activation(meanT[:, :, :], ps[:, 2, 0:DC].unsqueeze(2).broadcast_to([P, DC, P]), ACT.Copy,
                           scale=1.0 / N).then_inc(mean_b, 1)
            for n, (dst, src) in enumerate([(2, 1), (6, 5), (10, 9)]):
                act.wait_ge(soft_in, n + 1)
                act.activation(rt[:, dst, :], rt[:, src, :], ACT.Exp).then_inc(soft_out, 1)

        func = ACT.Relu if layer == 0 else ACT.Gelu

        def split_hi(k):
            act.wait_ge(w_in, 32 * (k + 1))
            if k >= 2:
                act.wait_ge(h_used, HC + HC * NT * (k - 1))
            act.activation(W1[k % 2][0][:, :, :], W1r[:, :, :], ACT.Copy).then_inc(w_hi, 1)
            act.activation(W2[k % 2][0][:, :, :], W2r[:, :, :], ACT.Copy).then_inc(w_hi, 1)

        split_hi(0)
        for k in range(KE):
            act.wait_ge(b_in[k % 2], 32 * (k // 2 + 1))
            with act.Fori(0, NT) as tb:
                for c in range(HC):
                    act.wait_ge(h_psum, HC * NT * k + HC * tb + c + 1)
                    act.wait_ge(h_lo, HC * NT * k + HC * tb + c + 1)
                    act.activation(act_out[c % 2][:, :], ps[:, HB0 + c, :], func,
                                   bias=b1[k % 2][:, c:c + 1]).then_inc(h_act, 1)
            if k + 1 < KE:
                split_hi(k + 1)
        if layer == 1:
            act.wait_ge(last_stats, 1)
            act.activation(rstd[:, :], var[:, :], ACT.Sqrt).then_inc(last_sqrt, 1)

    @block.vector
    def _(dve):
        own = Tally(dve, dve_own)
        for t in range(T):
            own.add(dve.bn_stats(stats[:, t, :], x_sb[:, t, :]))
        own.settle()
        for t in range(T):
            own.add(dve.bn_aggr(mv[:, t, :], stats[:, t, :]))
        own.settle()
        dve.tensor_scalar(var[:, :], mv[:, :, 1], LN_EPS, None, ALU.add).then_inc(stats_done, 1)
        dve.wait_ge(stats_done, 1)
        newton_rsqrt(dve, own, sqrt_done, 1, var[:, :], rstd[:, :], tmp[:, :])

        def normalise(t, u, first):
            if not first:
                dve.wait_ge(xt_psum, t - 1)
                if layer == 1:
                    dve.wait_ge(gate_psum, t - 1)
            dve.tensor_scalar(xn[u][:, :], x_sb[:, bass.ds(t, 1), :], mv[:, bass.ds(t, 1), 0], rstd[:, bass.ds(t, 1)],
                              ALU.subtract, ALU.mult).then_inc(xn_ready, 1)

        def split(t, u):
            dve.wait_ge(xt_hi, t + 1)
            dve.tensor_tensor(XT[1][:, :, bass.ds(t * P, P)], xt[u][:, :, :], XT[0][:, :, bass.ds(t * P, P)],
                              ALU.subtract).then_inc(xt_lo, 1)

        for u in range(2):
            normalise(u, u, True)
        for u in range(2):
            split(u, u)
        with dve.Fori(1, T // 2) as pair:
            t = 2 * pair
            for u in range(2):
                normalise(t + u, u, False)
            for u in range(2):
                split(t + u, u)
        dve.wait_ge(g_in, 48 if layer == 0 else 64)
        dve.wait_ge(consts, 2)
        if layer == 0:
            def over_tiles(a):
                return a.unsqueeze(1).broadcast_to([P, T, E])

            dve.wait_ge(gate_psum, T)
            own.link(dve.tensor_tensor(logit[:, :, :], ps[:, 2, 0:T * E].rearrange("p (t e) -> p t e", e=E),
                                       over_tiles(bg[:, :]), ALU.add))
            own.link(dve.tensor_tensor(logit[:, :, :], logit[:, :, :], over_tiles(bg2[:, :]), ALU.add))
            for t in range(T):
                own.add(dve.max(best[:, t, :], logit[:, t, :]))
            own.settle()
            for t in range(T):
                own.add(dve.max_index(besti[:, t, :], best[:, t, :], logit[:, t, :]))
            dve.tensor_tensor(wtop[:, :, 0], best[:, :, 1], best[:, :, 0], ALU.subtract).then_inc(soft_in, 1)
            dve.wait_ge(soft_out, 1)
            own.link(dve.tensor_scalar(tmp[:, :], wtop[:, :, 1], 1.0, None, ALU.add))
            own.link(dve.reciprocal(wtop[:, :, 0], tmp[:, :]))
            own.link(dve.tensor_tensor(wtop[:, :, 1], wtop[:, :, 1], wtop[:, :, 0], ALU.mult))
            own.link(dve.tensor_copy(bestf[:, :, :], besti[:, :, 0:TOP]))
            for k in range(TOP):
                dst = comb if k == 0 else pick
                own.link(dve.tensor_tensor(dst[:, :, :], bestf[:, :, k:k + 1].broadcast_to([P, T, E]),
                                           over_tiles(iota[:, :]), ALU.is_equal))
                own.link(dve.tensor_tensor(dst[:, :, :], dst[:, :, :], wtop[:, :, k:k + 1].broadcast_to([P, T, E]),
                                           ALU.mult))
            own.link(dve.tensor_tensor(comb[:, :, :], comb[:, :, :], pick[:, :, :], ALU.add))
        else:
            r = [rt[:, i, :] for i in range(12)]
            c = [rt[:, 11, i:i + 1] for i in range(8)]
            tokens = float(N)
            cap = float(-(-int(N * CAPACITY_FACTOR * 4) // (E * 4)))

            def softmax(src, diff, ex, n, m, s, dst):
                own.link(dve.reduce_max(m, src, AX_X))
                own.link(dve.tensor_scalar(diff, src, m, None, ALU.subtract))
                dve.sem_inc(soft_in, 1)
                dve.wait_ge(soft_out, n)
                own.link(dve.reduce_sum(s, ex, AX_X))
                own.link(dve.reciprocal(s, s))
                own.link(dve.tensor_scalar(dst, ex, s, None, ALU.mult))

            dve.wait_ge(gate_psum, T + 1)
            own.link(dve.tensor_tensor(r[0], ps[:, 3, 0:E], bg[:, :], ALU.add))
            softmax(r[0], r[1], r[2], 1, c[0], c[1], r[3])
            own.link(dve.tensor_scalar(r[4], r[3], tokens, None, ALU.mult))
            own.link(dve.reciprocal(r[4], r[4]))
            own.link(dve.tensor_scalar(r[4], r[4], cap, 1.0, ALU.mult, ALU.min))
            own.link(dve.tensor_tensor(r[4], r[4], r[3], ALU.mult))
            softmax(r[4], r[5], r[6], 2, c[2], c[3], r[7])
            own.link(dve.max(r[8], r[7]))
            own.link(dve.max_index(besti[:, :], r[8], r[7]))
            own.link(dve.tensor_scalar(r[9], r[8], c8 := rt[:, 8, 0:1], None, ALU.subtract))
            dve.sem_inc(soft_in, 1)
            dve.wait_ge(soft_out, 3)
            own.link(dve.reduce_sum(c[4], rt[:, 10, 0:TOP], AX_X))
            own.link(dve.reciprocal(c[4], c[4]))
            own.link(dve.tensor_scalar(comb[:, 0, :], rt[:, 10, 0:TOP], c[4], None, ALU.mult))
        dve.sem_inc(comb_ready, 1)
        dve.wait_ge(y_zero, 1)

        def split_lo(k):
            for n, (Wk, Wr) in enumerate(((W1, W1r), (W2, W2r))):
                dve.wait_ge(w_hi, 2 * k + n + 1)
                dve.tensor_tensor(Wk[k % 2][1][:, :, :], Wr[:, :, :], Wk[k % 2][0][:, :, :],
                                  ALU.subtract).then_inc(w_lo, 1)

        def split_h(m, c):
            dve.wait_ge(h_act, m + 1)
            dve.wait_ge(h_used, m + 1)
            dve.tensor_copy(hT[c][0][:, :], act_out[c % 2][:, :]).then_inc(h_hi, 1)
            dve.wait_ge(h_hi, m + 1)
            dve.tensor_tensor(hT[c][1][:, :], act_out[c % 2][:, :], hT[c][0][:, :], ALU.subtract).then_inc(h_lo, 1)

        def add_y(k, tb, n):
            m = TB // 2 * n
            for g in range(TB // 2):
                if g < TB // 2 - 1:
                    dve.wait_ge(y_psum, n + g + 1)
                else:
                    dve.wait_ge(h_used, HC * n + 2 * HC)
                pair = ps[:, YB0 + g, :].rearrange("p (a n) -> p a n", n=D)
                dve.tensor_tensor(pair, pair, b2[k % 2][:, :].unsqueeze(1).broadcast_to([P, 2, D]),
                                  ALU.add).then_inc(act_own, 1)
                dve.wait_ge(act_own, m + g + 1)
                for v in range(2):
                    t = TB * tb + 2 * g + v
                    cw = comb[:, bass.ds(t, 1), k] if layer == 0 else comb[:, 0, k:k + 1]
                    ins = dve.scalar_tensor_tensor(Y[:, bass.ds(t, 1), :], pair[:, v:v + 1, :], cw,
                                                   Y[:, bass.ds(t, 1), :], ALU.mult, ALU.add)
                ins.then_inc(y_added, 1)

        dve.sem_inc(h_lo, 2)
        split_lo(0)
        for k in range(KE):
            dve.wait_ge(b_in[k % 2], 32 * (k // 2 + 1))
            for c in range(HC):
                split_h(HC * NT * k + c, c)
            with dve.Fori(1, NT) as tb:
                for c in range(HC):
                    split_h(HC * NT * k + HC * tb + c, c)
                    if c == 1:
                        add_y(k, tb - 1, NT * k + tb - 1)
            add_y(k, NT - 1, NT * k + NT - 1)
            if k + 1 < KE:
                split_lo(k + 1)
        dve.wait_ge(y_added, KE * NT * TB // 2)
        if layer == 0:
            for t in range(0, T, 4):
                dve.tensor_tensor(x_sb[:, t:t + 4, :], x_sb[:, t:t + 4, :], Y[:, t:t + 4, :], ALU.add)
        else:
            for t in range(T):
                xt_, yt = x_sb[:, t, :], Y[:, t, :]
                own.link(dve.tensor_scalar(xn[t % 2][:, :], xt_, mv[:, t, 0:1], rstd[:, t:t + 1], ALU.subtract, ALU.mult))
                own.link(dve.tensor_tensor(yt, yt, xn[t % 2][:, :], ALU.add))
                own.add(dve.bn_stats(stats[:, t, :], yt))
            own.settle()
            for t in range(T):
                own.add(dve.bn_aggr(mv[:, t, :], stats[:, t, :]))
            own.settle()
            own.link(dve.tensor_scalar(var[:, :], mv[:, :, 1], LN_EPS, None, ALU.add))
            dve.sem_inc(last_stats, 1)
            newton_rsqrt(dve, own, last_sqrt, 1, var[:, :], rstd[:, :], tmp[:, :])
            for t in range(T):
                yt, o = Y[:, t, :], y2[t % 2][:, :]
                own.link(dve.tensor_scalar(yt, yt, mv[:, t, 0:1], rstd[:, t:t + 1], ALU.subtract, ALU.mult))
                own.link(dve.tensor_tensor(yt, yt, gamma[:, :], ALU.mult))
                own.link(dve.tensor_tensor(yt, yt, beta[:, :], ALU.add))
                if t >= 2:
                    dve.wait_ge(out_done[t % 2], 16 * (t // 2))
                dve.tensor_tensor(o, yt, x_sb[:, t, :], ALU.add).then_inc(out_ready, 1)

    @block.tensor
    def _(pe):
        pe.wait_ge(g_in, 48 if layer == 0 else 64)
        pe.wait_ge(consts, 2)

        def transposes(t, u, first):
            pe.wait_ge(xn_ready, t + 1)
            if not first:
                pe.wait_ge(xt_sb, t - 1)
            for c in range(DC):
                mm = pe.transpose(ps[:, u, c * P:(c + 1) * P], xn[u][:, c * P:(c + 1) * P], ident[:, :])
            mm.then_inc(xt_psum, 1)

        def gate(t, u, first):
            if layer == 0:
                pe.wait_ge(xt_sb, t + 1)
                for c in range(DC):
                    mm = pe.matmul(ps[:, 2, bass.ds(t * E, E)], xt[u][:, c, :], Wg[:, c, :],
                                   start=(c == 0), stop=(c == DC - 1), skip_group_check=True)
            else:
                for c in range(DC):
                    mm = pe.matmul(ps[:, 2, c:c + 1], xn[u][:, c * P:(c + 1) * P], ones[:, :],
                                   start=(first and u == 0 and c == 0), stop=False, skip_group_check=True)
            mm.then_inc(gate_psum, 1)

        for u in range(2):
            transposes(u, u, True)
        for u in range(2):
            gate(u, u, True)
        with pe.Fori(1, T // 2) as pair:
            t = 2 * pair
            for u in range(2):
                transposes(t + u, u, False)
            for u in range(2):
                gate(t + u, u, False)
        if layer == 1:
            pe.wait_ge(gate_psum, T)
            pe.sem_inc(mean_ready, 1)
            pe.wait_ge(mean_b, 1)
            for c in range(DC):
                mm = pe.matmul(ps[:, 3, 0:E], meanT[:, c, :], Wg[:, c, :], start=(c == 0), stop=(c == DC - 1))
            mm.then_inc(gate_psum, 1)
        pe.wait_ge(xt_lo, T)
        pe.wait_ge(comb_ready, 1)
        pe.sem_inc(h_used, HC)

        def up(k, tb, c, m):
            n = 0
            if m is not None:
                pe.wait_ge(h_act, m - HC + 1)
            for d in range(DC):
                for a, b in ((0, 0), (0, 1), (1, 0)):
                    mm = pe.matmul(ps[:, HB0 + c, :], W1[k % 2][a][:, d, c * P:(c + 1) * P],
                                   XT[b][:, d, bass.ds(tb * BLK, BLK)], start=(n == 0), stop=(n == 3 * DC - 1))
                    n += 1
            mm.then_inc(h_psum, 1)

        def down(k, tb, c, m, my):
            pe.wait_ge(h_lo, m + 3)
            for t in range(TB):
                if c == 0 and t % 2 == 0 and my is not None:
                    pe.wait_ge(y_added, my + t // 2 - 1)
                for n, (a, b) in enumerate(((0, 0), (0, 1), (1, 0))):
                    mm = pe.matmul(ps[:, YB0 + t // 2, (t % 2) * D:(t % 2 + 1) * D], hT[c][a][:, t * P:(t + 1) * P],
                                   W2[k % 2][b][:, c, :], start=(c == 0 and t % 2 == 0 and n == 0), stop=(c == HC - 1),
                                   skip_group_check=True)
                if c == HC - 1 and t % 2 == 1 and t < TB - 1:
                    mm.then_inc(y_psum, 1)
            mm.then_inc(h_used, 1)

        def block_of(k, tb, m, my, has_next):
            for c in range(HC):
                if c + 2 < HC:
                    up(k, tb, c + 2, m + c + 2 if m is not None else None)
                elif has_next:
                    up(k, tb + 1, c + 2 - HC, (m if m is not None else 0) + c + 2)
                down(k, tb, c, (m if m is not None else 0) + c, my)

        for k in range(KE):
            pe.wait_ge(w_lo, 2 * (k + 1))
            base = HC * NT * k
            for c in range(2):
                up(k, 0, c, base + c if k else None)
            block_of(k, 0, base if k else None, (TB // 2) * NT * k if k else None, True)
            with pe.Fori(1, NT - 1) as tb:
                block_of(k, tb, base + HC * tb, (TB // 2) * (NT * k + tb), True)
            block_of(k, NT - 1, base + HC * (NT - 1), (TB // 2) * (NT * k + NT - 1), False)


def moe0(nc, top, w, X, ident, ps, old_sems):
    E, D, H = w["W1"].shape
    XW = X.shape[2]
    N = X.shape[1] * P
    T = N // P
    DC, HC = D // P, H // P
    QUAD = 4
    NQ = T // QUAD
    TILES = (TOP * N + E * (P - 1)) // P
    RING = 8
    TILES = -(-TILES // RING) * RING
    NOWHERE = 1 << 20
    L = "m_"

    slots = nc.dram_tensor(L + "slots", (TILES * P, XW), F32, kind="Internal").ap()
    rows = nc.dram_tensor(L + "rows", (TOP * N, D), F32, kind="Internal").ap()
    x1 = nc.dram_tensor(L + "x1", (N, D), F32, kind="Internal").ap()

    def sem(name):
        return top.enter_context(nc.semaphore(L + name))

    def keep(name, shape, dt=F32):
        return top.enter_context(nc.sbuf_tensor(L + name, shape, dt))

    def two_banks(n):
        return ps[:, 2 * n:2 * n + 2, :].rearrange("p b n -> p (b n)")

    wtop = keep("wtop", [P, T, TOP])
    posu = keep("posu", [P, TOP, T], U32)
    eid = keep("eid", [P, TILES + 2], I32)

    with ExitStack() as ctx:
        def sb(name, shape, dt=F32):
            return ctx.enter_context(nc.sbuf_tensor(L + name, shape, dt))

        stats = sb("stats", [P, T, 6])
        mv = sb("mv", [P, T, 2])
        var = sb("var", [P, T])
        rstd = sb("rstd", [P, T])
        tmp = sb("tmp", [P, T])
        xn = [sb(f"xn{s}", [P, QUAD, D]) for s in range(2)]
        xt = [sb(f"xt{s}", [P, QUAD * DC * P]) for s in range(2)]
        Wg = sb("Wg", [P, DC, E])
        bg = sb("bg", [P, E])
        bg2 = sb("bg2", [P, E])
        iota_e = sb("iota_e", [P, E])
        iota_k = sb("iota_k", [P, TILES])
        below = sb("below", [P, P])
        ones = sb("ones", [P, P])
        pad = sb("pad", [P, XW])
        ids = sb("ids", [P, T], U32)
        logit = sb("logit", [P, T, E])
        best = sb("best", [P, T, 8])
        besti = sb("besti", [P, T, 8], U32)
        bestf = sb("bestf", [P, T, TOP])
        pick = [sb(f"pick{k}", [P, T, E]) for k in range(TOP)]
        both = sb("both", [P, T, E])
        total = sb("total", [P, T, E])
        upto = sb("upto", [P, T, E])
        pos = sb("pos", [P, T, E])
        posf = sb("posf", [P, TOP, T])
        cnt = sb("cnt", [P, E], I32)
        ntile = sb("ntile", [P, E])
        tend = sb("tend", [P, E])
        start = sb("start", [P, E])
        past = sb("past", [P, TILES, E])
        eidf = sb("eidf", [P, TILES])

        g_in, x_kept, padded = sem("g_in"), [sem(f"x_kept{s}") for s in range(2)], sem("padded")
        dve_own, pool_own = sem("dve_own"), sem("pool_own")
        consts, pad_made = sem("consts"), sem("pad_made")
        stats_done, sqrt_done = sem("stats_done"), sem("sqrt_done")
        xn_ready, xt_psum, xt_sb, gate_psum, row_ready = (
            sem(n) for n in ("xn_ready", "xt_psum", "xt_sb", "gate_psum", "row_ready"))
        soft_in, soft_out, both_ready, prefix = sem("soft_in"), sem("soft_out"), sem("both_ready"), sem("prefix")
        block = ctx.enter_context(nc.Block())

        @block.sync
        def _(sp):
            for h in range(2):
                sp.dma_start(x1.rearrange("(t p) d -> p t d", p=P)[:, h * T // 2:(h + 1) * T // 2, :],
                             X[:, h * T // 2:(h + 1) * T // 2, 0:D]).then_inc(x_kept[h], 16)
            sp.dma_start(Wg[:, :, :], w["Wg"].rearrange("(c p) e -> p c e", p=P)).then_inc(g_in, 16)
            sp.dma_start(bg[:, :], row_over_partitions(w["bg"])).then_inc(g_in, 16)
            sp.dma_start(bg2[:, :], row_over_partitions(w["bias"])).then_inc(g_in, 16)
            sp.wait_ge(pad_made, 3)
            sp.dma_start(slots.rearrange("(k p) n -> p k n", p=P),
                         pad[:, :].unsqueeze(1).broadcast_to([P, TILES, XW])).then_inc(padded, 16)
            sp.wait_ge(padded, 16)
            for h in range(2):
                sp.wait_ge(x_kept[h], 16)

        @block.gpsimd
        def _(pool):
            clear(pool, old_sems)
            pool.memset(ones[:, :], 1.0).then_inc(consts, 1)
            pool.iota(iota_e[:, :], [[1, E]], base=0, channel_multiplier=0,
                      allow_small_or_imprecise_dtypes=True).then_inc(consts, 1)
            pool.iota(iota_k[:, :], [[1, TILES]], base=0, channel_multiplier=0,
                      allow_small_or_imprecise_dtypes=True).then_inc(consts, 1)
            pool.memset(below[:, :], 1.0).then_inc(pool_own, 1)
            pool.wait_ge(pool_own, 1)
            pool.affine_select(out=below[:, :], in_=below[:, :], compare_op=ALU.is_gt, fill=0.0, base=0,
                               pattern=[[1, P]], channel_multiplier=-1).then_inc(consts, 1)
            pool.memset(pad[:, :], 0.0).then_inc(pad_made, 1)
            pool.wait_ge(pad_made, 1)
            pool.iota(pad[:, D:D + 1].bitcast(U32), [[0, 1]], base=NOWHERE, channel_multiplier=0).then_inc(pad_made, 2)
            pool.iota(ids[:, :], [[P, T]], base=0, channel_multiplier=1).then_inc(consts, 1)
            pool.wait_ge(consts, 5)
            pool.memset(X[:, :, D:XW], 0.0).then_inc(pool_own, 1)
            pool.wait_ge(pool_own, 2)
            pool.tensor_copy(X[:, :, D].bitcast(U32), ids[:, :]).then_inc(pool_own, 1)
            for h in range(2):
                pool.wait_ge(x_kept[h], 16)
                with pool.Fori(h * NQ // 4, (h + 1) * NQ // 4) as pair:
                    for par in range(2):
                        q = 2 * pair + par
                        pool.wait_ge(xn_ready, q + 1)
                        pool.tensor_copy(X[:, bass.ds(q * QUAD, QUAD), 0:D], xn[par][:, :, :]).then_inc(row_ready, 1)

        @block.scalar
        def _(act):
            act.wait_ge(stats_done, 1)
            act.activation(rstd[:, :], var[:, :], ACT.Sqrt).then_inc(sqrt_done, 1)

            def copy(q, par, first):
                act.wait_ge(xt_psum, q + 1)
                if not first:
                    act.wait_ge(gate_psum, q - 1)
                act.activation(xt[par][:, :], two_banks(par), ACT.Copy).then_inc(xt_sb, 1)

            for par in range(2):
                copy(par, par, True)
            with act.Fori(1, NQ // 2) as pair:
                for par in range(2):
                    copy(2 * pair + par, par, False)
            act.wait_ge(soft_in, 1)
            act.activation(wtop[:, :, 1], wtop[:, :, 0], ACT.Exp).then_inc(soft_out, 1)

        @block.tensor
        def _(pe):
            def transposes(q, par, first):
                pe.wait_ge(xn_ready, q + 1)
                if not first:
                    pe.wait_ge(xt_sb, q - 1)
                for v in range(QUAD):
                    for c in range(DC):
                        at = (v % 2) * D + c * P
                        mm = pe.transpose(ps[:, 2 * par + v // 2, at:at + P], xn[par][:, v, c * P:(c + 1) * P],
                                          ident[:, :])
                mm.then_inc(xt_psum, 1)

            def gate(q, par):
                pe.wait_ge(xt_sb, q + 1)
                for v in range(QUAD):
                    for c in range(DC):
                        mm = pe.matmul(ps[:, 4, bass.ds((QUAD * q + v) * E, E)],
                                       xt[par][:, (v * DC + c) * P:(v * DC + c + 1) * P], Wg[:, c, :],
                                       start=(c == 0), stop=(c == DC - 1), skip_group_check=True)
                mm.then_inc(gate_psum, 1)

            transposes(0, 0, True)
            transposes(1, 1, True)
            pe.wait_ge(g_in, 48)
            gate(0, 0)
            with pe.Fori(1, NQ // 2) as pair:
                q = 2 * pair
                transposes(q, 0, False)
                gate(q - 1, 1)
                transposes(q + 1, 1, False)
                gate(q, 0)
            gate(NQ - 1, 1)
            pe.wait_ge(both_ready, 1)
            pe.wait_ge(consts, 5)
            flat = both[:, :, :].rearrange("p t e -> p (t e)")
            pe.matmul(ps[:, 5, 0:T * E], below[:, :], flat, start=True, stop=True)
            pe.matmul(ps[:, 6, 0:T * E], ones[:, :], flat, start=True, stop=True).then_inc(prefix, 1)

        @block.vector
        def _(dve):
            own = Tally(dve, dve_own)
            for t in range(T):
                own.add(dve.bn_stats(stats[:, t, :], X[:, t, 0:D]))
            own.settle()
            for t in range(T):
                own.add(dve.bn_aggr(mv[:, t, :], stats[:, t, :]))
            own.settle()
            dve.tensor_scalar(var[:, :], mv[:, :, 1], LN_EPS, None, ALU.add).then_inc(stats_done, 1)
            dve.wait_ge(stats_done, 1)
            newton_rsqrt(dve, own, sqrt_done, 1, var[:, :], rstd[:, :], tmp[:, :])

            def normalise(q, par, first):
                if not first:
                    dve.wait_ge(xt_psum, q - 1)
                    dve.wait_ge(row_ready, q - 1)
                for v in range(QUAD):
                    t = q * QUAD + v
                    ins = dve.tensor_scalar(xn[par][:, v, :], X[:, bass.ds(t, 1), 0:D], mv[:, bass.ds(t, 1), 0],
                                            rstd[:, bass.ds(t, 1)], ALU.subtract, ALU.mult)
                ins.then_inc(xn_ready, 1)

            for par in range(2):
                normalise(par, par, True)
            with dve.Fori(1, NQ // 2) as pair:
                for par in range(2):
                    normalise(2 * pair + par, par, False)

            def over_tiles(a):
                return a.unsqueeze(1).broadcast_to([P, T, E])

            dve.wait_ge(g_in, 48)
            dve.wait_ge(consts, 5)
            dve.wait_ge(gate_psum, NQ)
            own.link(dve.tensor_tensor(logit[:, :, :], ps[:, 4, 0:T * E].rearrange("p (t e) -> p t e", e=E),
                                       over_tiles(bg[:, :]), ALU.add))
            own.link(dve.tensor_tensor(logit[:, :, :], logit[:, :, :], over_tiles(bg2[:, :]), ALU.add))
            for t in range(T):
                own.add(dve.max(best[:, t, :], logit[:, t, :]))
            own.settle()
            for t in range(T):
                own.add(dve.max_index(besti[:, t, :], best[:, t, :], logit[:, t, :]))
            own.settle()
            own.link(dve.tensor_copy(bestf[:, :, :], besti[:, :, 0:TOP]))
            for k in range(TOP):
                own.link(dve.tensor_tensor(pick[k][:, :, :], bestf[:, :, k:k + 1].broadcast_to([P, T, E]),
                                           over_tiles(iota_e[:, :]), ALU.is_equal))
            dve.tensor_tensor(both[:, :, :], pick[0][:, :, :], pick[1][:, :, :], ALU.add).then_inc(both_ready, 1)
            dve.tensor_tensor(wtop[:, :, 0], best[:, :, 1], best[:, :, 0], ALU.subtract).then_inc(soft_in, 1)
            dve.wait_ge(soft_out, 1)
            own.link(dve.tensor_scalar(tmp[:, :], wtop[:, :, 1], 1.0, None, ALU.add))
            own.link(dve.reciprocal(wtop[:, :, 0], tmp[:, :]))
            own.link(dve.tensor_tensor(wtop[:, :, 1], wtop[:, :, 1], wtop[:, :, 0], ALU.mult))
            dve.wait_ge(prefix, 1)
            own.link(dve.tensor_copy(total[:, :, :], ps[:, 6, 0:T * E].rearrange("p (t e) -> p t e", e=E)))
            for e in range(E):
                own.add(dve.tensor_tensor_scan(upto[:, :, e], ones[:, 0:T], total[:, :, e], 0.0, ALU.mult, ALU.add))
            own.settle()
            own.link(dve.tensor_scalar(cnt[:, :], upto[:, T - 1, :], float(P - 1), None, ALU.add))
            own.link(dve.tensor_scalar(cnt[:, :], cnt[:, :], P.bit_length() - 1, None, ALU.logical_shift_right))
            own.link(dve.tensor_copy(ntile[:, :], cnt[:, :]))
            own.link(dve.tensor_tensor_scan(tend[:, :], ones[:, 0:E], ntile[:, :], 0.0, ALU.mult, ALU.add))
            own.link(dve.tensor_tensor(start[:, :], tend[:, :], ntile[:, :], ALU.subtract))
            own.link(dve.tensor_scalar(start[:, :], start[:, :], float(P), None, ALU.mult))
            own.link(dve.tensor_tensor(upto[:, :, :], upto[:, :, :], total[:, :, :], ALU.subtract))
            own.link(dve.tensor_tensor(pos[:, :, :], ps[:, 5, 0:T * E].rearrange("p (t e) -> p t e", e=E),
                                       upto[:, :, :], ALU.add))
            own.link(dve.tensor_tensor(pos[:, :, :], pos[:, :, :], over_tiles(start[:, :]), ALU.add))
            for k in range(TOP):
                own.link(dve.tensor_tensor(pick[k][:, :, :], pick[k][:, :, :], pos[:, :, :], ALU.mult))
                own.link(dve.reduce_sum(posf[:, k, :], pick[k][:, :, :], AX_X))
            own.link(dve.tensor_copy(posu[:, :, :], posf[:, :, :]))
            own.link(dve.tensor_tensor(past[:, :, :], iota_k[:, :].unsqueeze(2).broadcast_to([P, TILES, E]),
                                       tend[:, :].unsqueeze(1).broadcast_to([P, TILES, E]), ALU.is_ge))
            own.link(dve.reduce_sum(eidf[:, :], past[:, :, :], AX_X))
            own.add(dve.memset(eid[:, 0:2], 0))
            own.link(dve.tensor_scalar(eid[:, 2:TILES + 2], eidf[:, :], float(E - 1), None, ALU.min))

    with ExitStack() as ctx:
        def sb(name, shape, dt=F32):
            return ctx.enter_context(nc.sbuf_tensor(L + name, shape, dt))

        W1 = sb("W1", [P, E * DC, 2, H], F32R)
        W2 = sb("W2", [P, E * HC, 2, D], F32R)
        b1 = sb("b1", [P, E, H])
        b2 = sb("b2", [P, E, D])
        STAGE = H
        stage = [sb(f"stage{s}", [P, STAGE]) for s in range(3)]
        xT = [[sb(f"xT{s}{h}", [P, D], F32R) for h in range(2)] for s in range(2)]
        hT = [[sb(f"hT{s}{h}", [P, H], F32R) for h in range(2)] for s in range(2)]
        xs = [X[:, s, :] for s in range(RING)]
        hs = [X[:, RING + 2 * s:RING + 2 + 2 * s, :].rearrange("p a n -> p (a n)")[:, 0:H] for s in range(2)]
        YS = 4
        ys = [X[:, RING + 4 + s, 0:D] for s in range(YS)]

        sent, id_moved = sem("sent"), sem("id_moved")
        stage_in = [sem(f"stage_in{s}") for s in range(3)]
        stage_hi, stage_lo, b_in = sem("stage_hi"), sem("stage_lo"), sem("b_in")
        xs_in = [sem(f"xs_in{s}") for s in range(RING)]
        xT_psum, xT_hi, xT_lo, h_psum, h_sb, hT_psum, hT_hi, hT_lo, y_psum, y_half, y_sb = (
            sem(n) for n in ("xT_psum", "xT_hi", "xT_lo", "h_psum", "h_sb", "hT_psum", "hT_hi", "hT_lo", "y_psum",
                             "y_half", "y_sb"))
        y_out = [sem(f"y_out{s}") for s in range(YS)]
        stores = sem("stores")
        block = ctx.enter_context(nc.Block())
        XB, HB, TB, YB = 0, 2, 4, 6
        n1, n2 = E * DC, E * HC * D // STAGE
        per = STAGE // D
        w1_v = w["W1"].rearrange("e (c p) h -> p (e c) h", p=P)
        w2_v = w["W2"].rearrange("e (c p) h -> p (e c) h", p=P)

        def piece(n, h):
            if n < n1:
                return W1[:, n, h, :]
            m = n - n1
            return W2[:, m * per:(m + 1) * per, h, :]

        def staged(n):
            return stage[n % 3][:, :] if n < n1 else stage[n % 3][:, :].rearrange("p (a n) -> p a n", n=D)

        def experts_of(eng, k):
            return eng_values(nc, eng, eid[0:1, bass.ds(k, RING + 2)], E - 1)

        @block.sync
        def _(sp):
            for n in range(n1 + n2):
                if n >= 3:
                    sp.wait_ge(stage_lo, n - 2)
                if n < n1:
                    sp.dma_start(stage[n % 3][:, :], w1_v[:, n, :]).then_inc(stage_in[n % 3], 16)
                else:
                    m = n - n1
                    sp.dma_start(stage[n % 3][:, :].rearrange("p (a n) -> p a n", n=D),
                                 w2_v[:, m * per:(m + 1) * per, :]).then_inc(stage_in[n % 3], 16)
            sp.dma_start(b1[:, :, :], w["b1"].rearrange("(a e) h -> a e h", a=1).broadcast_to([P, E, H])).then_inc(b_in, 16)
            sp.dma_start(b2[:, :, :], w["b2"].rearrange("(a e) h -> a e h", a=1).broadcast_to([P, E, D])).then_inc(b_in, 16)
            sp.wait_ge(sent, 16 * TOP * T)

            def load(k, v, first):
                if not first:
                    sp.wait_ge(xT_psum, k - RING + 1)
                    sp.wait_ge(y_out[v % YS], (k - v % YS) * (16 // YS) - 16)
                sp.dma_start(xs[v], slots[bass.ds(k * P, P), :]).then_inc(xs_in[v], 16)

            for v in range(RING):
                load(v, v, True)
            with sp.Fori(1, TILES // RING) as turn:
                for v in range(RING):
                    load(RING * turn + v, v, False)

        @block.gpsimd
        def _(pool):
            for k in range(TOP):
                if k:
                    pool.wait_ge(sent, 16 * T * k)
                    pool.tensor_scalar(X[:, :, D].bitcast(U32), X[:, :, D].bitcast(U32), float(N), None,
                                       ALU.add).then_inc(id_moved, 1)
                    pool.wait_ge(id_moved, k)
                for t in range(T):
                    pool.indirect_dma_start(slots, bass.IndirectOffsetOnAxis(ap=posu[:, k, t:t + 1], axis=0),
                                            X[:, t, :], None).then_inc(sent, 16)

            def store(k, v):
                pool.wait_ge(y_sb, k + 1)
                pool.sem_inc(stores, 1)
                pool.indirect_dma_start(rows, bass.IndirectOffsetOnAxis(ap=xs[v][:, D:D + 1].bitcast(U32), axis=0),
                                        ys[v % YS], None, bounds_check=TOP * N - 1,
                                        oob_is_err=False).then_inc(y_out[v % YS], 16)

            with pool.Fori(0, TILES // RING) as turn:
                for v in range(RING):
                    store(RING * turn + v, v)
            for s in range(YS):
                pool.wait_ge(y_out[s], 16 * (TILES // YS))

        @block.scalar
        def _(act):
            for n in range(n1 + n2):
                act.wait_ge(stage_in[n % 3], 16 * (n // 3 + 1))
                act.activation(piece(n, 0), staged(n), ACT.Copy).then_inc(stage_hi, 1)

            def x_hi(k, s, first):
                act.wait_ge(xT_psum, k + 1)
                if not first:
                    act.wait_ge(h_psum, k - 1)
                act.activation(xT[s][0][:, :], ps[:, XB + s, 0:D], ACT.Copy).then_inc(xT_hi, 1)

            def h_hi(k, s, first):
                act.wait_ge(hT_psum, k + 1)
                if not first:
                    act.wait_ge(y_psum, k - 1)
                act.activation(hT[s][0][:, :], ps[:, TB + s, :], ACT.Relu).then_inc(hT_hi, 1)

            x_hi(0, 0, True)
            x_hi(1, 1, True)
            h_hi(0, 0, True)
            x_hi(2, 0, False)
            h_hi(1, 1, True)
            x_hi(3, 1, False)
            with act.Fori(1, TILES // 2 - 1) as pair:
                for s in range(2):
                    k = 2 * pair + s
                    h_hi(k, s, False)
                    x_hi(k + 2, s, False)
            for s in range(2):
                h_hi(TILES - 2 + s, s, False)

        @block.vector
        def _(dve):
            for n in range(n1 + n2):
                dve.wait_ge(stage_hi, n + 1)
                dve.tensor_tensor(piece(n, 1), staged(n), piece(n, 0), ALU.subtract).then_inc(stage_lo, 1)
            dve.wait_ge(b_in, 32)

            def x_lo(k, s, first):
                dve.wait_ge(xT_hi, k + 1)
                dve.tensor_tensor(xT[s][1][:, :], ps[:, XB + s, 0:D], xT[s][0][:, :], ALU.subtract).then_inc(xT_lo, 1)

            def bias_h(k, s, first, e):
                dve.wait_ge(h_psum, k + 1)
                if not first:
                    dve.wait_ge(hT_psum, k - 1)
                dve.tensor_tensor(hs[s], ps[:, HB + s, :], b1[:, bass.ds(e, 1), :].rearrange("p a n -> p (a n)"),
                                  ALU.add).then_inc(h_sb, 1)

            def h_lo(k, s, first):
                dve.wait_ge(hT_hi, k + 1)
                dve.scalar_tensor_tensor(hT[s][1][:, :], ps[:, TB + s, :], 0.0, hT[s][0][:, :], ALU.max,
                                         ALU.subtract).then_inc(hT_lo, 1)

            def bias_y(k, v, first, e):
                s = v % 2
                dve.wait_ge(y_psum, k + 1)
                if not first:
                    dve.wait_ge(y_out[v % YS], (k - v % YS) * (16 // YS))
                dve.tensor_tensor(ys[v % YS], ps[:, YB + s, D:2 * D],
                                  b2[:, bass.ds(e, 1), :].rearrange("p a n -> p (a n)"), ALU.add).then_inc(y_half, 1)
                dve.wait_ge(y_half, k + 1)
                dve.tensor_tensor(ys[v % YS], ys[v % YS], ps[:, YB + s, 0:D], ALU.add).then_inc(y_sb, 1)

            def steps(turn, first=False, last=False):
                e = experts_of(dve, RING * turn)
                for v in range(RING + (2 if last else 0)):
                    k, s = RING * turn + v, v % 2
                    if not last or v < RING - 1:
                        x_lo(k + 1, 1 - s, False)
                    if v < RING:
                        bias_h(k, s, first and v < 2, e[v + 2])
                    if (not first or v >= 1) and v <= RING:
                        h_lo(k - 1, 1 - s, False)
                    if not first or v >= 2:
                        bias_y(k - 2, (v - 2) % RING, first and v - 2 < YS, e[v])

            x_lo(0, 0, True)
            steps(0, first=True)
            with dve.Fori(1, TILES // RING - 1) as turn:
                steps(turn)
            steps(TILES // RING - 1, last=True)

        @block.tensor
        def _(pe):
            def x_turn(k, v, first):
                s = v % 2
                pe.wait_ge(xs_in[v], (k - v) * (16 // RING) + 16)
                if not first:
                    pe.wait_ge(xT_lo, k - 1)
                for c in range(DC):
                    mm = pe.transpose(ps[:, XB + s, c * P:(c + 1) * P], xs[v][:, c * P:(c + 1) * P], ident[:, :])
                mm.then_inc(xT_psum, 1)

            def up(k, s, first, e):
                pe.wait_ge(xT_lo, k + 1)
                if not first:
                    pe.wait_ge(h_sb, k - 1)
                for c in range(DC):
                    for a, b in ((0, 0), (1, 0), (0, 1)):
                        mm = pe.matmul(ps[:, HB + s, :], xT[s][a][:, c * P:(c + 1) * P],
                                       W1[:, bass.ds(e * DC + c, 1), b, :], start=(c == 0 and a == 0 and b == 0),
                                       stop=(c == DC - 1 and b == 1))
                mm.then_inc(h_psum, 1)

            def h_turn(k, s, first):
                pe.wait_ge(h_sb, k + 1)
                if not first:
                    pe.wait_ge(hT_lo, k - 1)
                for c in range(HC):
                    mm = pe.transpose(ps[:, TB + s, c * P:(c + 1) * P], hs[s][:, c * P:(c + 1) * P], ident[:, :])
                mm.then_inc(hT_psum, 1)

            def down(k, s, first, e):
                pe.wait_ge(hT_lo, k + 1)
                if not first:
                    pe.wait_ge(y_sb, k - 1)
                for c in range(HC):
                    pe.matmul(ps[:, YB + s, :], hT[s][0][:, c * P:(c + 1) * P], W2[:, bass.ds(e * HC + c, 1), :, :],
                              start=(c == 0), stop=(c == HC - 1), skip_group_check=True)
                    mm = pe.matmul(ps[:, YB + s, 0:D], hT[s][1][:, c * P:(c + 1) * P],
                                   W2[:, bass.ds(e * HC + c, 1), 0, :], start=False, stop=(c == HC - 1),
                                   skip_group_check=True)
                mm.then_inc(y_psum, 1)

            def steps(turn, first=False, last=False):
                e = experts_of(pe, RING * turn)
                for v in range(RING + (2 if last else 0)):
                    k, s = RING * turn + v, v % 2
                    if not last or v < RING - 1:
                        x_turn(k + 1, (v + 1) % RING, first and v < 1)
                    if v < RING:
                        up(k, s, first and v < 2, e[v + 2])
                    if (not first or v >= 1) and v <= RING:
                        h_turn(k - 1, 1 - s, first and v < 3)
                    if not first or v >= 2:
                        down(k - 2, s, first and v < 4, e[v])

            pe.wait_ge(stage_lo, n1 + n2)
            x_turn(0, 0, True)
            steps(0, first=True)
            with pe.Fori(1, TILES // RING - 1) as turn:
                steps(turn)
            steps(TILES // RING - 1, last=True)

    with ExitStack() as ctx:
        def sb(name, shape, dt=F32):
            return ctx.enter_context(nc.sbuf_tensor(L + name, shape, dt))

        y0 = sb("y0", [P, T, D])
        y1 = sb("y1", [P, T, D])
        got = [sem(f"got{q}") for q in range(NQ)]
        part, added = sem("part"), sem("added")
        block = ctx.enter_context(nc.Block())

        def tiles_of(a, q):
            return a.rearrange("(t p) d -> p t d", p=P)[:, q * QUAD:(q + 1) * QUAD, :]

        @block.sync
        def _(sp):
            for q in range(NQ):
                sp.dma_start(y0[:, q * QUAD:(q + 1) * QUAD, :], tiles_of(rows[0:N, :], q)).then_inc(got[q], 16)
                sp.dma_start(y1[:, q * QUAD:(q + 1) * QUAD, :], tiles_of(rows[N:2 * N, :], q)).then_inc(got[q], 16)
                sp.dma_start(X[:, q * QUAD:(q + 1) * QUAD, 0:D], tiles_of(x1, q)).then_inc(got[q], 16)

        @block.scalar
        def _(act):
            for q in range(NQ):
                act.wait_ge(got[q], 48)
                for t in range(q * QUAD, (q + 1) * QUAD):
                    act.activation(y0[:, t, :], y0[:, t, :], ACT.Copy, scale=wtop[:, t, 0:1]).then_inc(part, 1)

        @block.vector
        def _(dve):
            for q in range(NQ):
                for t in range(q * QUAD, (q + 1) * QUAD):
                    dve.wait_ge(part, t + 1)
                    dve.scalar_tensor_tensor(y1[:, t, :], y1[:, t, :], wtop[:, t, 1:2], y0[:, t, :], ALU.mult,
                                             ALU.add).then_inc(added, 1)
                s = slice(q * QUAD, (q + 1) * QUAD)
                dve.wait_ge(added, (q + 1) * QUAD)
                dve.tensor_tensor(X[:, s, 0:D], X[:, s, 0:D], y1[:, s, :], ALU.add)


def build(nc, a, out):
    N, D = a["x"].shape
    T = N // P
    with ExitStack() as top:
        X = top.enter_context(nc.sbuf_tensor("X", [P, T, D + 4], F32))
        x_sb = X[:, :, 0:D]
        dinv = top.enter_context(nc.sbuf_tensor("dinv", [P, T], F32))
        ident = top.enter_context(nc.sbuf_tensor("ident", [P, P], F32))
        ps = top.enter_context(nc.psum_tensor("ps", [P, 8, 512], F32))
        made = top.enter_context(nc.semaphore("ident_made"))
        with nc.Block() as block:
            @block.gpsimd
            def _(pool):
                pool.memset(ident[:, :], 0.0).then_inc(made, 1)
                pool.wait_ge(made, 1)
                pool.affine_select(out=ident[:, :], in_=ident[:, :], compare_op=ALU.not_equal, fill=1.0,
                                   base=0, pattern=[[-1, P]], channel_multiplier=1)
        for layer in range(2):
            with ExitStack() as ctx:
                old_sems = gnn(nc, ctx, layer, a["x"], a["adj"], a["adjT"],
                    a["L0_gnn_W"] if layer == 0 else a["L1_gnn_WT"],
                    None if layer == 0 else a["L1_gnn_b"], x_sb, dinv, ident, ps)
            if layer == 0:
                w = {"Wg": a["L0_ffn_Wg"], "bg": a["L0_ffn_bg"], "bias": a["L0_ffn_bias"]}
            else:
                w = {"Wg": a["L1_ffn_Wr"], "bg": a["L1_ffn_br"], "gamma": a["L1_ffn_gamma"], "beta": a["L1_ffn_beta"]}
            w |= {n: a[f"L{layer}_ffn_{n}"] for n in ("W1", "b1", "W2", "b2")}
            with ExitStack() as ctx:
                if layer == 0:
                    moe0(nc, ctx, w, X, ident, ps, old_sems)
                else:
                    ffn(nc, ctx, layer, w, x_sb, ident, ps, out)


def kernel(**inputs):
    import numpy as np
    import concourse.bacc as bacc
    from concourse.bass_utils import run_bass_kernel_spmd

    data = {n: np.asarray(v) for n, v in inputs.items()}
    data["adjT"] = data["adj"].T
    data["L1_gnn_WT"] = data.pop("L1_gnn_W").T
    E, H = data["L1_ffn_b1"].shape
    data["L1_ffn_b1"] = data["L1_ffn_b1"].reshape(E, H // P, P).transpose(0, 2, 1)
    nc = bacc.Bacc("TRN2", target_bir_lowering=False, num_devices=1)
    arrays = {f"in_{n}": np.ascontiguousarray(data[n]) for n in NAMES}
    aps = {n: nc.dram_tensor(f"in_{n}", arrays[f"in_{n}"].shape, mybir.dt.from_np(arrays[f"in_{n}"].dtype),
                             kind="ExternalInput").ap() for n in NAMES}
    out = nc.dram_tensor("out", data["x"].shape, F32, kind="ExternalOutput").ap()
    build(nc, aps, out)
    return run_bass_kernel_spmd(nc, [arrays], core_ids=[0]).results[0]["out"]
```

```python
from contextlib import ExitStack

import concourse.bass as bass
from concourse import mybir

P = 128
F32 = mybir.dt.float32
F32R = mybir.dt.float32r
U32 = mybir.dt.uint32
I32 = mybir.dt.int32
ALU = mybir.AluOpType
ACT = mybir.ActivationFunctionType
AX_X = mybir.AxisListType.X
LN_EPS = 1e-5
NORM_EPS = 1e-12
CAPACITY_FACTOR = 1.25
TOP = 2

NAMES = ["x", "adj", "adjT", "L0_gnn_W", "L0_ffn_Wg", "L0_ffn_bg", "L0_ffn_bias", "L0_ffn_W1", "L0_ffn_b1",
         "L0_ffn_W2", "L0_ffn_b2", "L1_gnn_WT", "L1_gnn_b", "L1_ffn_Wr", "L1_ffn_br", "L1_ffn_W1", "L1_ffn_b1",
         "L1_ffn_W2", "L1_ffn_b2", "L1_ffn_gamma", "L1_ffn_beta"]


class Tally:

    def __init__(self, eng, sem):
        self.eng, self.sem, self.n = eng, sem, 0

    def add(self, ins):
        ins.then_inc(self.sem, 1)
        self.n = self.n + 1
        return ins

    def settle(self):
        self.eng.wait_ge(self.sem, self.n)

    def link(self, ins):
        self.add(ins)
        self.settle()


def row_over_partitions(ap, parts=P):
    return ap.rearrange("(a n) -> a n", a=1).broadcast_to([parts, ap.shape[0]])


def newton_rsqrt(dve, own, act_sqrt_done, count, a, r, t):
    dve.wait_ge(act_sqrt_done, count)
    own.link(dve.reciprocal(r, r))
    own.link(dve.tensor_tensor(t, r, r, ALU.mult))
    own.link(dve.tensor_tensor(t, t, a, ALU.mult))
    own.link(dve.tensor_scalar(t, t, -0.5, 1.5, ALU.mult, ALU.add))
    own.link(dve.tensor_tensor(r, r, t, ALU.mult))


def eng_values(nc, eng, ap, top):
    _, values = nc.values_load_multi_w_load_instructions(
        ap, engines=[eng.engine], min_val=0, max_val=top,
        skip_runtime_bounds_check_because="computed on chip as min(count of experts, top), never below 0")
    return values


def clear(pool, sems):
    for s in sems:
        pool.sem_clear(s)


def gnn(nc, ctx, layer, x_dram, adj, adjT, W, b, x_sb, dinv, mv, ident, ps, x1, x_kept, rows, wtop):
    N, D = x_dram.shape
    T = N // P
    DC = D // P
    HALF = N // 2
    IT = HALF // P
    GS = 4
    NBLK = 2 * T // GS
    BANKS = 8
    HALF_BANKS = BANKS // 2
    PER_BANK = IT // BANKS
    PIECE = HALF // 2
    SLOTS = 4
    GT = 2 * GS
    QUAD = 4
    NQ = T // QUAD
    PARTS = 8
    X_PARTS = 4
    NAT_LEAD = 22
    NAT_PER = 3
    NAT_BLKS = (2 * T - NAT_LEAD) // NAT_PER
    L = f"g{layer}_"

    def sb(name, shape, dt=F32):
        return ctx.enter_context(nc.sbuf_tensor(L + name, shape, dt))

    sems = []

    def sem(name):
        sems.append(ctx.enter_context(nc.semaphore(L + name)))
        return sems[-1]

    U = sb("U", [P, T, D])
    G = sb("G", [P, GT, 2, D], F32R)
    ACC = sb("ACC", [P, T, D])
    raw = [sb(f"raw{s}", [P, HALF]) for s in range(SLOTS)]
    ahi = [sb(f"ahi{s}", [P, PIECE], F32R) for s in range(SLOTS)]
    alo = [sb(f"alo{s}", [P, PIECE], F32R) for s in range(SLOTS)]
    nat = [sb(f"nat{s}", [P, HALF]) for s in range(2)] if layer == 0 else None
    degp = sb("degp", [P, T, 2])
    deg = sb("deg", [P, T])
    tmp = sb("tmp", [P, T])
    stats = sb("stats", [P, T, 6])
    var = sb("var", [P, T])
    rstd = sb("rstd", [P, T])
    xn = [ACC[:, QUAD * (s + 1):QUAD * (s + 2), :] for s in range(2)]
    sq = [sb(f"sq{s}", [P, D]) for s in range(2)] if layer == 0 else None
    Wp = sb("Wp", [P, DC, 2, D], F32R)
    bias = sb("bias", [P, D]) if layer == 1 else None
    Wraw = ACC[:, 0:DC, :]

    x_in = [sem(f"x_in{n}") for n in range(X_PARTS)] if layer == 0 else None
    w_in = sem("w_in")
    raw_full = [sem(f"raw_full{s}") for s in range(SLOTS)]
    nat_full = [sem(f"nat_full{s}") for s in range(2)]
    nat_sum = sem("nat_sum")
    dve_own = sem("dve_own")
    stats_done, sqrt_done, dve_small = sem("stats_done"), sem("sqrt_done"), sem("dve_small")
    w_split = sem("w_split")
    xn_ready, xt_psum, xt_hi, xt_lo, u_psum, u_ready = (
        sem(n) for n in ("xn_ready", "xt_psum", "xt_hi", "xt_lo", "u_psum", "u_ready"))
    acc_init = sem("acc_init")
    hi_ready, lo_ready, step_done = sem("hi_ready"), sem("lo_ready"), sem("step_done")
    g_hi, g_lo = sem("g_hi"), sem("g_lo")
    deg_ready, deg_sqrt, dinv_ready = sem("deg_ready"), sem("deg_sqrt"), sem("dinv_ready")
    bank_done, bank_free = sem("bank_done"), sem("bank_free")
    x_done = sem("x_done")
    scaled, weighed, x_sum = (sem(n) for n in ("scaled", "weighed", "x_sum"))
    u_raw = sem("u_raw")
    sum_ready, relu_ready, square_ready, norm_sqrt, norm_ready = (
        sem(n) for n in ("sum_ready", "relu_ready", "square_ready", "norm_sqrt", "norm_ready"))
    block = ctx.enter_context(nc.Block())

    def two_banks(n):
        return ps[:, 2 * n:2 * n + 2, :].rearrange("p b n -> p (b n)")

    def pieces_from(t, h, count):
        return [(t + (h + i) // 2, (h + i) % 2) for i in range(count)]

    def pieces_of(pair, par):
        return pieces_from(NAT_LEAD // 2 + NAT_PER * pair + NAT_PER * par // 2, NAT_PER * par % 2, NAT_PER)

    RAW_BASE = 0 if layer == 0 else 3 * 16 * NQ // SLOTS

    def y_of(q):
        return [raw[q % SLOTS][:, k * QUAD * D:(k + 1) * QUAD * D].rearrange("p (t d) -> p t d", d=D)
                for k in range(TOP)]

    def nat_of(t, h):
        return adj[bass.ds(t * P, P), h * HALF:(h + 1) * HALF]

    @block.sync
    def _(sp):
        if layer == 0:
            for n in range(X_PARTS):
                s = slice(n * T // X_PARTS, (n + 1) * T // X_PARTS)
                sp.dma_start(x_sb[:, s, :], x_dram.rearrange("(t p) d -> p t d", p=P)[:, s, :]).then_inc(x_in[n], 16)
        sp.dma_start(Wraw, W.rearrange("(c p) n -> p c n", p=P)).then_inc(w_in, 16)
        if layer == 1:
            sp.dma_start(bias[:, :], row_over_partitions(b)).then_inc(w_in, 16)
            for q in range(NQ):
                if q >= SLOTS:
                    sp.wait_ge(weighed, q - SLOTS + 1)
                s = slice(q * QUAD, (q + 1) * QUAD)
                for y, src in zip(y_of(q), (rows[0:N, :], rows[N:2 * N, :])):
                    sp.dma_start(y, src.rearrange("(t p) d -> p t d", p=P)[:, s, :]).then_inc(raw_full[q % SLOTS], 16)
                sp.dma_start(x_sb[:, s, :],
                             x1.rearrange("(t p) d -> p t d", p=P)[:, s, :]).then_inc(raw_full[q % SLOTS], 16)
            sp.wait_ge(weighed, NQ)

        def load_nat(t, h, first=False):
            if not first:
                sp.wait_ge(nat_sum, 2 * t + h - 1)
            sp.dma_start(nat[h][:, :], nat_of(t, h)).then_inc(nat_full[h], 16)

        def load_raw(jt, half, s, n=None):
            if n is not None:
                sp.wait_ge(lo_ready, 2 * n - 2 * SLOTS + 2)
            sp.dma_start(raw[s][:, :], adjT[bass.ds(jt * P, P), bass.ds(half * HALF, HALF)]).then_inc(raw_full[s], 16)

        def blk(bb, pieces=(), first=False):
            for j in range(GS):
                jt = (bb // 2) * GS + j
                load_raw(jt, bb % 2, j, None if first else GS * bb + j)
                for t, h in pieces[j:j + 1]:
                    load_nat(t, h)

        if layer == 0:
            for t, h in pieces_from(0, 0, NAT_LEAD):
                load_nat(t, h, first=(t == 0))
            blk(0, pieces_of(0, 0), first=True)
            blk(1, pieces_of(0, 1))
            with sp.Fori(1, NAT_BLKS // 2) as pair:
                for par in range(2):
                    blk(2 * pair + par, pieces_of(pair, par))
        else:
            blk(0, first=True)
        with sp.Fori(NAT_BLKS if layer == 0 else 1, NBLK) as bb:
            blk(bb)
        if layer == 0:
            for n in range(PARTS):
                if n < PARTS // 2:
                    sp.wait_ge(x_sum, n + 1)
                else:
                    sp.wait_ge(x_done, n - PARTS // 2 + 1)
                s = slice(n * T // PARTS, (n + 1) * T // PARTS)
                sp.dma_start(x1.rearrange("(t p) d -> p t d", p=P)[:, s, :],
                             x_sb[:, s, :]).then_inc(x_kept[2 * n // PARTS], 16)

    @block.gpsimd
    def _(pool):
        if layer == 1:
            for i in range(NQ + 5):
                if i < NQ:
                    s = slice(i * QUAD, (i + 1) * QUAD)
                    pool.wait_ge(scaled, TOP * QUAD * i + QUAD)
                    pool.tensor_tensor(x_sb[:, s, :], x_sb[:, s, :], y_of(i)[1], ALU.add).then_inc(x_sum, 1)
                q = i - 5
                if q >= 0:
                    s = slice(q * QUAD, (q + 1) * QUAD)
                    pool.wait_ge(u_raw, q + 1)
                    pool.tensor_tensor(U[:, s, :], U[:, s, :], bias[:, :].unsqueeze(1).broadcast_to([P, QUAD, D]),
                                       ALU.add).then_inc(u_ready, 1)
        pool.wait_ge(w_split, 2)
        pool.wait_ge(xt_psum, NQ)
        if layer == 0:
            pool.memset(ACC[:, :, :], 0.0).then_inc(acc_init, T)
            for n in range(PARTS // 2):
                s = slice(n * T // PARTS, (n + 1) * T // PARTS)
                pool.wait_ge(scaled, (n + 1) * T // PARTS)
                pool.tensor_tensor(x_sb[:, s, :], x_sb[:, s, :], ACC[:, s, :], ALU.add).then_inc(x_sum, 1)
        else:
            pool.wait_ge(u_ready, NQ)
            for t in range(T):
                pool.tensor_scalar(ACC[:, t, :], U[:, t, :], dinv[:, t:t + 1], None, ALU.mult).then_inc(acc_init, 1)

    @block.scalar
    def _(act):
        def sum_nat(t, h):
            act.wait_ge(nat_full[h], t * 16 + 16)
            act.activation(nat[h][:, :], nat[h][:, :], ACT.Copy,
                           accum_out=degp[:, bass.ds(t, 1), h]).then_inc(nat_sum, 1)

        act.wait_ge(w_in, 16 * (1 + layer))
        act.activation(Wp[:, :, 0, :], Wraw, ACT.Copy).then_inc(w_split, 1)
        if layer == 0:
            for t, h in pieces_from(0, 0, 4):
                sum_nat(t, h)
        if layer == 0:
            act.wait_ge(stats_done, 1)
            act.activation(rstd[:, :], var[:, :], ACT.Sqrt).then_inc(sqrt_done, 1)
            for t, h in pieces_from(2, 0, 2):
                sum_nat(t, h)

        def prep(q, par, first):
            act.wait_ge(xt_psum, q + 1)
            if not first:
                act.wait_ge(u_psum, q - 1)
            act.activation(ahi[par][:, :], two_banks(par), ACT.Copy).then_inc(xt_hi, 1)

        def u_copy(q, par):
            act.wait_ge(u_psum, q + 1)
            act.activation(U[:, bass.ds(q * QUAD, QUAD), :], two_banks(2 + par).rearrange("p (t n) -> p t n", n=D),
                           ACT.Copy).then_inc(u_ready if layer == 0 else u_raw, 1)

        def scale_y(q):
            act.wait_ge(raw_full[q % SLOTS], 48 * (q // SLOTS + 1))
            for k in (1, 0):
                for v in range(QUAD):
                    t = q * QUAD + v
                    y = y_of(q)[k][:, v, :]
                    act.activation(y, y, ACT.Copy, scale=wtop[:, t, k:k + 1]).then_inc(scaled, 1)

        def root(q):
            act.wait_ge(stats_done, q + 1)
            s = slice(q * QUAD, (q + 1) * QUAD)
            act.activation(rstd[:, s], var[:, s], ACT.Sqrt).then_inc(sqrt_done, 1)

        if layer == 0:
            prep(0, 0, True)
            for h in range(2):
                sum_nat(3, h)
            prep(1, 1, True)
            u_copy(0, 0)
            for h in range(2):
                sum_nat(4, h)
            with act.Fori(1, NQ // 2) as pair:
                for par in range(2):
                    q = 2 * pair + par
                    prep(q, par, False)
                    u_copy(q - 1, 1 - par)
                    for h in range(2):
                        sum_nat(NAT_LEAD // 2 - NQ + q, h)
            u_copy(NQ - 1, 1)
        else:
            for i in range(NQ + 4):
                if i < NQ:
                    scale_y(i)
                if 0 <= i - 1 < NQ:
                    root(i - 1)
                if 0 <= i - 3 < NQ:
                    prep(i - 3, (i - 3) % 2, i - 3 < 2)
                if 0 <= i - 4:
                    u_copy(i - 4, i % 2)

        def g_tile(t):
            act.activation(G[:, bass.ds(t % GT, 1), 0, :], U[:, bass.ds(t, 1), :], ACT.Copy,
                           scale=dinv[:, bass.ds(t, 1)]).then_inc(g_hi, 1)

        def deg_sqrt_of(t):
            act.wait_ge(deg_ready, t // 2 + 1)
            act.activation(dinv[:, bass.ds(t, 2)], deg[:, bass.ds(t, 2)], ACT.Sqrt).then_inc(deg_sqrt, 1)

        act.wait_ge(u_ready, NQ)
        if layer == 0:
            deg_sqrt_of(0)
            deg_sqrt_of(2)
            act.wait_ge(dinv_ready, 2)
        for t in range(GS):
            g_tile(t)

        def features_of(n):
            tiles = range(n * T // PARTS, (n + 1) * T // PARTS)
            for t in [*tiles, None]:
                if t is not None:
                    act.wait_ge(sum_ready, t + 1)
                    act.activation(ACC[:, t, :], ACC[:, t, :], ACT.Relu, scale=dinv[:, t:t + 1]).then_inc(relu_ready, 1)
                if t != tiles[0]:
                    v = tiles[-1] if t is None else t - 1
                    act.wait_ge(relu_ready, v + 1)
                    act.activation(sq[v % 2][:, :], ACC[:, v, :], ACT.Square,
                                   accum_out=deg[:, v:v + 1]).then_inc(square_ready, 1)
            s = slice(tiles[0], tiles[-1] + 1)
            act.wait_ge(square_ready, tiles[-1] + 1)
            act.activation(tmp[:, s], deg[:, s], ACT.Sqrt).then_inc(norm_sqrt, 1)

        def blk(bb, pieces=(), with_g=True, after=None):
            for j in range(GS):
                act.wait_ge(raw_full[j], bb * 16 + 16 + RAW_BASE)
                for q in range(2):
                    act.wait_ge(step_done, 2 * GS * bb + 2 * j + q + 1)
                    act.activation(ahi[(2 * j + q) % SLOTS][:, :], raw[j][:, q * PIECE:(q + 1) * PIECE],
                                   ACT.Copy).then_inc(hi_ready, 1)
                    if after is not None and 2 * j + q >= 4:
                        after(2 * j + q - 4)
                    if with_g and layer == 0 and (j, q) == (GS - 1, 0):
                        deg_sqrt_of(2 * bb + GS)
                if with_g and j == GS - 1:
                    if layer == 0:
                        act.wait_ge(dinv_ready, bb + GS // 2 + 1)
                    for v in range(2):
                        g_tile(2 * bb + GS + v)
                for t, h in pieces[j:j + 1]:
                    sum_nat(t, h)

        if layer == 0:
            blk(0, pieces_of(0, 0))
            blk(1, pieces_of(0, 1))
            with act.Fori(1, NAT_BLKS // 2) as pair:
                for par in range(2):
                    blk(2 * pair + par, pieces_of(pair, par))
        else:
            with act.Fori(0, NBLK - 2) as bb:
                blk(bb)
        blk(NBLK - 2, with_g=False)
        blk(NBLK - 1, with_g=False, after=features_of if layer == 0 else None)
        if layer == 0:
            for n in range(PARTS // 2):
                act.wait_ge(norm_ready, n + 1)
                for t in range(n * T // PARTS, (n + 1) * T // PARTS):
                    act.activation(ACC[:, t, :], ACC[:, t, :], ACT.Copy, scale=tmp[:, t:t + 1]).then_inc(scaled, 1)
                features_of(PARTS // 2 + n)

    @block.vector
    def _(dve):
        own = Tally(dve, dve_own)
        if layer == 0:
            for t in range(T):
                if t % (T // X_PARTS) == 0:
                    dve.wait_ge(x_in[t // (T // X_PARTS)], 16)
                own.add(dve.bn_stats(stats[:, t, :], x_sb[:, t, :]))
            own.settle()
            for t in range(T):
                own.add(dve.bn_aggr(mv[:, t, :], stats[:, t, :]))
            own.settle()
            dve.tensor_scalar(var[:, :], mv[:, :, 1], LN_EPS, None, ALU.add).then_inc(stats_done, 1)
        dve.wait_ge(w_split, 1)
        dve.tensor_tensor(Wp[:, :, 1, :], Wraw, Wp[:, :, 0, :], ALU.subtract).then_inc(w_split, 1)
        if layer == 0:
            dve.wait_ge(stats_done, 1)
            newton_rsqrt(dve, own, sqrt_done, 1, var[:, :], rstd[:, :], tmp[:, :])

        def statistics(q):
            tiles = range(q * QUAD, (q + 1) * QUAD)
            s = slice(tiles[0], tiles[-1] + 1)
            dve.wait_ge(scaled, TOP * QUAD * (q + 1))
            dve.wait_ge(x_sum, q + 1)
            dve.tensor_tensor(x_sb[:, s, :], x_sb[:, s, :], y_of(q)[0], ALU.add).then_inc(weighed, 1)
            dve.wait_ge(weighed, q + 1)
            for t in tiles:
                own.add(dve.bn_stats(stats[:, t, :], x_sb[:, t, :]))
            own.settle()
            for t in tiles:
                own.add(dve.bn_aggr(mv[:, t, :], stats[:, t, :]))
            own.settle()
            s = slice(tiles[0], tiles[-1] + 1)
            dve.tensor_scalar(var[:, s], mv[:, s, 1], LN_EPS, None, ALU.add).then_inc(stats_done, 1)

        def normalise(q, par, first):
            if not first:
                dve.wait_ge(xt_psum, q - 1)
            for v in range(QUAD):
                t = q * QUAD + v
                ins = dve.tensor_scalar(xn[par][:, v, :], x_sb[:, bass.ds(t, 1), :], mv[:, bass.ds(t, 1), 0],
                                        rstd[:, bass.ds(t, 1)], ALU.subtract, ALU.mult)
            ins.then_inc(xn_ready, 1)

        def split(q, par):
            dve.wait_ge(xt_hi, q + 1)
            dve.tensor_tensor(alo[par][:, :], two_banks(par), ahi[par][:, :], ALU.subtract).then_inc(xt_lo, 1)

        if layer == 0:
            normalise(0, 0, True)
            normalise(1, 1, True)
            split(0, 0)
            normalise(2, 0, False)
            split(1, 1)
            normalise(3, 1, False)
            with dve.Fori(1, NQ // 2 - 1) as pair:
                for par in range(2):
                    q = 2 * pair + par
                    split(q, par)
                    normalise(q + 2, par, False)
            for q in (NQ - 2, NQ - 1):
                split(q, q % 2)
        else:
            dve.wait_ge(w_in, 32)
            for i in range(NQ + 3):
                if 0 <= i - 1 < NQ:
                    statistics(i - 1)
                if 0 <= i - 2 < NQ:
                    q = i - 2
                    s = slice(q * QUAD, (q + 1) * QUAD)
                    newton_rsqrt(dve, own, sqrt_done, q + 1, var[:, s], rstd[:, s], tmp[:, s])
                    normalise(q, q % 2, q < 2)
                if 0 <= i - 3:
                    split(i - 3, (i - 3) % 2)

        small = Tally(dve, dve_small)

        def degrees(t, n):
            d2 = deg[:, bass.ds(t, 2)]
            dve.wait_ge(nat_sum, 2 * t + 4)
            dve.tensor_tensor(d2, degp[:, bass.ds(t, 2), 0], degp[:, bass.ds(t, 2), 1], ALU.add).then_inc(dve_small, 1)
            dve.wait_ge(dve_small, n + 1)
            dve.tensor_scalar(d2, d2, 1.0, None, ALU.add).then_inc(deg_ready, 1)

        def inverse_root(t, n):
            d2, r2, t2 = deg[:, bass.ds(t, 2)], dinv[:, bass.ds(t, 2)], tmp[:, bass.ds(t, 2)]
            dve.wait_ge(deg_sqrt, t // 2 + 1)
            dve.reciprocal(r2, r2).then_inc(dve_small, 1)
            dve.wait_ge(dve_small, n + 2)
            dve.tensor_tensor(t2, r2, r2, ALU.mult).then_inc(dve_small, 1)
            dve.wait_ge(dve_small, n + 3)
            dve.tensor_tensor(t2, t2, d2, ALU.mult).then_inc(dve_small, 1)
            dve.wait_ge(dve_small, n + 4)
            dve.tensor_scalar(t2, t2, -0.5, 1.5, ALU.mult, ALU.add).then_inc(dve_small, 1)
            dve.wait_ge(dve_small, n + 5)
            dve.tensor_tensor(r2, r2, t2, ALU.mult).then_inc(dinv_ready, 1)

        PER_DEG = 5

        def g_tile(t):
            dve.wait_ge(g_hi, t + 1)
            dve.scalar_tensor_tensor(G[:, bass.ds(t % GT, 1), 1, :], U[:, bass.ds(t, 1), :], dinv[:, bass.ds(t, 1)],
                                     G[:, bass.ds(t % GT, 1), 0, :], ALU.mult, ALU.subtract).then_inc(g_lo, 1)

        dve.wait_ge(u_ready, NQ)
        if layer == 0:
            for t in (0, 2):
                degrees(t, PER_DEG * (t // 2))
                inverse_root(t, PER_DEG * (t // 2))
            dve.wait_ge(dinv_ready, 2)
        for t in range(GS):
            g_tile(t)

        def lo(bb, j, q):
            dve.wait_ge(hi_ready, 2 * GS * bb + 2 * j + q + 1)
            dve.tensor_tensor(alo[(2 * j + q) % SLOTS][:, :], raw[j][:, q * PIECE:(q + 1) * PIECE],
                              ahi[(2 * j + q) % SLOTS][:, :], ALU.subtract).then_inc(lo_ready, 1)

        def evacuate(bb, banks):
            for k in banks:
                if k % HALF_BANKS == HALF_BANKS - 1:
                    dve.wait_ge(step_done, SLOTS + 2 * GS * (bb + 1) - 1 + k // HALF_BANKS)
                else:
                    dve.wait_ge(bank_done, (BANKS - 2) * bb + k - k // HALF_BANKS + 1)
                half = ACC[:, bass.ds((bb % 2) * IT + PER_BANK * k, PER_BANK), :]
                dve.tensor_tensor(half, ps[:, k, :].rearrange("p (t n) -> p t n", n=D), half,
                                  ALU.add).then_inc(bank_free, 1)

        def total(n):
            for t in range(n * T // PARTS, (n + 1) * T // PARTS):
                dve.scalar_tensor_tensor(ACC[:, t, :], U[:, t, :], dinv[:, t:t + 1], ACC[:, t, :], ALU.mult,
                                         ALU.add).then_inc(sum_ready, 1)

        def norm(n):
            s = slice(n * T // PARTS, (n + 1) * T // PARTS)
            dve.wait_ge(norm_sqrt, n + 1)
            own.link(dve.tensor_scalar(tmp[:, s], tmp[:, s], NORM_EPS, None, ALU.max))
            own.link(dve.reciprocal(tmp[:, s], tmp[:, s]))
            dve.sem_inc(norm_ready, 1)

        def finish(n):
            tiles = range(n * T // PARTS, (n + 1) * T // PARTS)
            if layer == 0 and n < PARTS // 2:
                dve.wait_ge(x_sum, n + 1)
            else:
                factor = dinv if layer == 1 else tmp
                for t in tiles:
                    own.add(dve.scalar_tensor_tensor(x_sb[:, t, :], ACC[:, t, :], factor[:, t:t + 1], x_sb[:, t, :],
                                                     ALU.mult, ALU.add))
                own.settle()
                if layer == 0:
                    dve.sem_inc(x_done, 1)
            for t in tiles:
                own.add(dve.bn_stats(stats[:, t, :], x_sb[:, t, :]))
            own.settle()
            for t in tiles:
                own.add(dve.bn_aggr(mv[:, t, :], stats[:, t, :]))

        def blk(bb, first=False, with_g=True, last=False):
            for q in range(2):
                lo(bb, 0, q)
            if not first:
                evacuate(bb - 1, range(0, BANKS // 2))
            lo(bb, 1, 0)
            if not first:
                evacuate(bb - 1, range(BANKS // 2, BANKS))
            lo(bb, 1, 1)
            if last:
                dve.wait_ge(bank_free, BANKS * NBLK)
            for j in range(2, GS):
                for q in range(2):
                    n = 2 * j + q - 4
                    if last and layer == 0:
                        total(n)
                    lo(bb, j, q)
                    if last and layer == 0 and n >= 1:
                        norm(n - 1)
                    if last and layer == 1:
                        finish(n)
                    if with_g and layer == 0:
                        t = 2 * bb + GS
                        small = PER_DEG * (bb + GS // 2)
                        if (j, q) == (GS - 2, 1):
                            degrees(t, small)
                        if (j, q) == (GS - 1, 0):
                            inverse_root(t, small)
            if with_g:
                for v in range(2):
                    g_tile(2 * bb + GS + v)

        blk(0, first=True)
        dve.wait_ge(acc_init, T // 2)
        blk(1)
        dve.wait_ge(acc_init, T)
        with dve.Fori(2, NBLK - 2) as bb:
            blk(bb)
        blk(NBLK - 2, with_g=False)
        blk(NBLK - 1, with_g=False, last=True)
        for h in range(2):
            evacuate(NBLK - 1, range(h * BANKS // 2, (h + 1) * BANKS // 2))
            dve.wait_ge(bank_free, BANKS * NBLK + (h + 1) * BANKS // 2)
            parts = range(PARTS // 2 + h * PARTS // 4, PARTS // 2 + (h + 1) * PARTS // 4)
            for n in parts:
                if layer == 0:
                    total(n)
                else:
                    finish(n)
            if layer == 0 and h == 0:
                norm(PARTS // 2 - 1)
        if layer == 0:
            for n in range(PARTS // 2, PARTS):
                norm(n)
                finish(n)
            for n in range(PARTS // 2):
                finish(n)

    @block.tensor
    def _(pe):
        def transposes(q, par, first):
            pe.wait_ge(xn_ready, q + 1)
            if not first:
                pe.wait_ge(xt_lo, q - 1)
            for v in range(QUAD):
                for c in range(DC):
                    at = (v % 2) * D + c * P
                    mm = pe.transpose(ps[:, 2 * par + v // 2, at:at + P], xn[par][:, v, c * P:(c + 1) * P], ident[:, :])
            mm.then_inc(xt_psum, 1)

        def product(q, par, first):
            pe.wait_ge(xt_lo, q + 1)
            if not first:
                pe.wait_ge(u_ready, q - 1)
            for v in range(QUAD):
                n = 0
                for c in range(DC):
                    for a, w in ((ahi, 0), (ahi, 1), (alo, 0)):
                        mm = pe.matmul(ps[:, 4 + 2 * par + v // 2, (v % 2) * D:(v % 2 + 1) * D],
                                       a[par][:, (v * DC + c) * P:(v * DC + c + 1) * P], Wp[:, c, w, :],
                                       start=(n == 0), stop=(n == 3 * DC - 1))
                        n += 1
            mm.then_inc(u_psum, 1)

        pe.wait_ge(w_split, 2)
        transposes(0, 0, True)
        transposes(1, 1, True)
        product(0, 0, True)
        transposes(2, 0, False)
        product(1, 1, True)
        transposes(3, 1, False)
        with pe.Fori(1, NQ // 2 - 1) as pair:
            for par in range(2):
                q = 2 * pair + par
                product(q, par, False)
                transposes(q + 2, par, False)
        product(NQ - 2, 0, False)
        product(NQ - 1, 1, False)
        pe.wait_ge(u_ready, NQ)
        pe.wait_ge(g_lo, GS)
        pe.sem_inc(step_done, SLOTS)
        pe.sem_inc(bank_free, BANKS)

        with pe.Fori(0, NBLK) as bb:
            g0 = ((bb // 2) % 2) * GS
            for j in range(GS):
                pe.wait_ge(g_lo, (bb // 2) * GS + j + 1)
                ghi, glo = (G[:, bass.ds(g0 + j, 1), w, :] for w in range(2))
                for q in range(2):
                    s = (2 * j + q) % SLOTS
                    out = [ps[:, (q * BANKS // 2) + i // PER_BANK, (i % PER_BANK) * D:(i % PER_BANK + 1) * D]
                           for i in range(IT // 2)]
                    a = [slice(i * P, (i + 1) * P) for i in range(IT // 2)]
                    pe.wait_ge(hi_ready, 2 * GS * bb + 2 * j + q + 1)
                    for i in range(IT // 2):
                        lead = j == 0 and i % PER_BANK == 0
                        if lead:
                            pe.wait_ge(bank_free, BANKS * bb + (q * BANKS // 2) + i // PER_BANK + 1)
                        pe.matmul(out[i], ahi[s][:, a[i]], ghi, start=lead, stop=False, skip_group_check=True)
                        pe.matmul(out[i], ahi[s][:, a[i]], glo, start=False, stop=False, skip_group_check=True)
                    pe.wait_ge(lo_ready, 2 * GS * bb + 2 * j + q + 1)
                    for i in range(IT // 2):
                        mm = pe.matmul(out[i], alo[s][:, a[i]], ghi, start=False, stop=(j == GS - 1),
                                       skip_group_check=True)
                        if j == GS - 1 and i % PER_BANK == PER_BANK - 1 and i < IT // 2 - 1:
                            mm.then_inc(bank_done, 1)
                    mm.then_inc(step_done, 1)
    return sems


def ffn1(nc, ctx, w, x_sb, mv, ident, ps, out_dram):
    E, D, H = w["W1"].shape
    N = x_sb.shape[1] * P
    T = N // P
    DC, HC = D // P, H // P
    QUAD = 4
    BLK = QUAD * P
    NT = N // BLK
    CHUNKS = TOP * HC
    L = "f1_"

    def sb(name, shape, dt=F32):
        return ctx.enter_context(nc.sbuf_tensor(L + name, shape, dt))

    def sem(name):
        return ctx.enter_context(nc.semaphore(L + name))

    XT = [sb(f"XT{h}", [P, DC, N], F32R) for h in range(2)]
    XN = sb("XN", [P, T, D])
    W1r = [sb(f"W1r{k}", [P, DC, H]) for k in range(TOP)]
    W2r = [sb(f"W2r{k}", [P, HC, D]) for k in range(TOP)]
    W1 = [[sb(f"W1_{k}{h}", [P, DC, H], F32R) for h in range(2)] for k in range(TOP)]
    W2 = [[sb(f"W2_{k}{h}", [P, HC, D], F32R) for h in range(2)] for k in range(TOP)]
    b1 = [sb(f"b1_{k}", [P, HC]) for k in range(TOP)]
    b2 = [sb(f"b2_{k}", [P, D]) for k in range(TOP)]
    act_out = [W1r[0][:, s, :] for s in range(2)]
    hT = [[sb(f"hT{c}{h}", [P, BLK], F32R) for h in range(2)] for c in range(HC)]
    z_st = [sb(f"z_st{par}", [P, QUAD, 6]) for par in range(2)]
    z_mv = [sb(f"z_mv{par}", [P, QUAD, 2]) for par in range(2)]
    var = sb("var", [P, T])
    rstd = sb("rstd", [P, T])
    tmp = sb("tmp", [P, T])
    Wg = sb("Wg", [P, DC, E])
    bg = sb("bg", [P, E])
    comb = sb("comb", [P, TOP])
    sums = sb("sums", [P, NT, DC])
    mean = sb("mean", [P, DC])
    rt = sb("rt", [P, 12, E])
    besti = sb("besti", [P, 8], U32)
    meanT = sb("meanT", [P, DC, P])
    gamma = sb("gamma", [P, D])
    beta = sb("beta", [P, D])

    g_in = sem("g_in")
    dve_own, pool_own = sem("dve_own"), sem("pool_own")
    stats_done, sqrt_done = sem("stats_done"), sem("sqrt_done")
    xn_ready, xt_psum, xt_hi, xt_lo, mean_ready = (sem(n) for n in ("xn_ready", "xt_psum", "xt_hi", "xt_lo", "mean_ready"))
    mean_b, logit_psum = sem("mean_b"), sem("logit_psum")
    soft_in, soft_out, comb_ready = sem("soft_in"), sem("soft_out"), sem("comb_ready")
    w_in, b_in = [sem(f"w_in{k}") for k in range(TOP)], sem("b_in")
    w_hi, w_lo, b2_ready = sem("w_hi"), sem("w_lo"), sem("b2_ready")
    h_psum, h_act, h_hi, h_lo, h_used = (sem(n) for n in ("h_psum", "h_act", "h_hi", "h_lo", "h_used"))
    y_psum, y_free = sem("y_psum"), sem("y_free")
    z_paced = sem("z_paced")
    xn_b, z_stats, z_var, z_sqrt, z_newton, z_norm, z_gamma, out_ready, out_done = (
        sem(n) for n in ("xn_b", "z_stats", "z_var", "z_sqrt", "z_newton", "z_norm", "z_gamma", "out_ready", "out_done"))
    block = ctx.enter_context(nc.Block())
    YB = 4

    def quad(a, q):
        return a[:, bass.ds(q * QUAD, QUAD), :]

    @block.sync
    def _(sp):
        sp.dma_start(Wg[:, :, :], w["Wg"].rearrange("(c p) e -> p c e", p=P)).then_inc(g_in, 16)
        sp.dma_start(bg[:, :], row_over_partitions(w["bg"])).then_inc(g_in, 16)
        sp.dma_start(gamma[:, :], row_over_partitions(w["gamma"])).then_inc(g_in, 16)
        sp.dma_start(beta[:, :], row_over_partitions(w["beta"])).then_inc(g_in, 16)
        sp.wait_ge(comb_ready, 1)
        for k in range(TOP):
            e = sp.value_load(besti[0:1, k:k + 1], min_val=0, max_val=E - 1)
            for Wr, name in ((W1r, "W1"), (W2r, "W2")):
                sp.dma_start(Wr[k][:, :, :], w[name][bass.ds(e, 1), :, :].rearrange(
                    "a (c p) h -> p (a c) h", p=P)).then_inc(w_in[k], 16)
            sp.dma_start(b1[k][:, :], w["b1"][bass.ds(e, 1), :, :].rearrange("a p c -> p (a c)")).then_inc(b_in, 16)
            sp.dma_start(b2[k][:, :], w["b2"][bass.ds(e, 1), :].broadcast_to([P, D])).then_inc(b_in, 16)
        with sp.Fori(0, NT) as tb:
            sp.wait_ge(out_ready, tb + 1)
            sp.dma_start(out_dram[bass.ds(tb * BLK, BLK), :].rearrange("(t p) d -> p t d", p=P),
                         quad(XN, tb)).then_inc(out_done, 16)
        sp.wait_ge(out_done, 16 * NT)

    @block.gpsimd
    def _(pool):
        def over_quad(a):
            return a[:, :].unsqueeze(1).broadcast_to([P, QUAD, D])

        pool.wait_ge(g_in, 64)
        pool.wait_ge(b2_ready, 2)
        with pool.Fori(0, NT) as q:
            pool.tensor_tensor(quad(XN, q), quad(XN, q), over_quad(b2[0]), ALU.add).then_inc(xn_b, 1)
            pool.tensor_tensor(quad(x_sb, q), quad(x_sb, q), over_quad(beta), ALU.add).then_inc(pool_own, 1)
        pool.wait_ge(pool_own, NT)
        with pool.Fori(0, NT) as tb:
            pool.wait_ge(z_norm, tb + 1)
            pool.tensor_tensor(quad(XN, tb), quad(XN, tb), over_quad(gamma), ALU.mult).then_inc(z_gamma, 1)
            pool.wait_ge(z_gamma, tb + 1)
            pool.tensor_tensor(quad(XN, tb), quad(XN, tb), quad(x_sb, tb), ALU.add).then_inc(out_ready, 1)

    @block.scalar
    def _(act):
        act.wait_ge(stats_done, 1)
        act.activation(rstd[:, :], var[:, :], ACT.Sqrt).then_inc(sqrt_done, 1)

        def hi(q, par):
            act.wait_ge(xt_psum, q + 1)
            for d in range(DC):
                act.activation(XT[0][:, d, bass.ds(q * BLK, BLK)], ps[:, 2 * par + d, :], ACT.Copy,
                               accum_out=sums[:, bass.ds(q, 1), d]).then_inc(xt_hi, 1)

        with act.Fori(0, NT // 2) as pair:
            for par in range(2):
                hi(2 * pair + par, par)
        act.wait_ge(mean_ready, 1)
        act.activation(meanT[:, :, :], mean[:, :].unsqueeze(2).broadcast_to([P, DC, P]), ACT.Copy,
                       scale=1.0 / N).then_inc(mean_b, 1)
        for n, (dst, src) in enumerate([(2, 1), (6, 5), (10, 9)]):
            act.wait_ge(soft_in, n + 1)
            act.activation(rt[:, dst, :], rt[:, src, :], ACT.Exp).then_inc(soft_out, 1)
        act.wait_ge(comb_ready, 1)
        for k in range(TOP):
            act.wait_ge(w_in[k], 32)
            act.activation(W1[k][0][:, :, :], W1r[k][:, :, :], ACT.Copy).then_inc(w_hi, 1)
            act.activation(W2[k][0][:, :, :], W2r[k][:, :, :], ACT.Copy, scale=comb[:, k:k + 1]).then_inc(w_hi, 1)
        act.wait_ge(b_in, 64)
        act.wait_ge(w_lo, 2)
        act.sem_inc(h_hi, HC)

        def gelu(m, k, c):
            act.wait_ge(h_psum, m + 1)
            act.wait_ge(h_lo, m + 1)
            act.activation(act_out[c % 2], ps[:, c, :], ACT.Gelu, bias=b1[k][:, c:c + 1]).then_inc(h_act, 1)
            act.wait_ge(h_used, m + 1)
            act.activation(hT[c][0][:, :], ps[:, c, :], ACT.Gelu, bias=b1[k][:, c:c + 1]).then_inc(h_hi, 1)

        def root(tb):
            act.wait_ge(z_var, tb + 1)
            act.activation(rstd[:, bass.ds(tb * QUAD, QUAD)], var[:, bass.ds(tb * QUAD, QUAD)], ACT.Sqrt).then_inc(z_sqrt, 1)

        for k in range(TOP):
            for c in range(HC):
                gelu(HC * k + c, k, c)
        with act.Fori(1, NT) as tb:
            for k in range(TOP):
                for c in range(HC):
                    gelu(CHUNKS * tb + HC * k + c, k, c)
                    if (k, c) == (1, 0):
                        root(tb - 1)
        root(NT - 1)

    @block.vector
    def _(dve):
        own = Tally(dve, dve_own)
        dve.tensor_scalar(var[:, :], mv[:, :, 1], LN_EPS, None, ALU.add).then_inc(stats_done, 1)
        dve.wait_ge(stats_done, 1)
        newton_rsqrt(dve, own, sqrt_done, 1, var[:, :], rstd[:, :], tmp[:, :])

        def normalise(q):
            for v in range(QUAD):
                t = q * QUAD + v
                ins = dve.tensor_scalar(XN[:, bass.ds(t, 1), :], x_sb[:, bass.ds(t, 1), :], mv[:, bass.ds(t, 1), 0],
                                        rstd[:, bass.ds(t, 1)], ALU.subtract, ALU.mult)
            ins.then_inc(xn_ready, 1)

        def split(q, par):
            dve.wait_ge(xt_hi, DC * (q + 1))
            s = bass.ds(q * BLK, BLK)
            dve.tensor_tensor(XT[1][:, :, s], ps[:, 2 * par:2 * par + 2, :], XT[0][:, :, s], ALU.subtract).then_inc(xt_lo, 1)

        normalise(0)
        normalise(1)
        with dve.Fori(0, NT // 2 - 1) as pair:
            for par in range(2):
                split(2 * pair + par, par)
                normalise(2 * pair + par + 2)
        for par in range(2):
            split(NT - 2 + par, par)

        dve.reduce_sum(mean[:, :], sums[:, :, :].rearrange("p q d -> p d q"), AX_X).then_inc(mean_ready, 1)
        dve.wait_ge(g_in, 64)
        r = [rt[:, i, :] for i in range(12)]
        c = [rt[:, 11, i:i + 1] for i in range(8)]
        tokens = float(N)
        cap = float(-(-int(N * CAPACITY_FACTOR * 4) // (E * 4)))

        def softmax(src, diff, ex, n, m, s, dst):
            own.link(dve.reduce_max(m, src, AX_X))
            own.link(dve.tensor_scalar(diff, src, m, None, ALU.subtract))
            dve.sem_inc(soft_in, 1)
            dve.wait_ge(soft_out, n)
            own.link(dve.reduce_sum(s, ex, AX_X))
            own.link(dve.reciprocal(s, s))
            own.link(dve.tensor_scalar(dst, ex, s, None, ALU.mult))

        dve.wait_ge(logit_psum, 1)
        own.link(dve.tensor_tensor(r[0], ps[:, 5, 0:E], bg[:, :], ALU.add))
        softmax(r[0], r[1], r[2], 1, c[0], c[1], r[3])
        own.link(dve.tensor_scalar(r[4], r[3], tokens, None, ALU.mult))
        own.link(dve.reciprocal(r[4], r[4]))
        own.link(dve.tensor_scalar(r[4], r[4], cap, 1.0, ALU.mult, ALU.min))
        own.link(dve.tensor_tensor(r[4], r[4], r[3], ALU.mult))
        softmax(r[4], r[5], r[6], 2, c[2], c[3], r[7])
        own.link(dve.max(r[8], r[7]))
        own.link(dve.max_index(besti[:, :], r[8], r[7]))
        own.link(dve.tensor_scalar(r[9], r[8], rt[:, 8, 0:1], None, ALU.subtract))
        dve.sem_inc(soft_in, 1)
        dve.wait_ge(soft_out, 3)
        own.link(dve.reduce_sum(c[4], rt[:, 10, 0:TOP], AX_X))
        own.link(dve.reciprocal(c[4], c[4]))
        own.link(dve.tensor_scalar(comb[:, :], rt[:, 10, 0:TOP], c[4], None, ALU.mult))
        dve.sem_inc(comb_ready, 1)

        dve.sem_inc(h_lo, 2)
        dve.sem_inc(y_free, 4)
        for k in range(TOP):
            dve.wait_ge(w_hi, 2 * k + 1)
            dve.tensor_tensor(W1[k][1][:, :, :], W1r[k][:, :, :], W1[k][0][:, :, :], ALU.subtract).then_inc(w_lo, 1)
            dve.wait_ge(w_hi, 2 * k + 2)
            dve.scalar_tensor_tensor(W2[k][1][:, :, :], W2r[k][:, :, :], comb[:, k:k + 1], W2[k][0][:, :, :],
                                     ALU.mult, ALU.subtract).then_inc(w_lo, 1)
        dve.wait_ge(b_in, 64)
        dve.tensor_scalar(b2[0][:, :], b2[0][:, :], comb[:, 0:1], None, ALU.mult).then_inc(b2_ready, 1)
        dve.wait_ge(b2_ready, 1)
        dve.scalar_tensor_tensor(b2[0][:, :], b2[1][:, :], comb[:, 1:2], b2[0][:, :], ALU.mult, ALU.add).then_inc(b2_ready, 1)

        def split_h(m, c):
            dve.wait_ge(h_act, m + 1)
            dve.wait_ge(h_hi, m + 1 + HC)
            dve.tensor_tensor(hT[c][1][:, :], act_out[c % 2], hT[c][0][:, :], ALU.subtract).then_inc(h_lo, 1)

        def tail(tb, par, part):
            if part == 0:
                dve.wait_ge(xn_b, tb + 1)
                for g in range(2):
                    if g == 0:
                        dve.wait_ge(y_psum, tb + 1)
                    else:
                        dve.wait_ge(h_used, CHUNKS * (tb + 1) + HC)
                    z = XN[:, bass.ds(tb * QUAD + 2 * g, 2), :]
                    dve.tensor_tensor(z, z, ps[:, YB + 2 * par + g, :].rearrange("p (t n) -> p t n", n=D),
                                      ALU.add).then_inc(y_free, 1)
            if part == 1:
                dve.wait_ge(y_free, 2 * (tb + 1) + 4)
                dve.sem_inc(z_paced, 1)
                for v in range(QUAD):
                    t = tb * QUAD + v
                    dve.bn_stats(z_st[par][:, v, :],
                                 XN[:, bass.ds(t, 1), :].rearrange("p a n -> p (a n)")).then_inc(z_stats, 1)
                dve.wait_ge(z_stats, 2 * QUAD * tb + QUAD)
                dve.sem_inc(z_paced, 1)
                for v in range(QUAD):
                    dve.bn_aggr(z_mv[par][:, v, :], z_st[par][:, v, :]).then_inc(z_stats, 1)
            if part == 2:
                dve.wait_ge(z_stats, 2 * QUAD * (tb + 1))
                dve.tensor_scalar(var[:, bass.ds(tb * QUAD, QUAD)], z_mv[par][:, :, 1], LN_EPS, None,
                                  ALU.add).then_inc(z_var, 1)
            if part == 3:
                a, r_, t_ = (v[:, bass.ds(tb * QUAD, QUAD)] for v in (var, rstd, tmp))
                dve.wait_ge(z_sqrt, tb + 1)
                dve.reciprocal(r_, r_).then_inc(z_newton, 1)
                dve.wait_ge(z_newton, 5 * tb + 1)
                dve.tensor_tensor(t_, r_, r_, ALU.mult).then_inc(z_newton, 1)
                dve.wait_ge(z_newton, 5 * tb + 2)
                dve.tensor_tensor(t_, t_, a, ALU.mult).then_inc(z_newton, 1)
                dve.wait_ge(z_newton, 5 * tb + 3)
                dve.tensor_scalar(t_, t_, -0.5, 1.5, ALU.mult, ALU.add).then_inc(z_newton, 1)
                dve.wait_ge(z_newton, 5 * tb + 4)
                dve.tensor_tensor(r_, r_, t_, ALU.mult).then_inc(z_newton, 1)
                dve.wait_ge(z_newton, 5 * tb + 5)
                for v in range(QUAD):
                    t = tb * QUAD + v
                    ins = dve.tensor_scalar(XN[:, bass.ds(t, 1), :], XN[:, bass.ds(t, 1), :], z_mv[par][:, v:v + 1, 0],
                                            rstd[:, bass.ds(t, 1)], ALU.subtract, ALU.mult)
                ins.then_inc(z_norm, 1)

        AFTER = {1: 0, 2: 1, 3: 2, 5: 3}

        def features(tb, par, with_tail):
            for m in range(CHUNKS):
                split_h(CHUNKS * tb + m, m % HC)
                if with_tail and m in AFTER:
                    tail(tb - 1, 1 - par, AFTER[m])

        features(0, 0, False)
        features(1, 1, True)
        with dve.Fori(1, NT // 2) as pair:
            for par in range(2):
                features(2 * pair + par, par, True)
        for part in range(4):
            tail(NT - 1, 1, part)

    @block.tensor
    def _(pe):
        def transposes(q, par, first):
            pe.wait_ge(xn_ready, q + 1)
            if not first:
                pe.wait_ge(xt_lo, q - 1)
            for d in range(DC):
                for v in range(QUAD):
                    mm = pe.transpose(ps[:, 2 * par + d, v * P:(v + 1) * P], XN[:, q * QUAD + v, d * P:(d + 1) * P],
                                      ident[:, :])
            mm.then_inc(xt_psum, 1)

        for q in range(NT):
            transposes(q, q % 2, q < 2)
        pe.wait_ge(g_in, 64)
        pe.wait_ge(mean_b, 1)
        for d in range(DC):
            mm = pe.matmul(ps[:, 5, 0:E], meanT[:, d, :], Wg[:, d, :], start=(d == 0), stop=(d == DC - 1))
        mm.then_inc(logit_psum, 1)
        pe.wait_ge(xt_lo, NT)
        pe.wait_ge(comb_ready, 1)
        pe.sem_inc(h_used, HC)

        def up(tb, m):
            k, c = m // HC, m % HC
            pe.wait_ge(h_hi, CHUNKS * tb + m + 1)
            n = 0
            for d in range(DC):
                for a, b in ((0, 0), (0, 1), (1, 0)):
                    mm = pe.matmul(ps[:, c, :], W1[k][a][:, d, c * P:(c + 1) * P],
                                   XT[b][:, d, bass.ds(tb * BLK, BLK)], start=(n == 0), stop=(n == 3 * DC - 1))
                    n += 1
            mm.then_inc(h_psum, 1)

        def down(tb, par, m):
            k, c = m // HC, m % HC
            pe.wait_ge(h_lo, CHUNKS * tb + m + 3)
            for t in range(QUAD):
                g = t // 2
                if m == 0 and t % 2 == 0:
                    pe.wait_ge(y_free, 2 * tb + g + 1)
                for n, (a, b) in enumerate(((0, 0), (0, 1), (1, 0))):
                    mm = pe.matmul(ps[:, YB + 2 * par + g, (t % 2) * D:(t % 2 + 1) * D],
                                   hT[c][a][:, t * P:(t + 1) * P], W2[k][b][:, c, :],
                                   start=(m == 0 and t % 2 == 0 and n == 0), stop=(m == CHUNKS - 1),
                                   skip_group_check=True)
                if m == CHUNKS - 1 and t == 1:
                    mm.then_inc(y_psum, 1)
            mm.then_inc(h_used, 1)

        def block_of(tb, par, has_next=True):
            for m in range(CHUNKS):
                if m + 2 < CHUNKS:
                    if m + 2 == HC and par == 0 and isinstance(tb, int):
                        pe.wait_ge(w_lo, 4)
                    up(tb, m + 2)
                elif has_next:
                    up(tb + 1, m + 2 - CHUNKS)
                down(tb, par, m)

        pe.wait_ge(w_lo, 2)
        for m in range(2):
            up(0, m)
        block_of(0, 0)
        block_of(1, 1)
        with pe.Fori(1, NT // 2 - 1) as pair:
            for par in range(2):
                block_of(2 * pair + par, par)
        block_of(NT - 2, 0)
        block_of(NT - 1, 1, has_next=False)


def moe0(nc, top, w, X, mv, ident, ps, x_kept, rows, wtop, gnn_sems):
    E, D, H = w["W1"].shape
    XW = X.shape[2]
    N = X.shape[1] * P
    T = N // P
    DC, HC = D // P, H // P
    QUAD = 4
    NQ = T // QUAD
    TILES = (TOP * N + E * (P - 1)) // P
    RING = 8
    TILES = -(-TILES // RING) * RING
    NOWHERE = 1 << 20
    L = "m_"

    slots = nc.dram_tensor(L + "slots", (TILES * P, XW), F32, kind="Internal").ap()

    def sem(name):
        return top.enter_context(nc.semaphore(L + name))

    def keep(name, shape, dt=F32):
        return top.enter_context(nc.sbuf_tensor(L + name, shape, dt))

    def two_banks(n):
        return ps[:, 2 * n:2 * n + 2, :].rearrange("p b n -> p (b n)")

    posu = keep("posu", [P, TOP, T], U32)
    eid = keep("eid", [P, TILES + 2], I32)

    with ExitStack() as ctx:
        def sb(name, shape, dt=F32):
            return ctx.enter_context(nc.sbuf_tensor(L + name, shape, dt))

        var = sb("var", [P, T])
        rstd = sb("rstd", [P, T])
        tmp = sb("tmp", [P, T])
        xt = [[sb(f"xt{s}{h}", [P, QUAD * DC * P], F32R) for h in range(2)] for s in range(2)]
        Wgr = sb("Wgr", [P, DC, E])
        Wg = sb("Wg", [P, DC, 2, E], F32R)
        bg = sb("bg", [P, E])
        bg2 = sb("bg2", [P, E])
        iota_e = sb("iota_e", [P, E])
        iota_k = sb("iota_k", [P, TILES])
        below = sb("below", [P, P])
        ones = sb("ones", [P, P])
        pad = sb("pad", [P, XW])
        ids = sb("ids", [P, T], U32)
        logit = sb("logit", [P, T, E])
        best = sb("best", [P, T, 8])
        besti = sb("besti", [P, T, 8], U32)
        bestf = sb("bestf", [P, T, TOP])
        pick = [sb(f"pick{k}", [P, T, E]) for k in range(TOP)]
        both = sb("both", [P, T, E])
        total = sb("total", [P, T, E])
        upto = sb("upto", [P, T, E])
        pos = sb("pos", [P, T, E])
        posf = sb("posf", [P, TOP, T])
        cnt = sb("cnt", [P, E], I32)
        ntile = sb("ntile", [P, E])
        tend = sb("tend", [P, E])
        start = sb("start", [P, E])
        past = sb("past", [P, TILES, E])
        eidf = sb("eidf", [P, TILES])

        g_in, padded = sem("g_in"), sem("padded")
        dve_own, pool_own = sem("dve_own"), sem("pool_own")
        consts, pad_made = sem("consts"), sem("pad_made")
        stats_done, sqrt_done = sem("stats_done"), sem("sqrt_done")
        xn_ready, xt_psum, xt_hi, xt_lo, gate_psum, wg_split = (
            sem(n) for n in ("xn_ready", "xt_psum", "xt_hi", "xt_lo", "gate_psum", "wg_split"))
        soft_in, soft_out, both_ready, prefix = sem("soft_in"), sem("soft_out"), sem("both_ready"), sem("prefix")
        block = ctx.enter_context(nc.Block())

        @block.sync
        def _(sp):
            sp.dma_start(Wgr[:, :, :], w["Wg"].rearrange("(c p) e -> p c e", p=P)).then_inc(g_in, 16)
            sp.dma_start(bg[:, :], row_over_partitions(w["bg"])).then_inc(g_in, 16)
            sp.dma_start(bg2[:, :], row_over_partitions(w["bias"])).then_inc(g_in, 16)
            sp.wait_ge(pad_made, 3)
            sp.dma_start(slots.rearrange("(k p) n -> p k n", p=P),
                         pad[:, :].unsqueeze(1).broadcast_to([P, TILES, XW])).then_inc(padded, 16)
            sp.wait_ge(padded, 16)

        @block.gpsimd
        def _(pool):
            clear(pool, gnn_sems)
            pool.memset(ones[:, :], 1.0).then_inc(consts, 1)
            pool.iota(iota_e[:, :], [[1, E]], base=0, channel_multiplier=0,
                      allow_small_or_imprecise_dtypes=True).then_inc(consts, 1)
            pool.iota(iota_k[:, :], [[1, TILES]], base=0, channel_multiplier=0,
                      allow_small_or_imprecise_dtypes=True).then_inc(consts, 1)
            pool.memset(below[:, :], 1.0).then_inc(pool_own, 1)
            pool.wait_ge(pool_own, 1)
            pool.affine_select(out=below[:, :], in_=below[:, :], compare_op=ALU.is_gt, fill=0.0, base=0,
                               pattern=[[1, P]], channel_multiplier=-1).then_inc(consts, 1)
            pool.memset(pad[:, :], 0.0).then_inc(pad_made, 1)
            pool.wait_ge(pad_made, 1)
            pool.iota(pad[:, D:D + 1].bitcast(U32), [[0, 1]], base=NOWHERE, channel_multiplier=0).then_inc(pad_made, 2)
            pool.iota(ids[:, :], [[P, T]], base=0, channel_multiplier=1).then_inc(consts, 1)
            pool.wait_ge(consts, 5)
            pool.memset(X[:, :, D:XW], 0.0).then_inc(pool_own, 1)
            pool.wait_ge(pool_own, 2)
            pool.tensor_copy(X[:, :, D].bitcast(U32), ids[:, :]).then_inc(pool_own, 1)

        @block.scalar
        def _(act):
            act.wait_ge(stats_done, 1)
            act.activation(rstd[:, :], var[:, :], ACT.Sqrt).then_inc(sqrt_done, 1)

            act.wait_ge(g_in, 48)
            act.activation(Wg[:, :, 0, :], Wgr[:, :, :], ACT.Copy).then_inc(wg_split, 1)

            def copy(q, par, first):
                act.wait_ge(xt_psum, q + 1)
                if not first:
                    act.wait_ge(gate_psum, q - 1)
                act.activation(xt[par][0][:, :], two_banks(par), ACT.Copy).then_inc(xt_hi, 1)

            for par in range(2):
                copy(par, par, True)
            with act.Fori(1, NQ // 2) as pair:
                for par in range(2):
                    copy(2 * pair + par, par, False)
            act.wait_ge(soft_in, 1)
            act.activation(wtop[:, :, 1], wtop[:, :, 0], ACT.Exp).then_inc(soft_out, 1)

        @block.tensor
        def _(pe):
            def transposes(q):
                par = q % 2
                pe.wait_ge(xn_ready, q + 1)
                if q >= 2:
                    pe.wait_ge(xt_lo, q - 1)
                for v in range(QUAD):
                    for c in range(DC):
                        at = (v % 2) * D + c * P
                        mm = pe.transpose(ps[:, 2 * par + v // 2, at:at + P],
                                          X[:, q * QUAD + v, c * P:(c + 1) * P], ident[:, :])
                mm.then_inc(xt_psum, 1)

            def gate(q):
                pe.wait_ge(xt_lo, q + 1)
                for v in range(QUAD):
                    at = v * 2 * E
                    for c in range(DC):
                        x = slice((v * DC + c) * P, (v * DC + c + 1) * P)
                        pe.matmul(ps[:, 4 + q % 4, at:at + 2 * E], xt[q % 2][0][:, x], Wg[:, c, :, :],
                                  start=(v == 0 and c == 0), stop=(c == DC - 1), skip_group_check=True)
                        mm = pe.matmul(ps[:, 4 + q % 4, at:at + E], xt[q % 2][1][:, x], Wg[:, c, 0, :], start=False,
                                       stop=(c == DC - 1), skip_group_check=True)
                mm.then_inc(gate_psum, 1)

            transposes(0)
            pe.wait_ge(wg_split, 2)
            for q in range(1, NQ):
                transposes(q)
                gate(q - 1)
            gate(NQ - 1)
            pe.wait_ge(both_ready, 1)
            pe.wait_ge(consts, 5)
            flat = both[:, :, :].rearrange("p t e -> p (t e)")
            pe.matmul(ps[:, 5, 0:T * E], below[:, :], flat, start=True, stop=True)
            pe.matmul(ps[:, 6, 0:T * E], ones[:, :], flat, start=True, stop=True).then_inc(prefix, 1)

        @block.vector
        def _(dve):
            own = Tally(dve, dve_own)
            dve.tensor_scalar(var[:, :], mv[:, :, 1], LN_EPS, None, ALU.add).then_inc(stats_done, 1)
            dve.wait_ge(stats_done, 1)
            newton_rsqrt(dve, own, sqrt_done, 1, var[:, :], rstd[:, :], tmp[:, :])

            dve.wait_ge(wg_split, 1)
            dve.tensor_tensor(Wg[:, :, 1, :], Wgr[:, :, :], Wg[:, :, 0, :], ALU.subtract).then_inc(wg_split, 1)

            def split(q):
                dve.wait_ge(xt_hi, q + 1)
                dve.tensor_tensor(xt[q % 2][1][:, :], two_banks(q % 2), xt[q % 2][0][:, :], ALU.subtract).then_inc(xt_lo, 1)

            def over_tiles(a, n=T):
                return a.unsqueeze(1).broadcast_to([P, n, E])

            def choose(q):
                s = slice(q * QUAD, (q + 1) * QUAD)
                halves = ps[:, 4 + q % 4, 0:2 * E * QUAD].rearrange("p (t h e) -> p t h e", h=2, e=E)
                dve.wait_ge(gate_psum, q + 1)
                own.link(dve.tensor_copy(logit[:, s, :], halves[:, :, 1, :]))
                own.link(dve.tensor_tensor(logit[:, s, :], logit[:, s, :], halves[:, :, 0, :], ALU.add))
                own.link(dve.tensor_tensor(logit[:, s, :], logit[:, s, :], over_tiles(bg[:, :], QUAD), ALU.add))
                own.link(dve.tensor_tensor(logit[:, s, :], logit[:, s, :], over_tiles(bg2[:, :], QUAD), ALU.add))
                for t in range(T)[s]:
                    own.add(dve.max(best[:, t, :], logit[:, t, :]))
                own.settle()
                for t in range(T)[s]:
                    own.add(dve.max_index(besti[:, t, :], best[:, t, :], logit[:, t, :]))

            for q in range(NQ + 3):
                if q < NQ:
                    if q % (NQ // 2) == 0:
                        dve.wait_ge(x_kept[2 * q // NQ], 16 * NQ // 2)
                    for t in range(q * QUAD, (q + 1) * QUAD):
                        ins = dve.tensor_scalar(X[:, t, 0:D], X[:, t, 0:D], mv[:, t, 0:1], rstd[:, t:t + 1],
                                                ALU.subtract, ALU.mult)
                    ins.then_inc(xn_ready, 1)
                if 0 <= q - 1 < NQ:
                    split(q - 1)
                if q - 3 >= 0:
                    choose(q - 3)
            own.settle()
            dve.wait_ge(consts, 5)
            own.link(dve.tensor_copy(bestf[:, :, :], besti[:, :, 0:TOP]))
            for k in range(TOP):
                own.link(dve.tensor_tensor(pick[k][:, :, :], bestf[:, :, k:k + 1].broadcast_to([P, T, E]),
                                           over_tiles(iota_e[:, :]), ALU.is_equal))
            dve.tensor_tensor(both[:, :, :], pick[0][:, :, :], pick[1][:, :, :], ALU.add).then_inc(both_ready, 1)
            dve.tensor_tensor(wtop[:, :, 0], best[:, :, 1], best[:, :, 0], ALU.subtract).then_inc(soft_in, 1)
            dve.wait_ge(soft_out, 1)
            own.link(dve.tensor_scalar(tmp[:, :], wtop[:, :, 1], 1.0, None, ALU.add))
            own.link(dve.reciprocal(wtop[:, :, 0], tmp[:, :]))
            own.link(dve.tensor_tensor(wtop[:, :, 1], wtop[:, :, 1], wtop[:, :, 0], ALU.mult))
            dve.wait_ge(prefix, 1)
            own.link(dve.tensor_copy(total[:, :, :], ps[:, 6, 0:T * E].rearrange("p (t e) -> p t e", e=E)))
            for e in range(E):
                own.add(dve.tensor_tensor_scan(upto[:, :, e], ones[:, 0:T], total[:, :, e], 0.0, ALU.mult, ALU.add))
            own.settle()
            own.link(dve.tensor_scalar(cnt[:, :], upto[:, T - 1, :], float(P - 1), None, ALU.add))
            own.link(dve.tensor_scalar(cnt[:, :], cnt[:, :], P.bit_length() - 1, None, ALU.logical_shift_right))
            own.link(dve.tensor_copy(ntile[:, :], cnt[:, :]))
            own.link(dve.tensor_tensor_scan(tend[:, :], ones[:, 0:E], ntile[:, :], 0.0, ALU.mult, ALU.add))
            own.link(dve.tensor_tensor(start[:, :], tend[:, :], ntile[:, :], ALU.subtract))
            own.link(dve.tensor_scalar(start[:, :], start[:, :], float(P), None, ALU.mult))
            own.link(dve.tensor_tensor(upto[:, :, :], upto[:, :, :], total[:, :, :], ALU.subtract))
            own.link(dve.tensor_tensor(pos[:, :, :], ps[:, 5, 0:T * E].rearrange("p (t e) -> p t e", e=E),
                                       upto[:, :, :], ALU.add))
            own.link(dve.tensor_tensor(pos[:, :, :], pos[:, :, :], over_tiles(start[:, :]), ALU.add))
            for k in range(TOP):
                own.link(dve.tensor_tensor(pick[k][:, :, :], pick[k][:, :, :], pos[:, :, :], ALU.mult))
                own.link(dve.reduce_sum(posf[:, k, :], pick[k][:, :, :], AX_X))
            own.link(dve.tensor_copy(posu[:, :, :], posf[:, :, :]))
            own.link(dve.tensor_tensor(past[:, :, :], iota_k[:, :].unsqueeze(2).broadcast_to([P, TILES, E]),
                                       tend[:, :].unsqueeze(1).broadcast_to([P, TILES, E]), ALU.is_ge))
            own.link(dve.reduce_sum(eidf[:, :], past[:, :, :], AX_X))
            own.add(dve.memset(eid[:, 0:2], 0))
            own.link(dve.tensor_scalar(eid[:, 2:TILES + 2], eidf[:, :], float(E - 1), None, ALU.min))

    with ExitStack() as ctx:
        def sb(name, shape, dt=F32):
            return ctx.enter_context(nc.sbuf_tensor(L + name, shape, dt))

        W1 = sb("W1", [P, E * DC, 2, H], F32R)
        W2 = sb("W2", [P, E * HC, 2, D], F32R)
        b1 = sb("b1", [P, E, H])
        b2 = sb("b2", [P, E, D])
        STAGE = H
        stage = [sb(f"stage{s}", [P, STAGE]) for s in range(3)]
        xT = [[sb(f"xT{s}{h}", [P, D], F32R) for h in range(2)] for s in range(2)]
        hT = [[sb(f"hT{s}{h}", [P, H], F32R) for h in range(2)] for s in range(2)]
        xs = [X[:, s, :] for s in range(RING)]
        hs = [X[:, RING + 2 * s:RING + 2 + 2 * s, :].rearrange("p a n -> p (a n)")[:, 0:H] for s in range(2)]
        YS = 4
        ys = [X[:, RING + 4 + s, 0:D] for s in range(YS)]

        sent = [[sem(f"sent{k}{h}") for h in range(2)] for k in range(TOP)]
        id_moved = sem("id_moved")
        stage_in = [sem(f"stage_in{s}") for s in range(3)]
        stage_hi, stage_lo, b_in = sem("stage_hi"), sem("stage_lo"), sem("b_in")
        xs_in = [sem(f"xs_in{s}") for s in range(RING)]
        xT_psum, xT_hi, xT_lo, h_psum, h_sb, hT_psum, hT_hi, hT_lo, y_psum, y_half, y_sb = (
            sem(n) for n in ("xT_psum", "xT_hi", "xT_lo", "h_psum", "h_sb", "hT_psum", "hT_hi", "hT_lo", "y_psum",
                             "y_half", "y_sb"))
        y_out = [sem(f"y_out{s}") for s in range(YS)]
        stores = sem("stores")
        block = ctx.enter_context(nc.Block())
        XB, HB, TB, YB = 0, 2, 4, 6
        n1, n2 = E * DC, E * HC * D // STAGE
        per = STAGE // D
        w1_v = w["W1"].rearrange("e (c p) h -> p (e c) h", p=P)
        w2_v = w["W2"].rearrange("e (c p) h -> p (e c) h", p=P)

        def piece(n, h):
            if n < n1:
                return W1[:, n, h, :]
            m = n - n1
            return W2[:, m * per:(m + 1) * per, h, :]

        def staged(n):
            return stage[n % 3][:, :] if n < n1 else stage[n % 3][:, :].rearrange("p (a n) -> p a n", n=D)

        def experts_of(eng, k):
            return eng_values(nc, eng, eid[0:1, bass.ds(k, RING + 2)], E - 1)

        @block.sync
        def _(sp):
            for n in range(n1 + n2):
                if n >= 3:
                    sp.wait_ge(stage_lo, n - 2)
                if n < n1:
                    sp.dma_start(stage[n % 3][:, :], w1_v[:, n, :]).then_inc(stage_in[n % 3], 16)
                else:
                    m = n - n1
                    sp.dma_start(stage[n % 3][:, :].rearrange("p (a n) -> p a n", n=D),
                                 w2_v[:, m * per:(m + 1) * per, :]).then_inc(stage_in[n % 3], 16)
            sp.dma_start(b1[:, :, :], w["b1"].rearrange("(a e) h -> a e h", a=1).broadcast_to([P, E, H])).then_inc(b_in, 16)
            sp.dma_start(b2[:, :, :], w["b2"].rearrange("(a e) h -> a e h", a=1).broadcast_to([P, E, D])).then_inc(b_in, 16)
            for k in range(TOP):
                for h in range(2):
                    sp.wait_ge(sent[k][h], 16 * T // 2)

            def load(k, v, first):
                if not first:
                    sp.wait_ge(xT_psum, k - RING + 1)
                    sp.wait_ge(y_out[v % YS], (k - v % YS) * (16 // YS) - 16)
                sp.dma_start(xs[v], slots[bass.ds(k * P, P), :]).then_inc(xs_in[v], 16)

            for v in range(RING):
                load(v, v, True)
            with sp.Fori(1, TILES // RING) as turn:
                for v in range(RING):
                    load(RING * turn + v, v, False)

        @block.gpsimd
        def _(pool):
            for k in range(TOP):
                for h in range(2):
                    s = slice(h * T // 2, (h + 1) * T // 2)
                    if k:
                        pool.wait_ge(sent[k - 1][h], 16 * T // 2)
                        pool.tensor_scalar(X[:, s, D].bitcast(U32), X[:, s, D].bitcast(U32), float(N), None,
                                           ALU.add).then_inc(id_moved, 1)
                        pool.wait_ge(id_moved, h + 1)
                    for t in range(T)[s]:
                        pool.indirect_dma_start(slots, bass.IndirectOffsetOnAxis(ap=posu[:, k, t:t + 1], axis=0),
                                                X[:, t, :], None).then_inc(sent[k][h], 16)

            def store(k, v):
                pool.wait_ge(y_sb, k + 1)
                pool.sem_inc(stores, 1)
                pool.indirect_dma_start(rows, bass.IndirectOffsetOnAxis(ap=xs[v][:, D:D + 1].bitcast(U32), axis=0),
                                        ys[v % YS], None, bounds_check=TOP * N - 1,
                                        oob_is_err=False).then_inc(y_out[v % YS], 16)

            with pool.Fori(0, TILES // RING) as turn:
                for v in range(RING):
                    store(RING * turn + v, v)
            for s in range(YS):
                pool.wait_ge(y_out[s], 16 * (TILES // YS))

        @block.scalar
        def _(act):
            for n in range(n1 + n2):
                act.wait_ge(stage_in[n % 3], 16 * (n // 3 + 1))
                act.activation(piece(n, 0), staged(n), ACT.Copy).then_inc(stage_hi, 1)

            def x_hi(k, s, first):
                act.wait_ge(xT_psum, k + 1)
                if not first:
                    act.wait_ge(h_psum, k - 1)
                act.activation(xT[s][0][:, :], ps[:, XB + s, 0:D], ACT.Copy).then_inc(xT_hi, 1)

            def h_hi(k, s, first):
                act.wait_ge(hT_psum, k + 1)
                if not first:
                    act.wait_ge(y_psum, k - 1)
                act.activation(hT[s][0][:, :], ps[:, TB + s, :], ACT.Relu).then_inc(hT_hi, 1)

            x_hi(0, 0, True)
            x_hi(1, 1, True)
            h_hi(0, 0, True)
            x_hi(2, 0, False)
            h_hi(1, 1, True)
            x_hi(3, 1, False)
            with act.Fori(1, TILES // 2 - 1) as pair:
                for s in range(2):
                    k = 2 * pair + s
                    h_hi(k, s, False)
                    x_hi(k + 2, s, False)
            for s in range(2):
                h_hi(TILES - 2 + s, s, False)

        @block.vector
        def _(dve):
            for n in range(n1 + n2):
                dve.wait_ge(stage_hi, n + 1)
                dve.tensor_tensor(piece(n, 1), staged(n), piece(n, 0), ALU.subtract).then_inc(stage_lo, 1)
            dve.wait_ge(b_in, 32)

            def x_lo(k, s, first):
                dve.wait_ge(xT_hi, k + 1)
                dve.tensor_tensor(xT[s][1][:, :], ps[:, XB + s, 0:D], xT[s][0][:, :], ALU.subtract).then_inc(xT_lo, 1)

            def bias_h(k, s, first, e):
                dve.wait_ge(h_psum, k + 1)
                if not first:
                    dve.wait_ge(hT_psum, k - 1)
                dve.tensor_tensor(hs[s], ps[:, HB + s, :], b1[:, bass.ds(e, 1), :].rearrange("p a n -> p (a n)"),
                                  ALU.add).then_inc(h_sb, 1)

            def h_lo(k, s, first):
                dve.wait_ge(hT_hi, k + 1)
                dve.scalar_tensor_tensor(hT[s][1][:, :], ps[:, TB + s, :], 0.0, hT[s][0][:, :], ALU.max,
                                         ALU.subtract).then_inc(hT_lo, 1)

            def bias_y(k, v, first, e):
                s = v % 2
                dve.wait_ge(y_psum, k + 1)
                if not first:
                    dve.wait_ge(y_out[v % YS], (k - v % YS) * (16 // YS))
                dve.tensor_tensor(ys[v % YS], ps[:, YB + s, D:2 * D],
                                  b2[:, bass.ds(e, 1), :].rearrange("p a n -> p (a n)"), ALU.add).then_inc(y_half, 1)
                dve.wait_ge(y_half, k + 1)
                dve.tensor_tensor(ys[v % YS], ys[v % YS], ps[:, YB + s, 0:D], ALU.add).then_inc(y_sb, 1)

            def steps(turn, first=False, last=False):
                e = experts_of(dve, RING * turn)
                for v in range(RING + (2 if last else 0)):
                    k, s = RING * turn + v, v % 2
                    if not last or v < RING - 1:
                        x_lo(k + 1, 1 - s, False)
                    if v < RING:
                        bias_h(k, s, first and v < 2, e[v + 2])
                    if (not first or v >= 1) and v <= RING:
                        h_lo(k - 1, 1 - s, False)
                    if not first or v >= 2:
                        bias_y(k - 2, (v - 2) % RING, first and v - 2 < YS, e[v])

            x_lo(0, 0, True)
            steps(0, first=True)
            with dve.Fori(1, TILES // RING - 1) as turn:
                steps(turn)
            steps(TILES // RING - 1, last=True)

        @block.tensor
        def _(pe):
            PARTS = ((0, 0), (1, 0), (0, 1))
            PRODUCTS = [(c, a, b) for c in range(DC) for a, b in PARTS]

            def x_turn(s, v, c):
                mm = pe.transpose(ps[:, XB + s, c * P:(c + 1) * P], xs[v][:, c * P:(c + 1) * P], ident[:, :])
                if c == DC - 1:
                    mm.then_inc(xT_psum, 1)

            def up(s, e, n):
                c, a, b = PRODUCTS[n]
                mm = pe.matmul(ps[:, HB + s, :], xT[s][a][:, c * P:(c + 1) * P], W1[:, bass.ds(e * DC + c, 1), b, :],
                               start=(n == 0), stop=(n == len(PRODUCTS) - 1))
                if n == len(PRODUCTS) - 1:
                    mm.then_inc(h_psum, 1)

            def h_turn(s, c):
                mm = pe.transpose(ps[:, TB + s, c * P:(c + 1) * P], hs[s][:, c * P:(c + 1) * P], ident[:, :])
                if c == HC - 1:
                    mm.then_inc(hT_psum, 1)

            def down(k, s, first, e):
                pe.wait_ge(hT_lo, k + 1)
                if not first:
                    pe.wait_ge(y_sb, k - 1)
                for c in range(HC):
                    pe.matmul(ps[:, YB + s, :], hT[s][0][:, c * P:(c + 1) * P], W2[:, bass.ds(e * HC + c, 1), :, :],
                              start=(c == 0), stop=(c == HC - 1), skip_group_check=True)
                    mm = pe.matmul(ps[:, YB + s, 0:D], hT[s][1][:, c * P:(c + 1) * P],
                                   W2[:, bass.ds(e * HC + c, 1), 0, :], start=False, stop=(c == HC - 1),
                                   skip_group_check=True)
                mm.then_inc(y_psum, 1)

            def steps(turn, first=False, last=False):
                e = experts_of(pe, RING * turn)
                for v in range(RING + (2 if last else 0)):
                    k, s = RING * turn + v, v % 2
                    with_x, with_up, with_h = not last or v < RING - 1, v < RING, (not first or v >= 1) and v <= RING
                    n = 0
                    if with_x:
                        x_v = (v + 1) % RING
                        pe.wait_ge(xs_in[x_v], (k + 1 - x_v) * (16 // RING) + 16)
                        if not first or v >= 1:
                            pe.wait_ge(xT_lo, k)
                        x_turn(1 - s, x_v, 0)
                    if with_up:
                        pe.wait_ge(xT_lo, k + 1)
                        if not first or v >= 2:
                            pe.wait_ge(h_sb, k - 1)
                    if with_x:
                        for c in range(1, DC):
                            up(s, e[v + 2], n)
                            n += 1
                            x_turn(1 - s, x_v, c)
                    if with_up:
                        up(s, e[v + 2], n)
                        n += 1
                    if with_h:
                        pe.wait_ge(h_sb, k)
                        if not first or v >= 3:
                            pe.wait_ge(hT_lo, k - 2)
                        for c in range(HC):
                            h_turn(1 - s, c)
                            if with_up and n < len(PRODUCTS):
                                up(s, e[v + 2], n)
                                n += 1
                    while with_up and n < len(PRODUCTS):
                        up(s, e[v + 2], n)
                        n += 1
                    if not first or v >= 2:
                        down(k - 2, s, first and v < 4, e[v])

            pe.wait_ge(stage_lo, n1 + n2)
            pe.wait_ge(xs_in[0], 16)
            for c in range(DC):
                x_turn(0, 0, c)
            steps(0, first=True)
            with pe.Fori(1, TILES // RING - 1) as turn:
                steps(turn)
            steps(TILES // RING - 1, last=True)


def build(nc, a, out):
    N, D = a["x"].shape
    T = N // P
    with ExitStack() as top:
        X = top.enter_context(nc.sbuf_tensor("X", [P, T, D + 4], F32))
        x_sb = X[:, :, 0:D]
        dinv = top.enter_context(nc.sbuf_tensor("dinv", [P, T], F32))
        mv = top.enter_context(nc.sbuf_tensor("mv", [P, T, 2], F32))
        ident = top.enter_context(nc.sbuf_tensor("ident", [P, P], F32))
        ps = top.enter_context(nc.psum_tensor("ps", [P, 8, 512], F32))
        made = top.enter_context(nc.semaphore("ident_made"))
        x1 = nc.dram_tensor("x1", (N, D), F32, kind="Internal").ap()
        x_kept = [top.enter_context(nc.semaphore(f"x_kept{h}")) for h in range(2)]
        rows = nc.dram_tensor("rows", (TOP * N, D), F32, kind="Internal").ap()
        wtop = top.enter_context(nc.sbuf_tensor("wtop", [P, T, TOP], F32))
        with nc.Block() as block:
            @block.gpsimd
            def _(pool):
                pool.memset(ident[:, :], 0.0).then_inc(made, 1)
                pool.wait_ge(made, 1)
                pool.affine_select(out=ident[:, :], in_=ident[:, :], compare_op=ALU.not_equal, fill=1.0,
                                   base=0, pattern=[[-1, P]], channel_multiplier=1)
        for layer in range(2):
            with ExitStack() as ctx:
                gnn_sems = gnn(nc, ctx, layer, a["x"], a["adj"], a["adjT"],
                               a["L0_gnn_W"] if layer == 0 else a["L1_gnn_WT"],
                               None if layer == 0 else a["L1_gnn_b"], x_sb, dinv, mv, ident, ps, x1, x_kept, rows, wtop)
            if layer == 0:
                w = {"Wg": a["L0_ffn_Wg"], "bg": a["L0_ffn_bg"], "bias": a["L0_ffn_bias"]}
            else:
                w = {"Wg": a["L1_ffn_Wr"], "bg": a["L1_ffn_br"], "gamma": a["L1_ffn_gamma"], "beta": a["L1_ffn_beta"]}
            w |= {n: a[f"L{layer}_ffn_{n}"] for n in ("W1", "b1", "W2", "b2")}
            with ExitStack() as ctx:
                if layer == 0:
                    moe0(nc, ctx, w, X, mv, ident, ps, x_kept, rows, wtop, gnn_sems)
                else:
                    ffn1(nc, ctx, w, x_sb, mv, ident, ps, out)


def kernel(**inputs):
    import numpy as np
    import concourse.bacc as bacc
    from concourse.bass_utils import run_bass_kernel_spmd

    data = {n: np.asarray(v) for n, v in inputs.items()}
    data["adjT"] = data["adj"].T
    data["L1_gnn_WT"] = data.pop("L1_gnn_W").T
    E, H = data["L1_ffn_b1"].shape
    data["L1_ffn_b1"] = data["L1_ffn_b1"].reshape(E, H // P, P).transpose(0, 2, 1)
    nc = bacc.Bacc("TRN2", target_bir_lowering=False, num_devices=1)
    arrays = {f"in_{n}": np.ascontiguousarray(data[n]) for n in NAMES}
    aps = {n: nc.dram_tensor(f"in_{n}", arrays[f"in_{n}"].shape, mybir.dt.from_np(arrays[f"in_{n}"].dtype),
                             kind="ExternalInput").ap() for n in NAMES}
    out = nc.dram_tensor("out", data["x"].shape, F32, kind="ExternalOutput").ap()
    build(nc, aps, out)
    return run_bass_kernel_spmd(nc, [arrays], core_ids=[0]).results[0]["out"]
```
